# Optimizing a Trainium2 kernel written in Bass

```python
import numpy as np
import jax
import jax.numpy as jnp

def _softmax(x, axis=-1):
    return jax.nn.softmax(x, axis=axis)

def _gelu(x):
    return jax.nn.gelu(x, approximate=True)

def _silu(x):
    return jax.nn.silu(x)

def _sigmoid(x):
    return jax.nn.sigmoid(x)

def _layernorm(x, axis=-1, eps=1e-05):
    m = jnp.mean(x, axis=axis, keepdims=True)
    v = jnp.var(x, axis=axis, keepdims=True)
    return (x - m) / jnp.sqrt(v + eps)

def _scatter_add(tgt, idx, src, axis=0):
    return tgt.at[idx].add(src)

def _segment_sum(src, seg, n):
    return jax.ops.segment_sum(src, seg, n)
kernel_name = 'mk_gnn_preln_d4_gnn_r8_ddf823'

def setup_inputs(seed: int=0):
    np.random.seed(seed)
    _w = jnp.asarray

    def _rec_inputs():
        import jax
        import jax.numpy as jnp
        _gk = jax.random.key(seed)
        x = 0.0002685 + 0.9999 * jax.random.normal(jax.random.fold_in(_gk, 1), (6250, 256), jnp.float32)
        src = jax.random.randint(jax.random.fold_in(_gk, 2), (100000,), 0, 6250, jnp.int32)
        dst = jax.random.randint(jax.random.fold_in(_gk, 3), (100000,), 0, 6250, jnp.int32)
        _o = jnp.argsort(dst, stable=True)
        src = src[_o]
        dst = dst[_o]
        edge_type_8 = jax.random.randint(jax.random.fold_in(_gk, 13), (100000,), 0, 8, jnp.int32)
        edge_weight = jax.random.uniform(jax.random.fold_in(_gk, 14), (100000,), jnp.float32, 0.0, 1)
        node_vec = jax.random.uniform(jax.random.fold_in(_gk, 15), (6250,), jnp.float32, 0.0, 10025.9)
        return (x, src, dst, edge_type_8, edge_weight, node_vec)
    x, src, dst, edge_type_8, edge_weight, node_vec = _rec_inputs()

    def _L0_gnn_setup():
        import jax, jax.numpy as jnp
        import numpy as np
        NUM_NODES = 5000
        NUM_REL = 8
        NUM_BASES = 4
        EMB = 256
        NUM_LAYERS = 3
        NUM_EDGES = 80000

        def _rgcn_layer(x, src, seg, inv_cnt, comp, basis, root, bias):
            N, D = x.shape
            R = comp.shape[0]
            W = jnp.einsum('rb,bio->rio', comp, basis)
            agg = jax.ops.segment_sum(x[src], seg, num_segments=R * N) * inv_cnt
            agg = agg.reshape(R, N, D)
            out = jnp.einsum('rni,rio->no', agg, W) + x @ root + bias
            return out
        key = jax.random.key(seed)
        ks = jax.random.split(key, 7)
        edge_index = jax.random.randint(ks[0], (2, NUM_EDGES), 0, NUM_NODES)
        edge_type = jax.random.randint(ks[1], (NUM_EDGES,), 0, NUM_REL)
        embeddings = jax.random.normal(ks[2], (NUM_NODES, EMB), dtype=jnp.float32)
        scale = 1.0 / np.sqrt(EMB)
        comps = jax.random.normal(ks[3], (NUM_LAYERS, NUM_REL, NUM_BASES), dtype=jnp.float32) * scale
        bases = jax.random.normal(ks[4], (NUM_LAYERS, NUM_BASES, EMB, EMB), dtype=jnp.float32) * scale
        roots = jax.random.normal(ks[5], (NUM_LAYERS, EMB, EMB), dtype=jnp.float32) * scale
        biases = jnp.zeros((NUM_LAYERS, EMB), dtype=jnp.float32)
        return {'edge_index': edge_index, 'edge_type': edge_type, 'embeddings': embeddings, 'comps': comps, 'bases': bases, 'roots': roots, 'biases': biases}
    _L0_gnn_all = _L0_gnn_setup()
    _L0_gnn_in = {k: v for k, v in _L0_gnn_all.items() if k in ('comps', 'bases', 'roots', 'biases')}
    del _L0_gnn_all

    def _L1_gnn_setup():
        import jax, jax.numpy as jnp
        import numpy as np
        N_NODES = 12500
        N_EDGES = 400000
        D_IN = 256
        D_OUT = 256
        key = jax.random.key(seed)
        k1, k2, k3, k4, k5 = jax.random.split(key, 5)
        x = jax.random.normal(k1, (N_NODES, D_IN), dtype=jnp.float32)
        weight = jax.random.normal(k2, (D_IN, D_OUT), dtype=jnp.float32) * (1.0 / np.sqrt(D_IN))
        adj_val = jax.random.uniform(k3, (N_EDGES,), dtype=jnp.float32)
        edge_row = jax.random.randint(k4, (N_EDGES,), 0, N_NODES, dtype=jnp.int32)
        edge_col = jax.random.randint(k5, (N_EDGES,), 0, N_NODES, dtype=jnp.int32)
        return {'x': x, 'weight': weight, 'adj_val': adj_val, 'edge_row': edge_row, 'edge_col': edge_col}
    _L1_gnn_all = _L1_gnn_setup()
    _L1_gnn_in = {k: v for k, v in _L1_gnn_all.items() if k in ('weight',)}
    del _L1_gnn_all

    def _L2_gnn_setup():
        import jax, jax.numpy as jnp
        import numpy as np
        N_NODES = 6250
        IN_DIM = 256
        OUT_DIM = 128
        NUM_HEADS = 2
        N_EDGES = 100000

        def _gat_forward(x, edge_index, W_w, W_b, a):
            N = x.shape[0]
            H, D = (NUM_HEADS, OUT_DIM)
            Wh = (x @ W_w + W_b).reshape(N, H, D)
            src, dst = (edge_index[0], edge_index[1])
            a_src, a_dst = (a[:D], a[D:])
            s = jnp.einsum('nhd,d->nh', Wh, a_src)
            t = jnp.einsum('nhd,d->nh', Wh, a_dst)
            e = jax.nn.leaky_relu(s[src] + t[dst], negative_slope=0.2)
            m = jax.ops.segment_max(e, src, num_segments=N)
            ex = jnp.exp(e - m[src])
            denom = jax.ops.segment_sum(ex, src, num_segments=N)
            alpha = ex / denom[src]
            agg = jax.ops.segment_sum(alpha[:, :, None] * Wh[dst], src, num_segments=N)
            deg = jax.ops.segment_sum(jnp.ones_like(src, dtype=Wh.dtype), src, num_segments=N)
            h_prime = jnp.where(deg[:, None, None] > 0, agg, Wh)
            return h_prime.reshape(N, H * D)
        key = jax.random.key(seed)
        k1, k2, k3, k4, k5 = jax.random.split(key, 5)
        x = jax.random.normal(k1, (N_NODES, IN_DIM), dtype=jnp.float32)
        edge_index = jax.random.randint(k2, (2, N_EDGES), 0, N_NODES, dtype=jnp.int64)
        fan = IN_DIM + OUT_DIM * NUM_HEADS
        W_w = jax.random.uniform(k3, (IN_DIM, OUT_DIM * NUM_HEADS), dtype=jnp.float32, minval=-np.sqrt(6.0 / fan), maxval=np.sqrt(6.0 / fan))
        W_b = jnp.zeros((OUT_DIM * NUM_HEADS,), dtype=jnp.float32)
        fa = 1 + 2 * OUT_DIM
        a = jax.random.uniform(k4, (2 * OUT_DIM,), dtype=jnp.float32, minval=-np.sqrt(6.0 / fa), maxval=np.sqrt(6.0 / fa))
        return {'x': x, 'edge_index': edge_index, 'W_w': W_w, 'W_b': W_b, 'a': a}
    _L2_gnn_all = _L2_gnn_setup()
    _L2_gnn_in = {k: v for k, v in _L2_gnn_all.items() if k in ('W_w', 'W_b', 'a')}
    del _L2_gnn_all

    def _L3_gnn_setup():
        import jax, jax.numpy as jnp
        import numpy as np
        NEG_SLOPE = 0.2
        WINDOW = 5

        def build_edge_index(n):
            srcs, dsts = ([], [])
            for d in range(1, WINDOW + 1):
                i = np.arange(d, n)
                srcs.append(i)
                dsts.append(i - d)
                srcs.append(i - d)
                dsts.append(i)
            i = np.arange(n)
            srcs.append(i)
            dsts.append(i)
            return jnp.asarray(np.stack([np.concatenate(srcs), np.concatenate(dsts)]), dtype=jnp.int32)

        def gat_layer(x, src, dst, W, a_src, a_dst, b, heads, out_ch, concat, n):
            h = (x @ W.T).reshape(n, heads, out_ch)
            alpha_src = jnp.sum(h * a_src, axis=-1)
            alpha_dst = jnp.sum(h * a_dst, axis=-1)
            e = jax.nn.leaky_relu(alpha_src[src] + alpha_dst[dst], NEG_SLOPE)
            m = jax.ops.segment_max(e, dst, num_segments=n)
            e = jnp.exp(e - m[dst])
            s = jax.ops.segment_sum(e, dst, num_segments=n)
            alpha = e / (s[dst] + 1e-16)
            out = jax.ops.segment_sum(alpha[:, :, None] * h[src], dst, num_segments=n)
            out = out.reshape(n, heads * out_ch) if concat else out.mean(axis=1)
            return out + b
        key = jax.random.key(seed)
        N, F, C, H = (2500, 256, 128, 4)
        ks = jax.random.split(key, 8)
        inp = {'sequence_features': jax.random.normal(ks[0], (N, F), dtype=jnp.float32), 'timestamps': jnp.cumsum(jax.random.uniform(ks[1], (N,), dtype=jnp.float32)), 'edge_index': build_edge_index(N), 'W1': jax.random.normal(ks[2], (H * C, F), dtype=jnp.float32) * 0.05, 'a_src1': jax.random.normal(ks[3], (1, H, C), dtype=jnp.float32) * 0.05, 'a_dst1': jax.random.normal(ks[4], (1, H, C), dtype=jnp.float32) * 0.05, 'b1': jnp.zeros((H * C,), dtype=jnp.float32), 'W2': jax.random.normal(ks[5], (F, H * C), dtype=jnp.float32) * 0.05, 'a_src2': jax.random.normal(ks[6], (1, 1, F), dtype=jnp.float32) * 0.05, 'a_dst2': jax.random.normal(ks[7], (1, 1, F), dtype=jnp.float32) * 0.05, 'b2': jnp.zeros((F,), dtype=jnp.float32)}
        return inp
    _L3_gnn_all = _L3_gnn_setup()
    _L3_gnn_in = {k: v for k, v in _L3_gnn_all.items() if k in ('W1', 'a_src1', 'a_dst1', 'b1', 'W2', 'a_src2', 'a_dst2', 'b2')}
    del _L3_gnn_all
    return {'x': x, 'src': src, 'dst': dst, 'edge_type_8': edge_type_8, 'edge_weight': edge_weight, 'node_vec': node_vec, 'L0_gnn_comps': _L0_gnn_in['comps'], 'L0_gnn_bases': _L0_gnn_in['bases'], 'L0_gnn_roots': _L0_gnn_in['roots'], 'L0_gnn_biases': _L0_gnn_in['biases'], 'L1_gnn_weight': _L1_gnn_in['weight'], 'L2_gnn_W_w': _L2_gnn_in['W_w'], 'L2_gnn_W_b': _L2_gnn_in['W_b'], 'L2_gnn_a': _L2_gnn_in['a'], 'L3_gnn_W1': _L3_gnn_in['W1'], 'L3_gnn_a_src1': _L3_gnn_in['a_src1'], 'L3_gnn_a_dst1': _L3_gnn_in['a_dst1'], 'L3_gnn_b1': _L3_gnn_in['b1'], 'L3_gnn_W2': _L3_gnn_in['W2'], 'L3_gnn_a_src2': _L3_gnn_in['a_src2'], 'L3_gnn_a_dst2': _L3_gnn_in['a_dst2'], 'L3_gnn_b2': _L3_gnn_in['b2']}

def reference(x, src, dst, edge_type_8, edge_weight, node_vec, L0_gnn_comps, L0_gnn_bases, L0_gnn_roots, L0_gnn_biases, L1_gnn_weight, L2_gnn_W_w, L2_gnn_W_b, L2_gnn_a, L3_gnn_W1, L3_gnn_a_src1, L3_gnn_a_dst1, L3_gnn_b1, L3_gnn_W2, L3_gnn_a_src2, L3_gnn_a_dst2, L3_gnn_b2):
    import jax
    import jax.numpy as jnp

    def _L0_gnn_ref(edge_index, edge_type, embeddings, comps, bases, roots, biases):
        import jax, jax.numpy as jnp
        import numpy as np
        NUM_NODES = 5000
        NUM_REL = 8
        NUM_BASES = 4
        EMB = 256
        NUM_LAYERS = 3
        NUM_EDGES = 80000

        def _rgcn_layer(x, src, seg, inv_cnt, comp, basis, root, bias):
            N, D = x.shape
            R = comp.shape[0]
            W = jnp.einsum('rb,bio->rio', comp, basis)
            agg = jax.ops.segment_sum(x[src], seg, num_segments=R * N) * inv_cnt
            agg = agg.reshape(R, N, D)
            out = jnp.einsum('rni,rio->no', agg, W) + x @ root + bias
            return out
        src, dst = (edge_index[0], edge_index[1])
        N = embeddings.shape[0]
        R = comps.shape[1]
        seg = edge_type * N + dst
        cnt = jax.ops.segment_sum(jnp.ones_like(seg, dtype=embeddings.dtype), seg, num_segments=R * N)
        inv_cnt = (1.0 / jnp.maximum(cnt, 1.0))[:, None]
        x = _rgcn_layer(embeddings, src, seg, inv_cnt, comps[0], bases[0], roots[0], biases[0])
        for i in range(1, NUM_LAYERS - 1):
            x = _rgcn_layer(jax.nn.relu(x), src, seg, inv_cnt, comps[i], bases[i], roots[i], biases[i])
        return x

    def _L1_gnn_ref(x, weight, adj_val, edge_row, edge_col):
        import jax, jax.numpy as jnp
        import numpy as np
        N_NODES = 12500
        N_EDGES = 400000
        D_IN = 256
        D_OUT = 256
        support = jnp.matmul(x, weight)
        msgs = adj_val[:, None] * support[edge_col]
        out = jax.ops.segment_sum(msgs, edge_row, num_segments=x.shape[0])
        return out

    def _L2_gnn_ref(x, edge_index, W_w, W_b, a):
        import jax, jax.numpy as jnp
        import numpy as np
        N_NODES = 6250
        IN_DIM = 256
        OUT_DIM = 128
        NUM_HEADS = 2
        N_EDGES = 100000

        def _gat_forward(x, edge_index, W_w, W_b, a):
            N = x.shape[0]
            H, D = (NUM_HEADS, OUT_DIM)
            Wh = (x @ W_w + W_b).reshape(N, H, D)
            src, dst = (edge_index[0], edge_index[1])
            a_src, a_dst = (a[:D], a[D:])
            s = jnp.einsum('nhd,d->nh', Wh, a_src)
            t = jnp.einsum('nhd,d->nh', Wh, a_dst)
            e = jax.nn.leaky_relu(s[src] + t[dst], negative_slope=0.2)
            m = jax.ops.segment_max(e, src, num_segments=N)
            ex = jnp.exp(e - m[src])
            denom = jax.ops.segment_sum(ex, src, num_segments=N)
            alpha = ex / denom[src]
            agg = jax.ops.segment_sum(alpha[:, :, None] * Wh[dst], src, num_segments=N)
            deg = jax.ops.segment_sum(jnp.ones_like(src, dtype=Wh.dtype), src, num_segments=N)
            h_prime = jnp.where(deg[:, None, None] > 0, agg, Wh)
            return h_prime.reshape(N, H * D)
        return _gat_forward(x, edge_index, W_w, W_b, a)

    def _L3_gnn_ref(sequence_features, timestamps, edge_index, W1, a_src1, a_dst1, b1, W2, a_src2, a_dst2, b2):
        import jax, jax.numpy as jnp
        import numpy as np
        NEG_SLOPE = 0.2
        WINDOW = 5

        def build_edge_index(n):
            srcs, dsts = ([], [])
            for d in range(1, WINDOW + 1):
                i = np.arange(d, n)
                srcs.append(i)
                dsts.append(i - d)
                srcs.append(i - d)
                dsts.append(i)
            i = np.arange(n)
            srcs.append(i)
            dsts.append(i)
            return jnp.asarray(np.stack([np.concatenate(srcs), np.concatenate(dsts)]), dtype=jnp.int32)

        def gat_layer(x, src, dst, W, a_src, a_dst, b, heads, out_ch, concat, n):
            h = (x @ W.T).reshape(n, heads, out_ch)
            alpha_src = jnp.sum(h * a_src, axis=-1)
            alpha_dst = jnp.sum(h * a_dst, axis=-1)
            e = jax.nn.leaky_relu(alpha_src[src] + alpha_dst[dst], NEG_SLOPE)
            m = jax.ops.segment_max(e, dst, num_segments=n)
            e = jnp.exp(e - m[dst])
            s = jax.ops.segment_sum(e, dst, num_segments=n)
            alpha = e / (s[dst] + 1e-16)
            out = jax.ops.segment_sum(alpha[:, :, None] * h[src], dst, num_segments=n)
            out = out.reshape(n, heads * out_ch) if concat else out.mean(axis=1)
            return out + b
        n = sequence_features.shape[0]
        src, dst = (edge_index[0], edge_index[1])
        x = gat_layer(sequence_features, src, dst, W1, a_src1, a_dst1, b1, heads=4, out_ch=128, concat=True, n=n)
        x = jax.nn.elu(x)
        x = gat_layer(x, src, dst, W2, a_src2, a_dst2, b2, heads=1, out_ch=256, concat=False, n=n)
        return x
    edge_index = jnp.stack([src, dst])
    h = jnp.maximum(_layernorm(x, axis=-1), 0.0)
    x = x + _L0_gnn_ref(edge_index, edge_type_8, h, L0_gnn_comps, L0_gnn_bases, L0_gnn_roots, L0_gnn_biases)
    h = jnp.maximum(_layernorm(x, axis=-1), 0.0)
    x = x + _L1_gnn_ref(h, L1_gnn_weight, edge_weight, src, dst)
    h = jnp.maximum(_layernorm(x, axis=-1), 0.0)
    x = x + _L2_gnn_ref(h, edge_index, L2_gnn_W_w, L2_gnn_W_b, L2_gnn_a)
    h = jnp.maximum(_layernorm(x, axis=-1), 0.0)
    x = x + _L3_gnn_ref(h, node_vec, edge_index, L3_gnn_W1, L3_gnn_a_src1, L3_gnn_a_dst1, L3_gnn_b1, L3_gnn_W2, L3_gnn_a_src2, L3_gnn_a_dst2, L3_gnn_b2)
    return x

_drawn_inputs = setup_inputs


def setup_inputs(seed=0):
    import zlib

    import numpy as np

    out = dict(_drawn_inputs(seed))
    spreads = {'L0_gnn_biases': (0.0, 0.1),
     'L2_gnn_W_b': (0.0, 0.325),
     'L3_gnn_b1': (0.0, 0.311),
     'L3_gnn_b2': (0.0, 0.312)}
    factors = {'L2_gnn_a': 8.0,
     'L3_gnn_a_src1': 64.0,
     'L3_gnn_a_dst1': 64.0,
     'L3_gnn_a_src2': 64.0,
     'L3_gnn_a_dst2': 64.0}
    for name, (base, spread) in spreads.items():
        noise = np.random.default_rng([zlib.crc32(name.encode()), seed]).standard_normal(out[name].shape)
        drawn = base * np.exp(spread * noise) if base else spread * noise
        out[name] = jnp.asarray(drawn.astype(out[name].dtype))
    for name, factor in factors.items():
        out[name] = (out[name] * factor).astype(out[name].dtype)
    return out
```

```python
from contextlib import ExitStack

import numpy as np
import concourse.bass as bass
from concourse import mybir

ALU = mybir.AluOpType
ACT = mybir.ActivationFunctionType
AX = mybir.AxisListType
F32 = mybir.dt.float32
BF16 = mybir.dt.bfloat16
I32 = mybir.dt.int32
U32 = mybir.dt.uint32

P = 128
N = 6250
E = 100000
D = 256
REL, BASES = 8, 4
NT = -(-N // P)
NT += NT % 2
PAD_NODE = (NT - 1) * P
NP = NT * P
COLS = -(-E // P)
BODY = 16
QUAD = 4
NQ = BODY // QUAD
SLOTS = -(-((COLS * P + (P - 1) * NT) // P) // BODY) * BODY
TURNS = SLOTS // BODY
SL = SLOTS + BODY
PACK = 4
BITS = 6
KEY_NONE = 999.0
W_ACC = 516
X_AT = W_ACC - D
NEG = -1.0e30
EPS = 1e-5
SLOPE = 0.2
RING = 4
GROUP = next(g for g in range(20, 0, -1) if COLS % (2 * g) == 0)
assert NT <= 1 << BITS and SL % PACK == 0


def named(**parts):
    return type("Named", (), parts)


class Net:

    def __init__(self, nc):
        self.nc, self.ctx, self.sems = nc, ExitStack(), []

    def __enter__(self):
        self.ctx.__enter__()
        return self

    def __exit__(self, *a):
        done = self.ctx.__exit__(*a)
        if self.sems and not a[0]:
            self.nc.clear_and_free_semaphores(self.sems)
            self.nc.all_engine_barrier()
        return done

    def sb(self, name, shape, dt=F32):
        return self.ctx.enter_context(self.nc.sbuf_tensor(name, shape, dt))

    def ps(self, name, shape, dt=F32):
        return self.ctx.enter_context(self.nc.psum_tensor(name, shape, dt))

    def sem(self, name):
        self.sems.append(self.nc.alloc_semaphore(name=name))
        return self.sems[-1]

    def block(self):
        return self.ctx.enter_context(self.nc.Block())


def edges_as_tiles(a):
    full = E // COLS
    rest = E - full * COLS
    return ((0, full, COLS, a[0:full * COLS].rearrange("(p c) -> p c", c=COLS)),
            (full, full + 1, rest, a[full * COLS:E].rearrange("(p c) -> p c", p=1)))


def constants(nc, m):
    with Net(nc) as n:
        made = n.sem("c_made")
        moved = n.sem("c_moved")
        block = n.block()

        @block.gpsimd
        def _(pool):
            pool.iota(m.iota_n[:, :], [[1, P]], base=0, channel_multiplier=0,
                      allow_small_or_imprecise_dtypes=True).then_inc(made, 1)
            pool.iota(m.iota_b[:, :], [[1, P]], base=0, channel_multiplier=0,
                      allow_small_or_imprecise_dtypes=True).then_inc(made, 1)
            pool.iota(m.iota_p[:, :], [[0, 1]], base=0, channel_multiplier=1,
                      allow_small_or_imprecise_dtypes=True).then_inc(made, 1)
            pool.iota(m.iota_s[:, :], [[1, SL]], base=0, channel_multiplier=0,
                      allow_small_or_imprecise_dtypes=True).then_inc(made, 1)
            pool.memset(m.ones[:, :], 1.0).then_inc(made, 1)

        @block.vector
        def _(dve):
            dve.wait_ge(made, 5)
            dve.tensor_scalar(m.ident[:, :], m.iota_n[:, :], m.iota_p[:, 0:1], None, ALU.is_equal).then_inc(moved, 1)
            dve.tensor_scalar(m.ident_b[:, :], m.iota_n[:, :], m.iota_p[:, 0:1], None, ALU.is_equal).then_inc(moved, 1)
            dve.tensor_scalar(m.below[:, :], m.iota_n[:, :], m.iota_p[:, 0:1], None, ALU.is_gt).then_inc(moved, 1)


def rank_edges(nc, n, m, s, key, name):
    last = COLS - 1
    c = named(
        tot=n.sb(name + "tot", [P, NT]), mask=n.sb(name + "mask", [P, COLS]), cum=n.sb(name + "cum", [P, COLS]),
        sel=n.sb(name + "sel", [P, COLS]), place=n.sb(name + "place", [P, COLS]),
        zero=n.sb(name + "zero", [P, COLS]), base=n.sb(name + "base", [P, NT]),
        count=n.sb(name + "count", [NT, 1]), count_i=n.sb(name + "count_i", [NT, 1], I32),
        slots_i=n.sb(name + "slots_i", [NT, 1], I32), slots=n.sb(name + "slots", [NT, 1]),
        first=n.sb(name + "first", [NT, 1]), begun=n.sb(name + "begun", [NT, SL]),
        word=n.sb(name + "word", [1, SL // PACK]), place_i=n.sb(name + "place_i", [P, COLS], I32),
        lane=n.sb(name + "lane", [P, COLS], I32), slot=n.sb(name + "slot", [P, COLS], I32),
        small=m.ps[:, 0, :], wide=m.ps[:, 1:3, :])
    chain = n.sem(name + "chain")
    counted = n.sem(name + "counted")
    half = SL // 2

    def vector(dve, loaded, loads):
        k = 0
        dve.wait_ge(loaded, loads)
        dve.tensor_scalar(c.place_i[:, :], key[:, :], 7, None, ALU.logical_shift_right).then_inc(chain, 1)
        dve.tensor_scalar(c.lane[:, :], key[:, :], P - 1, None, ALU.bitwise_and).then_inc(chain, 1)
        dve.memset(c.zero[:, :], 0.0).then_inc(chain, 1)
        dve.memset(c.place[:, :], 0.0).then_inc(chain, 1)
        k = 4
        dve.wait_ge(chain, k)
        dve.tensor_copy(s.tile[:, :], c.place_i[:, :]).then_inc(chain, 1)
        dve.tensor_copy(s.key[:, :], c.lane[:, :]).then_inc(chain, 1)
        k += 2
        dve.wait_ge(chain, k)
        with dve.Fori(0, NT) as b:
            dve.wait_ge(chain, b + k)
            dve.tensor_scalar(c.mask[:, :], s.tile[:, :], m.iota_n[:, bass.ds(b, 1)], None, ALU.is_equal,
                              ALU.add, accum_out=c.tot[:, bass.ds(b, 1)]).then_inc(chain, 1)
        k += NT
        dve.wait_ge(counted, 1)
        dve.wait_ge(chain, k)
        dve.tensor_scalar(c.count_i[:, :], c.small[0:NT, 0:1], float(P - 1), None, ALU.add).then_inc(chain, 1)
        dve.wait_ge(chain, k + 1)
        dve.tensor_scalar(c.slots_i[:, :], c.count_i[:, :], 7, None, ALU.logical_shift_right).then_inc(chain, 1)
        dve.wait_ge(chain, k + 2)
        dve.tensor_copy(c.slots[:, :], c.slots_i[:, :]).then_inc(chain, 1)
        k += 3
        dve.wait_ge(counted, 4)
        dve.tensor_scalar(c.base[:, :], c.small[:, 64:64 + NT], float(P), None, ALU.mult).then_inc(chain, 1)
        dve.wait_ge(chain, k + 1)
        dve.tensor_tensor(c.base[:, :], c.base[:, :], c.small[:, 128:128 + NT], ALU.add).then_inc(chain, 1)
        dve.tensor_copy(c.first[:, :], c.small[0:NT, 1:2]).then_inc(chain, 1)
        k += 3
        dve.wait_ge(chain, k)
        dve.tensor_scalar(c.begun[:, :], m.iota_s[0:NT, :], c.first[:, 0:1], None, ALU.is_ge).then_inc(chain, 1)
        k += 1
        with dve.Fori(0, NT) as b:
            dve.wait_ge(chain, b * 4 + k)
            dve.tensor_scalar(c.mask[:, :], s.tile[:, :], m.iota_n[:, bass.ds(b, 1)], None, ALU.is_equal).then_inc(chain, 1)
            dve.wait_ge(chain, b * 4 + (k + 1))
            dve.tensor_tensor_scan(c.cum[:, :], c.mask[:, :], c.zero[:, :], c.base[:, bass.ds(b, 1)],
                                   ALU.add, ALU.add).then_inc(chain, 1)
            dve.wait_ge(chain, b * 4 + (k + 2))
            dve.tensor_tensor(c.sel[:, :], c.mask[:, :], c.cum[:, :], ALU.mult).then_inc(chain, 1)
            dve.wait_ge(chain, b * 4 + (k + 3))
            dve.tensor_tensor(c.place[:, :], c.place[:, :], c.sel[:, :], ALU.add).then_inc(chain, 1)
        k += 4 * NT
        dve.wait_ge(chain, k)
        dve.tensor_scalar(c.place_i[:, :], c.place[:, :], -1.0, None, ALU.add).then_inc(chain, 1)
        dve.wait_ge(chain, k + 1)
        dve.tensor_scalar(c.lane[:, :], c.place_i[:, :], P - 1, None, ALU.bitwise_and).then_inc(chain, 1)
        dve.tensor_scalar(c.slot[:, :], c.place_i[:, :], 7, None, ALU.logical_shift_right).then_inc(chain, 1)
        dve.wait_ge(chain, k + 3)
        dve.tensor_copy(c.cum[:, :], c.lane[:, :]).then_inc(chain, 1)
        dve.tensor_copy(c.sel[:, :], c.slot[:, :]).then_inc(chain, 1)
        dve.wait_ge(chain, k + 5)
        dve.scalar_tensor_tensor(out=s.row[:, :], in0=c.cum[:, :], scalar=float(SL), in1=c.sel[:, :],
                                 op0=ALU.mult, op1=ALU.add).then_inc(chain, 1)
        k += 6
        dve.wait_ge(counted, 6)
        t = [c.wide[0:1, h, 0:half].rearrange("o (w q) -> o w q", q=PACK) for h in range(2)]
        hw = half // PACK
        for h in range(2):
            w = c.word[:, h * hw:(h + 1) * hw]
            dve.tensor_scalar(w, t[h][:, :, PACK - 1], -1.0, None, ALU.add).then_inc(chain, 1)
            k += 1
            for q in range(PACK - 2, -1, -1):
                dve.wait_ge(chain, k)
                dve.tensor_scalar(w, w, float(1 << BITS), -1.0, ALU.mult, ALU.add).then_inc(chain, 1)
                dve.wait_ge(chain, k + 1)
                dve.tensor_tensor(w, w, t[h][:, :, q], ALU.add).then_inc(chain, 1)
                k += 2
        dve.wait_ge(chain, k)
        dve.tensor_copy(s.words[:, :], c.word[:, :]).then_inc(chain, 1)
        dve.wait_ge(chain, k + 1)
        return k + 1

    def tensor(pe, dve_before):
        k = dve_before + 6 + NT
        pe.wait_ge(chain, k)
        pe.matmul(c.small[0:NT, 0:1], c.tot[:, :], m.ones[:, 0:1], start=True, stop=True).then_inc(counted, 1)
        pe.wait_ge(chain, k + 3)
        pe.matmul(c.small[0:NT, 1:2], m.below[0:NT, 0:NT], c.slots[:, :], start=True, stop=True).then_inc(counted, 1)
        pe.matmul(c.small[:, 64:64 + NT], c.slots[:, 0:1].to_broadcast([NT, P]), m.below[0:NT, 0:NT],
                  start=True, stop=True).then_inc(counted, 1)
        pe.matmul(c.small[:, 128:128 + NT], m.below[:, :], c.tot[:, :], start=True, stop=True).then_inc(counted, 1)
        pe.wait_ge(chain, k + 7)
        for h in range(2):
            pe.matmul(c.wide[:, h, 0:half], m.ones[0:NT, :], c.begun[:, h * half:(h + 1) * half],
                      start=True, stop=True).then_inc(counted, 1)

    return vector, tensor


def rank_by_dst(nc, m, s, src, dst, etype, weight):
    with Net(nc) as n:
        loaded, filled, stored = n.sem("ld_edges"), n.sem("ld_filled"), n.sem("ld_stored")
        empty = n.sb("empty", [P, SL, 4])
        vector, tensor = rank_edges(nc, n, m, s.by_dst, s.dst, "rd_")
        blank, built = n.sem("ld_blank"), n.sem("ld_built")
        block = n.block()

        @block.gpsimd
        def _(pool):
            for a, v in ((s.src, PAD_NODE), (s.dst, PAD_NODE), (s.etype, 0)):
                pool.memset(a[:, :], v).then_inc(filled, 1)
            pool.memset(s.weight[:, :], 0.0).then_inc(filled, 1)
            pool.memset(empty[:, :, :], 0.0).then_inc(blank, 1)
            pool.wait_ge(blank, 1)
            pool.memset(empty[:, :, 1:2], KEY_NONE).then_inc(blank, 1)

        @block.sync
        def _(sp):
            sp.wait_ge(filled, 4)
            for a, d in ((s.dst, dst), (s.src, src), (s.etype, etype), (s.weight, weight)):
                for p0, p1, w, piece in edges_as_tiles(d):
                    sp.dma_start(a[p0:p1, 0:w], piece).then_inc(loaded, 16)
            sp.wait_ge(blank, 2)
            for rec in (m.rec_dst, m.rec_src):
                sp.dma_start(rec.rearrange("(p s) w -> p (s w)", p=P),
                             empty[:, :, :].rearrange("p s w -> p (s w)")).then_inc(stored, 16)
            sp.wait_ge(stored, 32)

        @block.tensor
        def _(pe):
            tensor(pe, 0)

        @block.vector
        def _(dve):
            vector(dve, loaded, 16 * 8)
            dve.tensor_copy(s.typef[:, :], s.etype[:, :]).then_inc(built, 1)
            dve.tensor_copy(s.srcf[:, :], s.src[:, :]).then_inc(built, 1)
            r = s.rec_a
            dve.wait_ge(built, 2)
            dve.scalar_tensor_tensor(out=r[:, :, 0].bitcast(U32), in0=s.typef[:, :], scalar=float(NP), in1=s.srcf[:, :],
                                     op0=ALU.mult, op1=ALU.add).then_inc(built, 1)
            dve.tensor_copy(r[:, :, 1], s.by_dst.key[:, :]).then_inc(built, 1)
            dve.tensor_copy(r[:, :, 2].bitcast(I32), s.src[:, :]).then_inc(built, 1)
            dve.tensor_copy(r[:, :, 3], s.typef[:, :]).then_inc(built, 1)
            dve.wait_ge(built, 6)


def scatter_records(pool, n, rows, rec, table, name):
    copied = n.sem(name + "copied")
    issuing = n.sem(name + "issuing")
    landed = [n.sem(name + f"landed{h}") for h in range(2)]
    ring_r = n.sb(name + "ring_r", [P, 2, GROUP], U32)
    ring_d = n.sb(name + "ring_d", [P, 2, GROUP, 4])

    def group(c, h, i):
        at = c * GROUP
        pool.tensor_copy(ring_r[:, h, :], rows[:, bass.ds(at, GROUP)]).then_inc(copied, 1)
        pool.tensor_copy(ring_d[:, h, :, :], rec[:, bass.ds(at, GROUP), :]).then_inc(copied, 1)
        pool.wait_ge(copied, c * 2 + 2)
        pool.sem_inc(issuing, 1)
        for g in range(GROUP):
            pool.indirect_dma_start(table, bass.IndirectOffsetOnAxis(ring_r[:, h, g:g + 1], 0),
                                    ring_d[:, h, g, :], None).then_inc(landed[h], 16)

    for h in range(2):
        group(h, h, 0)
    with pool.Fori(1, COLS // (2 * GROUP)) as i:
        for h in range(2):
            pool.wait_ge(landed[h], i * (16 * GROUP))
            group(i * 2 + h, h, i)
    for h in range(2):
        pool.wait_ge(landed[h], 16 * GROUP * (COLS // (2 * GROUP)))


def run_parts(block, *parts):
    @block.sync
    def _(sp):
        for p in parts:
            if "sp" in p:
                p["sp"](sp)

    @block.tensor
    def _(pe):
        for p in parts:
            if "pe" in p:
                p["pe"](pe)

    @block.vector
    def _(dve):
        for p in parts:
            if "dve" in p:
                p["dve"](dve)

    @block.scalar
    def _(act):
        for p in parts:
            if "act" in p:
                p["act"](act)

    @block.gpsimd
    def _(pool):
        for p in parts:
            if "pool" in p:
                p["pool"](pool)


def load_tiles(eng, words, slot, count):
    out = []
    for w in range(count // PACK):
        word = eng.value_load(words[0:1, bass.ds(slot // PACK + w, 1)], min_val=0, max_val=(1 << BITS * PACK) - 1)
        for q in range(PACK):
            v = (word >> (BITS * q)) & ((1 << BITS) - 1)
            out.append(eng.snap(v.with_bounds(min_val=0, max_val=NT - 1)))
    return out


def rank_by_src(nc, n, m, s):
    vector, tensor = rank_edges(nc, n, m, s.by_src, s.src, "rs_")
    ready, built = n.sem("rs_ready"), n.sem("rs_built")

    def dve(dve):
        dve.sem_inc(ready, 1)
        vector(dve, ready, 1)
        r = s.rec_b
        dve.tensor_copy(r[:, :, 0].bitcast(I32), s.dst[:, :]).then_inc(built, 1)
        dve.tensor_copy(r[:, :, 1], s.by_src.key[:, :]).then_inc(built, 1)
        dve.tensor_copy(r[:, :, 2], s.weight[:, :]).then_inc(built, 1)
        dve.memset(r[:, :, 3], 0.0).then_inc(built, 1)
        dve.wait_ge(built, 4)

    return {"dve": dve, "pe": lambda pe: tensor(pe, 0)}


def key_rows(n, m, loaded, name):
    blocks = -(-SL // P)
    turned, copied, stored = n.sem(name + "turned"), n.sem(name + "copied"), n.sem(name + "stored")
    kt = n.sb(name + "kt", [P, blocks, P], BF16)
    pt = m.ps[:, 0:2, :]

    def width(b):
        return min(P, SL - b * P)

    def view(b):
        return pt[0:width(b), b // 4, (b % 4) * P:(b % 4 + 1) * P]

    def pe(pe):
        pe.wait_ge(loaded, 16)
        for b in range(blocks):
            pe.transpose(view(b), m.rec[:, b * P:b * P + width(b), 1], m.ident[:, :]).then_inc(turned, 1)
        pe.wait_ge(copied, blocks)

    def act(act):
        for b in range(blocks):
            act.wait_ge(turned, min(b // 4 * 4 + 4, blocks))
            act.activation(kt[0:width(b), b, :], view(b), ACT.Copy).then_inc(copied, 1)

    def sp(sp):
        sp.wait_ge(copied, blocks)
        for b in range(blocks):
            sp.dma_start(m.key_rows[b * P:b * P + width(b), :], kt[0:width(b), b, :]).then_inc(stored, 16)
        sp.wait_ge(stored, 16 * blocks)

    return {"pe": pe, "act": act, "sp": sp}


def inverse_counts(nc, n, m):
    loaded = n.sem("ic_loaded")
    rows = key_rows(n, m, loaded, "kd_")
    HALF = BODY // 2
    oh = n.sb("ic_oh", [P, BODY, P], BF16)
    rel = n.sb("ic_rel", [P, BODY, REL], BF16)
    cnt = n.sb("ic_cnt", [P, NT, REL])
    kb = n.sb("ic_kb", [P, BODY * P], BF16)
    oht = n.sb("ic_oht", [P, BODY, P])
    rel_f = n.sb("ic_rel_f", [P, BODY, REL])
    prod = n.sb("ic_prod", [P, BODY, REL])
    per_edge = n.sb("ic_per_edge", [P, BODY])
    pc = [m.ps[:, 2 + k // QUAD % 2, k * REL:(k + 1) * REL] for k in range(BODY)]
    px = [m.ps[:, 4 + h, :] for h in range(2)]
    built = n.sem("ic_built")
    summed = n.sem("ic_summed")
    added = n.sem("ic_added")
    begun = n.sem("ic_begun")
    inv = n.sem("ic_inv")
    got = n.sem("ic_got")
    turned = n.sem("ic_oht_made")
    spread = n.sem("ic_spread")
    used = n.sem("ic_used")
    stored = n.sem("ic_stored")

    def sp(sp):
        sp.dma_start(m.rec[:, :, :].rearrange("p s w -> p (s w)"),
                     m.rec_dst.rearrange("(p s) w -> p (s w)", p=P)).then_inc(loaded, 16)
        rows["sp"](sp)

        def fetch(t):
            sp.dma_start(kb[:, :], m.key_rows[bass.ds(t * BODY, BODY), :].rearrange("s e -> (s e)").partition_broadcast(P))\
              .then_inc(got, 16)
        fetch(0)
        with sp.Fori(1, TURNS) as t:
            sp.wait_ge(turned, t * 2)
            fetch(t)
        sp.wait_ge(used, 4 * 2 * TURNS)
        sp.dma_start(m.rec_dst.rearrange("(p s) w -> p (s w)", p=P),
                     m.rec[:, :, :].rearrange("p s w -> p (s w)")).then_inc(stored, 16)
        sp.wait_ge(stored, 16)

    def pe(pe):
        rows["pe"](pe)
        pe.sem_inc(summed, NQ)
        with pe.Fori(0, TURNS) as t:
            for q in range(NQ):
                pe.wait_ge(built, t * NQ + (q + 1))
                pe.wait_ge(added, t * BODY + (q + 1) * QUAD)
                for k in range(q * QUAD, q * QUAD + QUAD):
                    mm = pe.matmul(pc[k], oh[:, k, :], rel[:, k, :], start=True, stop=True)
                mm.then_inc(summed, 1)
        pe.wait_ge(inv, 2)
        with pe.Fori(0, TURNS) as t:
            tiles = load_tiles(pe, m.words_dst, t * BODY, BODY)
            for h in range(2):
                pe.wait_ge(turned, t * 2 + (h + 1))
                for k in range(h * HALF, (h + 1) * HALF):
                    mm = pe.matmul(px[h][:, k * REL:(k + 1) * REL], oht[:, k, :], cnt[:, bass.ds(tiles[k], 1), :],
                                   start=True, stop=True)
                mm.then_inc(spread, 1)
        pe.wait_ge(used, 4 * 2 * TURNS)

    def dve(dve):
        dve.wait_ge(loaded, 16)
        dve.memset(cnt[:, :, :], 0.0).then_inc(begun, 1)
        dve.wait_ge(begun, 1)
        dve.sem_inc(added, 2 * QUAD)
        with dve.Fori(0, TURNS) as t:
            tiles = load_tiles(dve, m.words_dst, t * BODY, BODY)

            def add(q):
                dve.wait_ge(summed, t * NQ + (q + 1 + NQ))
                for k in range(q * QUAD, (q + 1) * QUAD):
                    at = cnt[:, bass.ds(tiles[k], 1), :]
                    dve.wait_ge(added, t * BODY + (k + 2 * QUAD))
                    dve.tensor_tensor(at, at, pc[k].rearrange("p (a r) -> p a r", a=1), ALU.add)\
                       .then_inc(added, 1)
            for q in range(NQ):
                dve.wait_ge(summed, t * NQ + (q + 1))
                for k in range(q * QUAD, (q + 1) * QUAD):
                    slot = t * BODY + k
                    dve.tensor_scalar(oh[:, k, :], m.iota_b[:, :], m.rec[:, bass.ds(slot, 1), 1:2], None, ALU.is_equal)
                dve.tensor_tensor(rel[:, q * QUAD:(q + 1) * QUAD, :],
                                  m.iota_b[:, 0:REL].unsqueeze(1).to_broadcast([P, QUAD, REL]),
                                  m.rec[:, bass.ds(t * BODY + q * QUAD, QUAD), 3:4].to_broadcast([P, QUAD, REL]),
                                  ALU.is_equal).then_inc(built, 1)
                if q:
                    add(q - 1)
            add(NQ - 1)
        dve.wait_ge(added, SLOTS + 2 * QUAD)
        dve.tensor_scalar(cnt[:, :, :], cnt[:, :, :], 1.0, None, ALU.max).then_inc(inv, 1)
        dve.wait_ge(inv, 1)
        dve.reciprocal(cnt[:, :, :], cnt[:, :, :]).then_inc(inv, 1)
        with dve.Fori(0, TURNS) as t:
            dve.wait_ge(got, t * 16 + 16)
            for h in range(2):
                dve.tensor_scalar(oht[:, h * HALF:(h + 1) * HALF, :].rearrange("p s e -> p (s e)"),
                                  kb[:, h * HALF * P:(h + 1) * HALF * P], m.iota_p[:, 0:1], None, ALU.is_equal)\
                   .then_inc(turned, 1)
            for h in range(2):
                a = slice(h * HALF, (h + 1) * HALF)
                u = t * 8 + 4 * h
                dve.tensor_tensor(rel_f[:, a, :], m.iota_n[:, 0:REL].unsqueeze(1).to_broadcast([P, HALF, REL]),
                                  m.rec[:, bass.ds(t * BODY + h * HALF, HALF), 3:4].to_broadcast([P, HALF, REL]),
                                  ALU.is_equal).then_inc(used, 1)
                dve.wait_ge(used, u + 1)
                dve.wait_ge(spread, t * 2 + (h + 1))
                dve.tensor_tensor(prod[:, a, :], rel_f[:, a, :],
                                  px[h][:, h * HALF * REL:(h + 1) * HALF * REL].rearrange("p (s r) -> p s r", r=REL), ALU.mult)\
                   .then_inc(used, 1)
                dve.wait_ge(used, u + 2)
                dve.tensor_reduce(per_edge[:, a], prod[:, a, :], AX.X, ALU.add).then_inc(used, 1)
                dve.wait_ge(used, u + 3)
                dve.tensor_scalar(m.rec[:, bass.ds(t * BODY + h * HALF, HALF), 3], per_edge[:, a], 1.0, None, ALU.mult)\
                   .then_inc(used, 1)

    return {"sp": sp, "pe": pe, "act": rows["act"], "dve": dve}


def load_records(sp, m, table, loaded):
    sp.dma_start(m.rec[:, :, :].rearrange("p s w -> p (s w)"), table.rearrange("(p s) w -> p (s w)", p=P))\
      .then_inc(loaded, 16)


class Gathers:

    def __init__(self, n, m, table, width, index, name):
        self.m, self.table, self.index = m, table, index
        self.ring = n.sb(name + "ring", [P, BODY, width])
        self.rows = n.sb(name + "rows", [P, BODY], U32)
        self.rows_ready = n.sem(name + "rows_ready")
        self.issuing = n.sem(name + "issuing")
        self.landed = [n.sem(name + f"landed{q}") for q in range(NQ)]
        self.slots_used = n.sem(name + "slots_used")

    def copy_rows(self, act, turn, q):
        at = self.m.rec[:, bass.ds(turn * BODY + q * QUAD, QUAD), self.index].bitcast(U32)
        act.copy(self.rows[:, q * QUAD:(q + 1) * QUAD], at).then_inc(self.rows_ready, 1)

    def copy_next_rows(self, act, t, q):
        act.wait_ge(self.slots_used, t * BODY + (q + 1) * QUAD + QUAD)
        self.copy_rows(act, t + 1, q)

    def issue(self, pool):
        with pool.Fori(0, TURNS) as t:
            for q in range(NQ):
                pool.wait_ge(self.rows_ready, t * NQ + (q + 1))
                pool.sem_inc(self.issuing, 1)
                for k in range(q * QUAD, (q + 1) * QUAD):
                    pool.indirect_dma_start(self.ring[:, k, :], None, self.table,
                                            bass.IndirectOffsetOnAxis(self.rows[:, k:k + 1], 0))\
                        .then_inc(self.landed[q], 16)

    def wait_quad(self, eng, t, q):
        eng.wait_ge(self.landed[q], t * (16 * QUAD) + 16 * QUAD)


def message_pass(nc, m, name, records, words, index, table, heads, width, acc_at, weight=None):
    W = heads * width
    BK = -(-W // 512)
    CB = W // BK
    HB = heads // BK
    RP = 4 // BK
    HALF = BODY // 2
    H2 = 2 * heads
    attend = weight is None
    with Net(nc) as n:
        g = Gathers(n, m, table, W, index, name)
        hot = n.sb(name + "hot", [P, RING, heads, P])
        loaded = n.sem(name + "loaded")
        hot_ready = n.sem(name + "hot_ready")
        added = n.sem(name + "added")
        if attend:
            kb = n.sb(name + "kb", [P, BODY * P], BF16)
            oht = n.sb(name + "oht", [P, BODY, P])
            z = n.sb(name + "z", [P, BODY, heads])
            keys = n.sem(name + "keys")
            turned = n.sem(name + "turned")
            spread = n.sem(name + "spread")
            zs = n.sem(name + "zs")
            weighed = n.sem(name + "weighed")
            px = m.ps[:, 4, 0:BODY * H2].rearrange("p (s c) -> p s c", c=H2)
        block = n.block()

        def product(k):
            return m.ps[:, k % RP * BK:(k % RP + 1) * BK, 0:CB]

        @block.sync
        def _(sp):
            load_records(sp, m, records, loaded)
            if attend:
                def fetch(t):
                    sp.dma_start(kb[:, :], m.key_rows[bass.ds(t * BODY, BODY), :].rearrange("s e -> (s e)")
                                 .partition_broadcast(P)).then_inc(keys, 16)
                fetch(0)
                with sp.Fori(0, TURNS) as t:
                    sp.wait_ge(turned, t * 2 + 2)
                    fetch(t + 1)

        @block.gpsimd
        def _(pool):
            g.issue(pool)

        @block.scalar
        def _(act):
            def weigh(t):
                act.wait_ge(zs, t * 5 + 5)
                act.activation(m.edge_t[:, bass.ds(t * BODY, BODY), :], z[:, :, :], ACT.Exp).then_inc(weighed, 1)

            act.wait_ge(loaded, 16)
            for q in range(NQ):
                g.copy_rows(act, 0, q)
            if attend:
                weigh(0)
            with act.Fori(0, TURNS) as t:
                g.copy_next_rows(act, t, 0)
                g.copy_next_rows(act, t, 1)
                if attend:
                    weigh(t + 1)
                g.copy_next_rows(act, t, 2)
                g.copy_next_rows(act, t, 3)

        @block.tensor
        def _(pe):
            def spread_turn(t):
                tiles = load_tiles(pe, words, t * BODY, BODY)
                for h in range(2):
                    pe.wait_ge(turned, t * 2 + (h + 1))
                    for k in range(h * HALF, (h + 1) * HALF):
                        mm = pe.matmul(px[:, k, :], oht[:, k, :], m.tab[:, bass.ds(tiles[k], 1), 0:H2],
                                       start=True, stop=True)
                mm.then_inc(spread, 1)

            pe.sem_inc(g.slots_used, QUAD)
            if attend:
                spread_turn(0)
            with pe.Fori(0, TURNS) as t:
                if attend:
                    pe.wait_ge(zs, t * 5 + 5)
                    spread_turn(t + 1)
                for k in range(BODY):
                    if k % QUAD == 0:
                        g.wait_quad(pe, t, k // QUAD)
                    pe.wait_ge(added, t * BODY + (k + 1))
                    pe.wait_ge(hot_ready, t * BODY + (k + 1))
                    out = product(k)
                    for h in range(heads):
                        c = h % HB * width
                        mm = pe.matmul(out[:, h // HB, c:c + width], hot[:, k % RING, h, :],
                                       g.ring[:, k, h * width:(h + 1) * width], start=True, stop=True)
                    mm.then_inc(g.slots_used, 1)

        @block.vector
        def _(dve):
            def turn_keys(t):
                dve.wait_ge(keys, t * 16 + 16)
                for h in range(2):
                    dve.tensor_scalar(oht[:, h * HALF:(h + 1) * HALF, :].rearrange("p s e -> p (s e)"),
                                      kb[:, h * HALF * P:(h + 1) * HALF * P], m.iota_p[:, 0:1], None, ALU.is_equal)\
                       .then_inc(turned, 1)

            def scores(t):
                at = t * 5
                dve.wait_ge(spread, t + 1)
                dve.tensor_tensor(z[:, :, :], px[:, :, 0:heads], m.edge_t[:, bass.ds(t * BODY, BODY), :], ALU.add)\
                   .then_inc(zs, 1)
                dve.wait_ge(zs, at + 1)
                dve.scalar_tensor_tensor(out=z[:, :, :], in0=z[:, :, :], scalar=SLOPE, in1=z[:, :, :],
                                         op0=ALU.mult, op1=ALU.max).then_inc(zs, 1)
                dve.wait_ge(zs, at + 2)
                dve.tensor_tensor(z[:, :, :], z[:, :, :], px[:, :, heads:H2], ALU.subtract).then_inc(zs, 1)
                dve.wait_ge(zs, at + 3)
                dve.tensor_scalar(z[:, :, :], z[:, :, :], 0.0, None, ALU.min).then_inc(zs, 2)

            def build(t, k):
                slot = t * BODY + k
                dve.wait_ge(g.slots_used, t * BODY + (k + 1))
                for h in range(heads):
                    w = m.edge_t[:, bass.ds(slot, 1), h:h + 1] if attend else m.rec[:, bass.ds(slot, 1), weight:weight + 1]
                    ins = dve.tensor_scalar(hot[:, k % RING, h, :], m.iota_n[:, :], m.rec[:, bass.ds(slot, 1), 1:2],
                                            w, ALU.is_equal, ALU.mult)
                ins.then_inc(hot_ready, 1)

            def add(t, k, tiles):
                at = m.acc[:, bass.ds(tiles[k], 1), acc_at:acc_at + W].rearrange("p a (b c) -> p (a b) c", b=BK)
                dve.wait_ge(g.slots_used, t * BODY + (k + 1 + QUAD))
                dve.wait_ge(added, t * BODY + (k + RP))
                dve.tensor_tensor(at, at, product(k), ALU.add).then_inc(added, 1)

            dve.sem_inc(added, RP)
            dve.wait_ge(loaded, 16)
            if attend:
                turn_keys(0)
                scores(0)
            lag = min(3, RP)
            with dve.Fori(0, TURNS) as t:
                if attend:
                    turn_keys(t + 1)
                    dve.wait_ge(weighed, t + 1)
                tiles = load_tiles(dve, words, t * BODY, BODY)
                for k in range(BODY):
                    build(t, k)
                    if k >= lag:
                        add(t, k - lag, tiles)
                    if attend and k == HALF:
                        scores(t + 1)
                for k in range(BODY - lag, BODY):
                    add(t, k, tiles)
            dve.wait_ge(added, SLOTS + RP)


def max_pass(nc, m, name, records, words, index, table, heads, turn_rows, cleared, fetch_x):
    with Net(nc) as n:
        g = Gathers(n, m, table, heads, index, name)
        loaded = n.sem(name + "loaded")
        off = n.sb(name + "off", [P, RING, P], BF16)
        slot_max = n.sb(name + "slot_max", [P, RING, heads])
        top = n.sb(name + "top", [P, NT, heads])
        off_ready = n.sem(name + "off_ready")
        steps = n.sem(name + "steps")
        kept = n.sem(name + "kept")
        blank, made, x_in = n.sem(name + "blank"), n.sem(name + "made"), n.sem(name + "x_in")
        rows = key_rows(n, m, loaded, name + "k") if turn_rows else None
        block = n.block()
        HC = heads * P

        @block.sync
        def _(sp):
            load_records(sp, m, records, loaded)
            if rows:
                rows["sp"](sp)
            if fetch_x:
                sp.dma_start(m.acc[:, :, X_AT:X_AT + D], node_rows(m.x_kept)).then_inc(x_in, 16)
                sp.wait_ge(x_in, 16)

        @block.gpsimd
        def _(pool):
            pool.memset(m.edge_t[:, SLOTS:SL, :], 0.0).then_inc(blank, 1)
            g.issue(pool)

        @block.scalar
        def _(act):
            if rows:
                rows["act"](act)
            act.wait_ge(loaded, 16)
            for q in range(NQ):
                g.copy_rows(act, 0, q)
            with act.Fori(0, TURNS) as t:
                for q in range(NQ):
                    g.wait_quad(act, t, q)
                    act.copy(m.edge_t[:, bass.ds(t * BODY + q * QUAD, QUAD), :], g.ring[:, q * QUAD:(q + 1) * QUAD, :])\
                       .then_inc(kept, 1)
                    act.wait_ge(kept, t * NQ + (q + 1))
                    g.copy_next_rows(act, t, q)

        @block.tensor
        def _(pe):
            if rows:
                rows["pe"](pe)
            pe.sem_inc(g.slots_used, QUAD)
            pe.wait_ge(blank, 2)
            with pe.Fori(0, TURNS) as t:
                for k in range(BODY):
                    if k % QUAD == 0:
                        g.wait_quad(pe, t, k // QUAD)
                    pe.wait_ge(steps, t * (2 * BODY) + (2 * k + 2))
                    pe.wait_ge(off_ready, t * BODY + (k + 1))
                    bank = m.ps[:, 4 + k % RING, 0:HC]
                    for h in range(heads):
                        pe.matmul(bank[:, h * P:(h + 1) * P], g.ring[:, k, h:h + 1].to_broadcast([P, P]), m.ident[:, :],
                                  start=(h == 0), stop=False, skip_group_check=True)
                    for h in range(heads):
                        mm = pe.matmul(bank[:, h * P:(h + 1) * P], off[:, k % RING, :], m.ident_b[:, :],
                                       start=False, stop=(h == heads - 1), skip_group_check=True)
                    mm.then_inc(g.slots_used, 1)

        @block.vector
        def _(dve):
            dve.memset(top[:, :, :], NEG).then_inc(blank, 1)
            dve.memset(m.acc[:, :, 0:cleared], 0.0)
            dve.sem_inc(steps, 2 * RING)
            dve.wait_ge(loaded, 16)
            dve.wait_ge(blank, 2)

            def build(t, k):
                dve.wait_ge(g.slots_used, t * BODY + (k + 1))
                dve.tensor_scalar(off[:, k % RING, :], m.iota_b[:, :], m.rec[:, bass.ds(t * BODY + k, 1), 1:2], NEG,
                                  ALU.not_equal, ALU.mult).then_inc(off_ready, 1)

            def take(t, k, tiles):
                at = top[:, bass.ds(tiles[k], 1), :]
                done = t * (2 * BODY) + (2 * k + 2 * RING)
                dve.wait_ge(g.slots_used, t * BODY + (k + 1 + QUAD))
                dve.wait_ge(steps, done)
                dve.tensor_reduce(slot_max[:, k % RING, :],
                                  m.ps[:, 4 + k % RING, 0:HC].rearrange("p (h e) -> p h e", h=heads), AX.X, ALU.max)\
                   .then_inc(steps, 1)
                dve.wait_ge(steps, done + 1)
                dve.tensor_tensor(at, at, slot_max[:, k % RING:k % RING + 1, :], ALU.max).then_inc(steps, 1)

            lag = 2
            with dve.Fori(0, TURNS) as t:
                tiles = load_tiles(dve, words, t * BODY, BODY)
                for k in range(BODY):
                    build(t, k)
                    if k >= lag:
                        take(t, k - lag, tiles)
                for k in range(BODY - lag, BODY):
                    take(t, k, tiles)
            dve.wait_ge(steps, 2 * SLOTS + 2 * RING)
            s, mx = m.tab[:, :, 0:heads], m.tab[:, :, heads:2 * heads]
            dve.tensor_tensor(mx, s, top[:, :, :], ALU.add).then_inc(made, 1)
            dve.wait_ge(made, 1)
            dve.scalar_tensor_tensor(out=mx, in0=mx, scalar=SLOPE, in1=mx, op0=ALU.mult, op1=ALU.max).then_inc(made, 1)


FULL = N // P
REST = N - FULL * P
PAIRS = NT // 2


def node_rows(a):
    return a.rearrange("(j p) d -> p j d", p=P)


def flat(ap):
    return ap.rearrange("p a c -> p (a c)")


def norm_part(n, m, name, ready, count):
    st = n.sb(name + "st", [P, NT, 6])
    mean = n.sb(name + "mean", [P, NT])
    rstd = n.sb(name + "rstd", [P, NT])
    half = n.sb(name + "half", [P, NT])
    var = n.sb(name + "var", [P, NT])
    steps, root = n.sem(name + "steps"), n.sem(name + "root")

    def dve(dve):
        dve.wait_ge(ready, count)
        with dve.Fori(0, NT) as j:
            dve.bn_stats(flat(st[:, bass.ds(j, 1), :]), flat(m.acc[:, bass.ds(j, 1), X_AT:X_AT + D])).then_inc(steps, 1)
        k = NT
        dve.wait_ge(steps, k)
        dve.tensor_tensor(mean[:, :], st[:, :, 1], st[:, :, 4], ALU.add).then_inc(steps, 1)
        dve.tensor_tensor(half[:, :], st[:, :, 1], st[:, :, 4], ALU.subtract).then_inc(steps, 1)
        dve.tensor_tensor(var[:, :], st[:, :, 2], st[:, :, 5], ALU.add).then_inc(steps, 1)
        dve.wait_ge(steps, k + 3)
        dve.tensor_scalar(mean[:, :], mean[:, :], 0.5, None, ALU.mult).then_inc(steps, 1)
        dve.scalar_tensor_tensor(out=half[:, :], in0=half[:, :], scalar=0.25, in1=half[:, :], op0=ALU.mult, op1=ALU.mult)\
           .then_inc(steps, 1)
        dve.tensor_scalar(var[:, :], var[:, :], 1.0 / D, EPS, ALU.mult, ALU.add).then_inc(steps, 1)
        dve.wait_ge(steps, k + 6)
        dve.tensor_tensor(var[:, :], var[:, :], half[:, :], ALU.add).then_inc(steps, 1)
        dve.wait_ge(root, 1)
        dve.reciprocal(rstd[:, :], var[:, :]).then_inc(steps, 1)
        dve.wait_ge(steps, k + 8)

    def act(act):
        act.wait_ge(steps, NT + 7)
        act.activation(var[:, :], var[:, :], ACT.Sqrt).then_inc(root, 1)

    return {"dve": dve, "act": act}, mean, rstd


def relation_weights(n, m, name, comps, bases, root, bias, wr, scratch):
    cb = n.sb(name + "cb", [P, REL * BASES])
    bb = n.sb(name + "bb", [P, D])
    loaded, made = n.sem(name + "loaded"), n.sem(name + "made")
    bs = scratch[:, 0:2 * BASES * D].rearrange("p (k b o) -> p k b o", k=2, b=BASES)

    def sp(sp):
        for b in range(BASES):
            sp.dma_start(bs[:, :, b, :], bases[b, :, :].rearrange("(k p) o -> p k o", p=P)).then_inc(loaded, 16)
        sp.dma_start(wr[:, :, REL * D:(REL + 1) * D], root.rearrange("(k p) o -> p k o", p=P)).then_inc(loaded, 16)
        sp.dma_start(cb[:, :], comps.rearrange("r b -> (r b)").partition_broadcast(P)).then_inc(loaded, 16)
        sp.dma_start(bb[:, :], bias.partition_broadcast(P)).then_inc(loaded, 16)

    def dve(dve):
        dve.wait_ge(loaded, 16 * (BASES + 3))
        for b in range(BASES):
            if b:
                dve.wait_ge(made, REL * b)
            for r in range(REL):
                w = wr[:, :, r * D:(r + 1) * D]
                c = cb[:, r * BASES + b:r * BASES + b + 1]
                if b == 0:
                    dve.tensor_scalar(w, bs[:, :, b, :], c, None, ALU.mult).then_inc(made, 1)
                else:
                    dve.scalar_tensor_tensor(out=w, in0=bs[:, :, b, :], scalar=c, in1=w, op0=ALU.mult, op1=ALU.add)\
                       .then_inc(made, 1)
        dve.wait_ge(made, REL * BASES)

    return {"sp": sp, "dve": dve}, made, REL * BASES, bb


def turned_weights(n, m, name, weights, w):
    rows, cols = weights.shape[0] // P, weights.shape[1] // P
    raw = n.sb(name + "raw", [P, rows, cols * P])
    loaded, turned, made = n.sem(name + "loaded"), n.sem(name + "turned"), n.sem(name + "made")
    pairs = [(a, k) for a in range(rows) for k in range(cols)]
    per = len(pairs) // 2

    def place(i):
        return m.ps[:, i // per, i % per * P:(i % per + 1) * P]

    def sp(sp):
        sp.dma_start(raw[:, :, :], weights.rearrange("(a p) c -> p a c", p=P)).then_inc(loaded, 16)

    def pe(pe):
        pe.wait_ge(loaded, 16)
        for i, (a, k) in enumerate(pairs):
            pe.transpose(place(i), raw[:, a, k * P:(k + 1) * P], m.ident[:, :]).then_inc(turned, 1)
        pe.wait_ge(made, len(pairs))

    def act(act):
        for i, (a, k) in enumerate(pairs):
            act.wait_ge(turned, (i // per + 1) * per)
            act.activation(w[:, k, a * P:(a + 1) * P], place(i), ACT.Copy).then_inc(made, 1)

    return {"sp": sp, "pe": pe, "act": act}, made, len(pairs)


def transform(n, m, name, source, w, w_ready, w_count, kind, norm=None, heads=0, table=None, t_table=None,
              bias=None, vectors=None, vectors_ready=None, vectors_count=0, elu=None):
    KT, cols = w.shape[1], w.shape[2]
    banks = -(-cols // 512)
    OW = {"relation": REL * D, "support": D, "attention": cols + heads}[kind]
    xn = n.sb(name + "xn", [P, 2, KT * P])
    ht = n.sb(name + "ht", [P, 2, KT * P])
    ob = n.sb(name + "ob", [P, 2, OW])
    given = n.sem(name + "given")
    turned = n.sem(name + "turned")
    cut = n.sem(name + "cut")
    done = n.sem(name + "done")
    taken_a = n.sem(name + "taken_a")
    taken_d = n.sem(name + "taken_d")
    ob_free = n.sem(name + "ob_free")
    stored = [n.sem(name + f"stored{r}") for r in range(2)]
    owner = {"relation": "aaadd", "support": "a", "attention": "d" if bias is not None else "a"}[kind]
    share = {e: [b for b in range(banks) if owner[b] == e] for e in "ad"}
    na, nd = len(share["a"]), len(share["d"])
    product = [m.ps[:, b, 0:min(512, cols - b * 512)] for b in range(banks)]
    ps_t = [m.ps[:, 6 + r, 0:KT * P] for r in range(2)]
    if kind == "attention":
        dh = cols // heads
        dots = n.sb(name + "dots", [P, 2, 2 * heads])
        junk = n.sb(name + "junk", [P, 2 * heads, dh])
        dotted = n.sem(name + "dotted")
        ones_set = n.sem(name + "ones_set")
        ob_h = [ob[:, r, :].rearrange("p (h c) -> p h c", h=heads) for r in range(2)]
        per_tile = 2 * heads

    def sp(sp):
        sp.sem_inc(ob_free, 2)
        with sp.Fori(0, PAIRS) as i:
            for r in range(2):
                j = i * 2 + r
                if na:
                    sp.wait_ge(taken_a, j * na + 2 * na)
                if kind == "relation":
                    sp.wait_ge(taken_d, j * nd + 2 * nd)
                    z = m.z.rearrange("(q j p) d -> p q j d", q=REL, p=P)[:, :, bass.ds(j, 1), :]
                    sp.dma_start(z.rearrange("p q j d -> p q (j d)"), ob[:, r, :].rearrange("p (q d) -> p q d", q=REL))\
                      .then_inc(stored[r], 16)
                else:
                    if nd:
                        sp.wait_ge(taken_d, j * nd + 2 * nd)
                    sp.dma_start(flat(node_rows(table)[:, bass.ds(j, 1), :]), ob[:, r, :]).then_inc(stored[r], 16)
                if kind == "attention":
                    sp.wait_ge(dotted, j * (per_tile + 1) + (per_tile + 1))
                    sp.dma_start(flat(node_rows(t_table)[:, bass.ds(j, 1), :]), dots[:, r, heads:]).then_inc(stored[r], 16)
                    sp.wait_ge(stored[r], i * 32 + 32)
                else:
                    sp.wait_ge(stored[r], i * 16 + 16)
                sp.sem_inc(ob_free, 1)

    def pe(pe):
        pe.wait_ge(w_ready, w_count)
        with pe.Fori(0, PAIRS) as i:
            for r in range(2):
                j = i * 2 + r
                pe.wait_ge(given, j + 1)
                for k in range(KT):
                    mm = pe.transpose(ps_t[r][:, k * P:(k + 1) * P], xn[:, r, k * P:(k + 1) * P], m.ident[:, :])
                mm.then_inc(turned, 1)
                pe.wait_ge(cut, j + 1)
                for b in range(banks):
                    e, sem, of = owner[b], (taken_a if owner[b] == "a" else taken_d), (na if owner[b] == "a" else nd)
                    pe.wait_ge(sem, j * of + (share[e].index(b) + 1))
                    width = product[b].shape[1]
                    for k in range(KT):
                        mm = pe.matmul(product[b], ht[:, r, k * P:(k + 1) * P], w[:, k, b * 512:b * 512 + width],
                                       start=(k == 0), stop=(k == KT - 1))
                    mm.then_inc(done, 1)

    def act(act):
        if na:
            act.sem_inc(taken_a, na)
        with act.Fori(0, PAIRS) as i:
            for r in range(2):
                j = i * 2 + r
                if elu:
                    elu["act"](act, r, j)
                act.wait_ge(turned, j + 1)
                if elu:
                    act.activation(ht[:, r, :], ps_t[r], ACT.Copy, bias=-1.0).then_inc(cut, 1)
                else:
                    act.activation(ht[:, r, :], ps_t[r], ACT.Relu).then_inc(cut, 1)
                for b in share["a"]:
                    act.wait_ge(done, j * banks + (b + 1))
                    if b == share["a"][0]:
                        act.wait_ge(ob_free, j + 1)
                    if kind == "attention":
                        act.activation(ob_h[r][:, :, 0:dh], product[b].rearrange("p (h c) -> p h c", h=heads), ACT.Copy)\
                           .then_inc(taken_a, 1)
                    else:
                        width = product[b].shape[1]
                        act.activation(ob[:, r, b * 512:b * 512 + width], product[b], ACT.Copy).then_inc(taken_a, 1)

    def dve(dve):
        if nd:
            dve.sem_inc(taken_d, nd)
        if kind == "attention":
            for r in range(2):
                dve.memset(ob_h[r][:, :, dh:dh + 1], 1.0).then_inc(ones_set, 1)
            dve.wait_ge(ones_set, 2)
            dve.wait_ge(vectors_ready, vectors_count)
        with dve.Fori(0, PAIRS) as i:
            for r in range(2):
                j = i * 2 + r
                if source == "norm":
                    dve.tensor_scalar(xn[:, r, :], flat(m.acc[:, bass.ds(j, 1), X_AT:X_AT + D]),
                                      norm[0][:, bass.ds(j, 1)], norm[1][:, bass.ds(j, 1)], ALU.subtract, ALU.mult)\
                       .then_inc(given, 1)
                elif source == "acc":
                    dve.tensor_scalar(xn[:, r, :], flat(m.acc[:, bass.ds(j, 1), 0:D]), 1.0, None, ALU.mult)\
                       .then_inc(given, 1)
                else:
                    elu["dve"](dve, r, j, xn, given)
                if kind == "relation":
                    dve.wait_ge(done, j * banks + 4)
                    dve.wait_ge(ob_free, j + 1)
                    dve.tensor_copy(ob[:, r, 3 * 512:4 * 512], product[3]).then_inc(taken_d, 1)
                    dve.wait_ge(done, j * banks + 5)
                    dve.tensor_tensor(m.acc[:, bass.ds(j, 1), 0:D], product[4].rearrange("p (a c) -> p a c", a=1),
                                      bias[:, :].rearrange("p (a c) -> p a c", a=1), ALU.add).then_inc(taken_d, 1)
                elif kind == "support":
                    dve.wait_ge(taken_a, j * na + 2 * na)
                else:
                    dve.wait_ge(done, j * banks + banks)
                    dve.wait_ge(ob_free, j + 1)
                    if nd:
                        dve.tensor_tensor(ob_h[r][:, :, 0:dh], product[0].rearrange("p (h c) -> p h c", h=heads),
                                          bias[:, :].rearrange("p (h c) -> p h c", h=heads), ALU.add).then_inc(taken_d, 1)
                        dve.wait_ge(taken_d, j + 2)
                    else:
                        dve.wait_ge(taken_a, j + 2)
                    for v in range(2 * heads):
                        dve.tensor_tensor_reduce(junk[:, v, :], ob_h[r][:, v % heads, 0:dh], vectors[:, v, :], 1.0, 0.0,
                                                 ALU.mult, ALU.add, dots[:, r, v:v + 1]).then_inc(dotted, 1)
                    dve.wait_ge(dotted, j * (per_tile + 1) + per_tile)
                    dve.tensor_scalar(m.tab[:, bass.ds(j, 1), 0:heads],
                                      dots[:, r, 0:heads].rearrange("p (a c) -> p a c", a=1), 1.0, None, ALU.mult)\
                       .then_inc(dotted, 1)

    return {"sp": sp, "pe": pe, "act": act, "dve": dve}


def attention_vectors(n, name, own, other, heads, dh, bias=None):
    v = n.sb(name + "v", [P, 2 * heads, dh])
    b = n.sb(name + "b", [P, heads * dh]) if bias is not None else None
    loaded = n.sem(name + "loaded")
    count = 0
    pieces = []
    for side, a in enumerate((own, other)):
        for h in range(heads):
            pieces.append((v[:, side * heads + h, :], a[h]))
    if b is not None:
        pieces.append((b[:, :], bias))

    def sp(sp):
        for to, a in pieces:
            sp.dma_start(to, a.partition_broadcast(P)).then_inc(loaded, 16)

    return {"sp": sp}, v, b, loaded, 16 * len(pieces)


def weights_part(n, name, weights, w):
    loaded = n.sem(name + "loaded")

    def sp(sp):
        sp.dma_start(w[:, :, :], weights.rearrange("(k p) o -> p k o", p=P)).then_inc(loaded, 16)

    return {"sp": sp}, loaded, 16



def rgcn_first(n, m, a):
    wr = n.sb("r0_wr", [P, 2, (REL + 1) * D])
    cleared, x_in = n.sem("r0_cleared"), n.sem("r0_x_in")
    norm, mean, rstd = norm_part(n, m, "r0_n_", x_in, 32)
    scratch = n.sb("r0_bases", [P, 2 * BASES * D])
    made, ready, count, bb = relation_weights(n, m, "r0_w_", a.comps[0, :, :], a.bases[0, :, :, :], a.roots[0, :, :],
                                              a.biases[0, :], wr, scratch[:, :])
    tr = transform(n, m, "r0_", "norm", wr, ready, count, "relation", norm=(mean, rstd), bias=bb)

    def sp(sp):
        sp.wait_ge(cleared, 1)
        to = m.acc[:, :, X_AT:X_AT + D]
        sp.dma_start(to[:, 0:FULL, :], node_rows(a.x[0:FULL * P, :])).then_inc(x_in, 16)
        sp.dma_start(to[0:REST, FULL, :], a.x[FULL * P:N, :]).then_inc(x_in, 16)

    def dve(dve):
        dve.memset(m.acc[:, FULL:NT, X_AT:X_AT + D], 0.0).then_inc(cleared, 1)

    return [{"sp": sp, "dve": dve}, made, norm, tr]


def rgcn_second(nc, m, a):
    with Net(nc) as n:
        wr = n.sb("r1_wr", [P, 2, (REL + 1) * D])
        scratch = n.sb("r1_bases", [P, 2 * BASES * D])
        made, ready, count, bb = relation_weights(n, m, "r1_w_", a.comps[1, :, :], a.bases[1, :, :, :],
                                                  a.roots[1, :, :], a.biases[1, :], wr, scratch[:, :])
        tr = transform(n, m, "r1_", "acc", wr, ready, count, "relation", bias=bb)
        run_parts(n.block(), made, tr)


def gcn_support(nc, m, a):
    with Net(nc) as n:
        w = n.sb("g_w", [P, 2, D])
        ready = n.sem("g_ready")
        wp, wl, wc = weights_part(n, "g_w_", a.gcn_w, w)
        norm, mean, rstd = norm_part(n, m, "g_n_", ready, 1)
        tr = transform(n, m, "g_", "norm", w, wl, wc, "support", norm=(mean, rstd), table=m.support)

        def dve(dve):
            x = m.acc[:, :, X_AT:X_AT + D]
            dve.tensor_tensor(x, x, m.acc[:, :, 0:D], ALU.add).then_inc(ready, 1)

        run_parts(n.block(), {"dve": dve}, wp, norm, tr)


def gat_tables(nc, m, a):
    with Net(nc) as n:
        w = n.sb("a_w", [P, 2, D])
        ready = n.sem("a_ready")
        wp, wl, wc = weights_part(n, "a_w_", a.gat_w, w)
        heads, dh = 2, D // 2
        vp, v, b, vl, vc = attention_vectors(n, "a_v_", [a.gat_a[0:dh]] * heads, [a.gat_a[dh:2 * dh]] * heads,
                                             heads, dh, a.gat_b)
        norm, mean, rstd = norm_part(n, m, "a_n_", ready, 1)
        tr = transform(n, m, "a_", "norm", w, wl, wc, "attention", norm=(mean, rstd), heads=heads, table=m.gat_rows,
                       t_table=m.gat_t, bias=b, vectors=v, vectors_ready=vl, vectors_count=vc)
        run_parts(n.block(), {"dve": lambda dve: dve.sem_inc(ready, 1)}, wp, vp, norm, tr)


def inverse_sums(n, m, name, heads, width, least):
    inv = n.sb(name + "inv", [P, NT, heads])
    step = n.sem(name + "inv_step")
    sums = m.acc[:, :, 0:heads * width].rearrange("p j (h c) -> p j h c", h=heads)[:, :, :, width - 1]

    def dve(dve):
        dve.tensor_scalar(inv[:, :, :], sums, least, None, ALU.add).then_inc(step, 1)
        dve.wait_ge(step, 1)
        dve.reciprocal(inv[:, :, :], inv[:, :, :]).then_inc(step, 1)
        dve.wait_ge(step, 2)

    return {"dve": dve}, inv, sums


def gat_first_of_two(nc, m, a):
    with Net(nc) as n:
        heads, dh = 2, D // 2
        own = n.sb("b_own", [P, NT, heads * (dh + 1)])
        none = n.sb("b_none", [P, NT, heads])
        step, ready, own_in, kept = n.sem("b_step"), n.sem("b_ready"), n.sem("b_own_in"), n.sem("b_kept")
        inv = n.sb("b_inv", [P, NT, heads])
        sums = m.acc[:, :, 0:heads * (dh + 1)].rearrange("p j (h c) -> p j h c", h=heads)[:, :, :, dh]

        def sp(sp):
            sp.dma_start(own[:, :, :], node_rows(m.gat_rows)).then_inc(own_in, 16)

        def dve(dve):
            dve.tensor_scalar(none[:, :, :], sums, 0.0, None, ALU.is_equal).then_inc(step, 1)
            dve.wait_ge(step, 1)
            dve.tensor_tensor(inv[:, :, :], sums, none[:, :, :], ALU.add).then_inc(step, 1)
            dve.wait_ge(step, 2)
            dve.reciprocal(inv[:, :, :], inv[:, :, :]).then_inc(step, 1)
            dve.wait_ge(own_in, 16)
            dve.wait_ge(step, 3)
            k = 3
            for h in range(heads):
                x = m.acc[:, :, X_AT + h * dh:X_AT + (h + 1) * dh]
                got = m.acc[:, :, h * (dh + 1):h * (dh + 1) + dh]
                self_row = own[:, :, h * (dh + 1):h * (dh + 1) + dh]
                dve.tensor_tensor(got, got, inv[:, :, h:h + 1].to_broadcast([P, NT, dh]), ALU.mult).then_inc(step, 1)
                dve.tensor_tensor(self_row, self_row, none[:, :, h:h + 1].to_broadcast([P, NT, dh]), ALU.mult)\
                   .then_inc(step, 1)
                dve.wait_ge(step, k + 1)
                dve.tensor_tensor(x, x, got, ALU.add).then_inc(step, 1)
                dve.wait_ge(step, k + 3)
                dve.tensor_tensor(x, x, self_row, ALU.add).then_inc(step, 1)
                k += 4
            dve.wait_ge(step, k)
            dve.sem_inc(ready, 1)

        def keep(sp):
            sp.wait_ge(ready, 1)
            sp.dma_start(node_rows(m.x_kept), m.acc[:, :, X_AT:X_AT + D]).then_inc(kept, 16)
            sp.wait_ge(kept, 16)

        run_parts(n.block(), {"sp": sp, "dve": dve}, {"sp": keep})
    with Net(nc) as n:
        heads, dh = 4, P
        w = n.sb("c_w", [P, 2, heads * dh])
        ready = n.sem("c_ready")
        wp, wl, wc = turned_weights(n, m, "c_w_", a.w1, w)
        vp, v, b, vl, vc = attention_vectors(n, "c_v_", [a.a_dst1[0, h, :] for h in range(heads)],
                                             [a.a_src1[0, h, :] for h in range(heads)], heads, dh)
        norm, mean, rstd = norm_part(n, m, "c_n_", ready, 1)
        tr = transform(n, m, "c_", "norm", w, wl, wc, "attention", norm=(mean, rstd), heads=heads, table=m.rows1,
                       t_table=m.t1, vectors=v, vectors_ready=vl, vectors_count=vc)
        run_parts(n.block(), {"dve": lambda dve: dve.sem_inc(ready, 1)}, wp, vp, norm, tr)


def gat_second_of_two(nc, m, a):
    heads, dh = 4, P
    with Net(nc) as n:
        w = n.sb("d_w", [P, 4, D])
        wp, wl, wc = turned_weights(n, m, "d_w_", a.w2, w)
        vp, v, b, vl, vc = attention_vectors(n, "d_v_", [a.a_dst2[0, 0, :]], [a.a_src2[0, 0, :]], 1, D)
        ip, inv, sums = inverse_sums(n, m, "d_", heads, dh + 1, 1e-16)
        b1 = n.sb("d_b1", [P, heads * dh])
        y = n.sb("d_y", [P, 2, heads * dh])
        low = n.sb("d_low", [P, 2, heads * dh])
        b_in, steps, raised = n.sem("d_b_in"), n.sem("d_steps"), n.sem("d_raised")
        PER = heads + 1

        def elu_dve(dve, r, j, xn, given):
            for h in range(heads):
                dve.scalar_tensor_tensor(out=y[:, r, h * dh:(h + 1) * dh],
                                         in0=flat(m.acc[:, bass.ds(j, 1), h * (dh + 1):h * (dh + 1) + dh]),
                                         scalar=flat(inv[:, bass.ds(j, 1), h:h + 1]), in1=b1[:, h * dh:(h + 1) * dh],
                                         op0=ALU.mult, op1=ALU.add).then_inc(steps, 1)
            dve.wait_ge(steps, j * PER + heads)
            dve.tensor_scalar(low[:, r, :], y[:, r, :], 0.0, None, ALU.min).then_inc(steps, 1)
            dve.wait_ge(raised, j + 1)
            dve.scalar_tensor_tensor(out=xn[:, r, :], in0=y[:, r, :], scalar=0.0, in1=low[:, r, :],
                                     op0=ALU.max, op1=ALU.add).then_inc(given, 1)

        def elu_act(act, r, j):
            act.wait_ge(steps, j * PER + PER)
            act.activation(low[:, r, :], low[:, r, :], ACT.Exp).then_inc(raised, 1)

        tr = transform(n, m, "d_", "elu", w, wl, wc, "attention", heads=1, table=m.rows2, t_table=m.t2,
                       vectors=v, vectors_ready=vl, vectors_count=vc, elu={"dve": elu_dve, "act": elu_act})
        run_parts(n.block(), {"sp": lambda sp: sp.dma_start(b1[:, :], a.b1.partition_broadcast(P)).then_inc(b_in, 16),
                              "dve": lambda dve: dve.wait_ge(b_in, 16)}, wp, vp, ip, tr)


def finish(nc, m, a, out):
    with Net(nc) as n:
        ip, inv, sums = inverse_sums(n, m, "f_", 1, D + 1, 1e-16)
        b2 = n.sb("f_b2", [P, D])
        b_in, step, stored = n.sem("f_b_in"), n.sem("f_step"), n.sem("f_stored")
        x, got = m.acc[:, :, X_AT:X_AT + D], m.acc[:, :, 0:D]
        b_all = b2[:, :].unsqueeze(1).to_broadcast([P, NT, D])

        def sp(sp):
            sp.dma_start(b2[:, :], a.b2.partition_broadcast(P)).then_inc(b_in, 16)
            sp.wait_ge(step, 3)
            sp.dma_start(node_rows(out[0:FULL * P, :]), x[:, 0:FULL, :]).then_inc(stored, 16)
            sp.dma_start(out[FULL * P:N, :], x[0:REST, FULL, :]).then_inc(stored, 16)
            sp.wait_ge(stored, 32)

        def dve(dve):
            dve.tensor_tensor(got, got, inv[:, :, 0:1].to_broadcast([P, NT, D]), ALU.mult).then_inc(step, 1)
            dve.wait_ge(b_in, 16)
            dve.wait_ge(step, 1)
            dve.tensor_tensor(x, x, got, ALU.add).then_inc(step, 1)
            dve.wait_ge(step, 2)
            dve.tensor_tensor(x, x, b_all, ALU.add).then_inc(step, 1)

        run_parts(n.block(), ip, {"sp": sp, "dve": dve})


def build(nc, a, out, upto=99):
    m = named()
    dram = nc.dram_tensor
    m.rec_dst = dram("rec_dst", [P * SL, 4], F32).ap()
    m.rec_src = dram("rec_src", [P * SL, 4], F32).ap()
    m.key_rows = dram("key_rows", [SL, P], BF16).ap()
    m.z = dram("z", [REL * NP, D], F32).ap()
    m.support = dram("support", [NP, D], F32).ap()
    m.gat_rows = dram("gat_rows", [NP, D + 2], F32).ap()
    m.gat_t = dram("gat_t", [NP, 2], F32).ap()
    m.rows1 = dram("rows1", [NP, 4 * (P + 1)], F32).ap()
    m.t1 = dram("t1", [NP, 4], F32).ap()
    m.rows2 = dram("rows2", [NP, D + 1], F32).ap()
    m.t2 = dram("t2", [NP, 1], F32).ap()
    m.x_kept = dram("x_kept", [NP, D], F32).ap()
    with Net(nc) as n:
        m.ps = n.ps("ps", [P, 8, 512])
        m.iota_n, m.iota_p = n.sb("iota_n", [P, P]), n.sb("iota_p", [P, 1])
        m.iota_b, m.ident_b = n.sb("iota_b", [P, P], BF16), n.sb("ident_b", [P, P], BF16)
        m.ident = n.sb("ident", [P, P])
        m.words_dst = n.sb("words_dst", [1, SL // PACK], I32)
        m.words_src = n.sb("words_src", [1, SL // PACK], I32)
        m.rec = n.sb("rec", [P, SL, 4])
        m.acc = n.sb("acc", [P, NT, W_ACC])
        sort_edges(nc, m, a)
        if upto < 1: return
        message_pass(nc, m, "p0_", m.rec_dst, m.words_dst, 0, m.z, 1, D, 0, weight=3)
        rgcn_second(nc, m, a)
        message_pass(nc, m, "p1_", m.rec_dst, m.words_dst, 0, m.z, 1, D, 0, weight=3)
        if upto < 2: return
        gcn_support(nc, m, a)
        message_pass(nc, m, "p2_", m.rec_src, m.words_src, 0, m.support, 1, D, X_AT, weight=2)
        if upto < 3: return
        for i, (heads, width, tables, rec, words, index, rows, t) in enumerate((
                (2, P + 1, gat_tables, m.rec_src, m.words_src, 0, m.gat_rows, m.gat_t),
                (4, P + 1, gat_first_of_two, m.rec_dst, m.words_dst, 2, m.rows1, m.t1),
                (1, D + 1, gat_second_of_two, m.rec_dst, m.words_dst, 2, m.rows2, m.t2))):
            with Net(nc) as k:
                m.tab = k.sb(f"tab{i}", [P, NT, 2 * heads])
                tables(nc, m, a)
                with Net(nc) as e:
                    m.edge_t = e.sb(f"edge_t{i}", [P, SL, heads])
                    max_pass(nc, m, f"m{i}_", rec, words, index, t, heads, i < 2, heads * width, i == 2)
                    message_pass(nc, m, f"q{i}_", rec, words, index, rows, heads, width, 0)
            if upto < 4 + i: return
        finish(nc, m, a, out)


def sort_edges(nc, m, a):
    with Net(nc) as k:
        row_b = k.sb("row_b", [P, COLS], U32)
        rec_b = k.sb("rec_b", [P, COLS, 4])
        with Net(nc) as n:
            m.ones, m.below = n.sb("ones", [P, P]), n.sb("below", [P, P])
            m.iota_s = n.sb("iota_s", [P, SL])
            constants(nc, m)
            column = {name: n.sb("s_" + name, [P, COLS], dt) for name, dt in
                      (("src", I32), ("dst", I32), ("etype", I32), ("weight", F32), ("typef", F32), ("srcf", F32))}
            s = named(rec_b=rec_b, rec_a=m.rec[:, 0:COLS, :], **column)
            s.by_dst = named(tile=n.sb("d_tile", [P, COLS]), key=n.sb("d_key", [P, COLS]),
                                       row=n.sb("d_row", [P, COLS], U32), words=m.words_dst)
            s.by_src = named(tile=s.typef, key=s.srcf, row=row_b, words=m.words_src)
            rank_by_dst(nc, m, s, a.src, a.dst, a.etype, a.weight)
            with Net(nc) as e:
                rank = rank_by_src(nc, e, m, s)
                run_parts(e.block(), rank,
                          {"pool": lambda pool: scatter_records(pool, e, s.by_dst.row, s.rec_a, m.rec_dst, "sa_")})
        with Net(nc) as n:
            parts = [inverse_counts(nc, n, m)] + rgcn_first(n, m, a)
            run_parts(n.block(), *parts,
                      {"pool": lambda pool: scatter_records(pool, n, row_b, rec_b, m.rec_src, "sb_")})


_INS = {"x": "x", "src": "src", "dst": "dst", "edge_type_8": "etype", "edge_weight": "weight",
        "L0_gnn_comps": "comps", "L0_gnn_bases": "bases", "L0_gnn_roots": "roots", "L0_gnn_biases": "biases",
        "L1_gnn_weight": "gcn_w", "L2_gnn_W_w": "gat_w", "L2_gnn_W_b": "gat_b", "L2_gnn_a": "gat_a",
        "L3_gnn_W1": "w1", "L3_gnn_a_src1": "a_src1", "L3_gnn_a_dst1": "a_dst1", "L3_gnn_b1": "b1",
        "L3_gnn_W2": "w2", "L3_gnn_a_src2": "a_src2", "L3_gnn_a_dst2": "a_dst2", "L3_gnn_b2": "b2"}


def kernel(**inputs):
    import concourse.bacc as _bacc
    from concourse.bass_utils import run_bass_kernel_spmd as _run

    nc = _bacc.Bacc("TRN2", target_bir_lowering=False, num_devices=1)
    arrays, aps = {}, {}
    for name, short in _INS.items():
        v = np.ascontiguousarray(inputs[name])
        arrays[f"in_{name}"] = v
        aps[short] = nc.dram_tensor(f"in_{name}", v.shape, mybir.dt.from_np(v.dtype), kind="ExternalInput").ap()
    out = nc.dram_tensor("out_x", (N, D), F32, kind="ExternalOutput").ap()
    build(nc, named(**aps), out)
    return _run(nc, [arrays], core_ids=[0]).results[0]["out_x"]
```

```python
from contextlib import ExitStack

import numpy as np
import concourse.bass as bass
from concourse import mybir

ALU = mybir.AluOpType
ACT = mybir.ActivationFunctionType
AX = mybir.AxisListType
F32 = mybir.dt.float32
BF16 = mybir.dt.bfloat16
I32 = mybir.dt.int32
U32 = mybir.dt.uint32

P = 128
N = 6250
E = 100000
D = 256
REL, BASES = 8, 4
NT = -(-N // P)
NT += NT % 2
PAD_NODE = (NT - 1) * P
NP = NT * P
COLS = -(-E // P)
BODY = 16
QUAD = 4
NQ = BODY // QUAD
SLOTS = -(-((COLS * P + (P - 1) * NT) // P) // BODY) * BODY
TURNS = SLOTS // BODY
SL = SLOTS + BODY
PACK = 4
BITS = 6
KEY_NONE = 999.0
W_ACC = 516
X_AT = W_ACC - D
NEG = -1.0e30
EPS = 1e-5
SLOPE = 0.2
RING = 4
HOTS = 8
LEAD = 4
GROUP = next(g for g in range(20, 0, -1) if COLS % (2 * g) == 0)
assert NT <= 1 << BITS and SL % PACK == 0


def named(**parts):
    return type("Named", (), parts)


class Net:

    def __init__(self, nc):
        self.nc, self.ctx, self.sems = nc, ExitStack(), []

    def __enter__(self):
        self.ctx.__enter__()
        return self

    def __exit__(self, *a):
        done = self.ctx.__exit__(*a)
        if self.sems and not a[0]:
            self.nc.clear_and_free_semaphores(self.sems)
            self.nc.all_engine_barrier()
        return done

    def sb(self, name, shape, dt=F32):
        return self.ctx.enter_context(self.nc.sbuf_tensor(name, shape, dt))

    def ps(self, name, shape, dt=F32):
        return self.ctx.enter_context(self.nc.psum_tensor(name, shape, dt))

    def sem(self, name):
        self.sems.append(self.nc.alloc_semaphore(name=name))
        return self.sems[-1]

    def block(self):
        return self.ctx.enter_context(self.nc.Block())


def edges_as_tiles(a):
    full = E // COLS
    rest = E - full * COLS
    return ((0, full, COLS, a[0:full * COLS].rearrange("(p c) -> p c", c=COLS)),
            (full, full + 1, rest, a[full * COLS:E].rearrange("(p c) -> p c", p=1)))


def constants(nc, m):
    with Net(nc) as n:
        made = n.sem("c_made")
        moved = n.sem("c_moved")
        block = n.block()

        @block.gpsimd
        def _(pool):
            pool.iota(m.iota_n[:, :], [[1, P]], base=0, channel_multiplier=0,
                      allow_small_or_imprecise_dtypes=True).then_inc(made, 1)
            pool.iota(m.iota_b[:, :], [[1, P]], base=0, channel_multiplier=0,
                      allow_small_or_imprecise_dtypes=True).then_inc(made, 1)
            pool.iota(m.iota_p[:, :], [[0, 1]], base=0, channel_multiplier=1,
                      allow_small_or_imprecise_dtypes=True).then_inc(made, 1)
            pool.iota(m.iota_s[:, :], [[1, SL]], base=0, channel_multiplier=0,
                      allow_small_or_imprecise_dtypes=True).then_inc(made, 1)
            pool.memset(m.ones[:, :], 1.0).then_inc(made, 1)

        @block.vector
        def _(dve):
            dve.wait_ge(made, 5)
            dve.tensor_scalar(m.ident[:, :], m.iota_n[:, :], m.iota_p[:, 0:1], None, ALU.is_equal).then_inc(moved, 1)
            dve.tensor_scalar(m.ident_b[:, :], m.iota_n[:, :], m.iota_p[:, 0:1], None, ALU.is_equal).then_inc(moved, 1)
            dve.tensor_scalar(m.below[:, :], m.iota_n[:, :], m.iota_p[:, 0:1], None, ALU.is_gt).then_inc(moved, 1)


def rank_edges(nc, n, m, s, key, name):
    last = COLS - 1
    c = named(
        tot=n.sb(name + "tot", [P, NT]), mask=n.sb(name + "mask", [P, COLS]), cum=n.sb(name + "cum", [P, COLS]),
        sel=n.sb(name + "sel", [P, COLS]), place=n.sb(name + "place", [P, COLS]),
        zero=n.sb(name + "zero", [P, COLS]), base=n.sb(name + "base", [P, NT]),
        count=n.sb(name + "count", [NT, 1]), count_i=n.sb(name + "count_i", [NT, 1], I32),
        slots_i=n.sb(name + "slots_i", [NT, 1], I32), slots=n.sb(name + "slots", [NT, 1]),
        first=n.sb(name + "first", [NT, 1]), begun=n.sb(name + "begun", [NT, SL]),
        word=n.sb(name + "word", [1, SL // PACK]), place_i=n.sb(name + "place_i", [P, COLS], I32),
        lane=n.sb(name + "lane", [P, COLS], I32), slot=n.sb(name + "slot", [P, COLS], I32),
        small=m.ps[:, 0, :], wide=m.ps[:, 1:3, :])
    chain = n.sem(name + "chain")
    counted = n.sem(name + "counted")
    half = SL // 2

    def vector(dve, loaded, loads):
        k = 0
        dve.wait_ge(loaded, loads)
        dve.tensor_scalar(c.place_i[:, :], key[:, :], 7, None, ALU.logical_shift_right).then_inc(chain, 1)
        dve.tensor_scalar(c.lane[:, :], key[:, :], P - 1, None, ALU.bitwise_and).then_inc(chain, 1)
        dve.memset(c.zero[:, :], 0.0).then_inc(chain, 1)
        dve.memset(c.place[:, :], 0.0).then_inc(chain, 1)
        k = 4
        dve.wait_ge(chain, k)
        dve.tensor_copy(s.tile[:, :], c.place_i[:, :]).then_inc(chain, 1)
        dve.tensor_copy(s.key[:, :], c.lane[:, :]).then_inc(chain, 1)
        k += 2
        dve.wait_ge(chain, k)
        with dve.Fori(0, NT) as b:
            dve.wait_ge(chain, b + k)
            dve.tensor_scalar(c.mask[:, :], s.tile[:, :], m.iota_n[:, bass.ds(b, 1)], None, ALU.is_equal,
                              ALU.add, accum_out=c.tot[:, bass.ds(b, 1)]).then_inc(chain, 1)
        k += NT
        dve.wait_ge(counted, 1)
        dve.wait_ge(chain, k)
        dve.tensor_scalar(c.count_i[:, :], c.small[0:NT, 0:1], float(P - 1), None, ALU.add).then_inc(chain, 1)
        dve.wait_ge(chain, k + 1)
        dve.tensor_scalar(c.slots_i[:, :], c.count_i[:, :], 7, None, ALU.logical_shift_right).then_inc(chain, 1)
        dve.wait_ge(chain, k + 2)
        dve.tensor_copy(c.slots[:, :], c.slots_i[:, :]).then_inc(chain, 1)
        k += 3
        dve.wait_ge(counted, 4)
        dve.tensor_scalar(c.base[:, :], c.small[:, 64:64 + NT], float(P), None, ALU.mult).then_inc(chain, 1)
        dve.wait_ge(chain, k + 1)
        dve.tensor_tensor(c.base[:, :], c.base[:, :], c.small[:, 128:128 + NT], ALU.add).then_inc(chain, 1)
        dve.tensor_copy(c.first[:, :], c.small[0:NT, 1:2]).then_inc(chain, 1)
        k += 3
        dve.wait_ge(chain, k)
        dve.tensor_scalar(c.begun[:, :], m.iota_s[0:NT, :], c.first[:, 0:1], None, ALU.is_ge).then_inc(chain, 1)
        k += 1
        with dve.Fori(0, NT) as b:
            dve.wait_ge(chain, b * 4 + k)
            dve.tensor_scalar(c.mask[:, :], s.tile[:, :], m.iota_n[:, bass.ds(b, 1)], None, ALU.is_equal).then_inc(chain, 1)
            dve.wait_ge(chain, b * 4 + (k + 1))
            dve.tensor_tensor_scan(c.cum[:, :], c.mask[:, :], c.zero[:, :], c.base[:, bass.ds(b, 1)],
                                   ALU.add, ALU.add).then_inc(chain, 1)
            dve.wait_ge(chain, b * 4 + (k + 2))
            dve.tensor_tensor(c.sel[:, :], c.mask[:, :], c.cum[:, :], ALU.mult).then_inc(chain, 1)
            dve.wait_ge(chain, b * 4 + (k + 3))
            dve.tensor_tensor(c.place[:, :], c.place[:, :], c.sel[:, :], ALU.add).then_inc(chain, 1)
        k += 4 * NT
        dve.wait_ge(chain, k)
        dve.tensor_scalar(c.place_i[:, :], c.place[:, :], -1.0, None, ALU.add).then_inc(chain, 1)
        dve.wait_ge(chain, k + 1)
        dve.tensor_scalar(c.lane[:, :], c.place_i[:, :], P - 1, None, ALU.bitwise_and).then_inc(chain, 1)
        dve.tensor_scalar(c.slot[:, :], c.place_i[:, :], 7, None, ALU.logical_shift_right).then_inc(chain, 1)
        dve.wait_ge(chain, k + 3)
        dve.tensor_copy(c.cum[:, :], c.lane[:, :]).then_inc(chain, 1)
        dve.tensor_copy(c.sel[:, :], c.slot[:, :]).then_inc(chain, 1)
        dve.wait_ge(chain, k + 5)
        dve.scalar_tensor_tensor(out=s.row[:, :], in0=c.cum[:, :], scalar=float(SL), in1=c.sel[:, :],
                                 op0=ALU.mult, op1=ALU.add).then_inc(chain, 1)
        k += 6
        dve.wait_ge(counted, 6)
        t = [c.wide[0:1, h, 0:half].rearrange("o (w q) -> o w q", q=PACK) for h in range(2)]
        hw = half // PACK
        for h in range(2):
            w = c.word[:, h * hw:(h + 1) * hw]
            dve.tensor_scalar(w, t[h][:, :, PACK - 1], -1.0, None, ALU.add).then_inc(chain, 1)
            k += 1
            for q in range(PACK - 2, -1, -1):
                dve.wait_ge(chain, k)
                dve.tensor_scalar(w, w, float(1 << BITS), -1.0, ALU.mult, ALU.add).then_inc(chain, 1)
                dve.wait_ge(chain, k + 1)
                dve.tensor_tensor(w, w, t[h][:, :, q], ALU.add).then_inc(chain, 1)
                k += 2
        dve.wait_ge(chain, k)
        dve.tensor_copy(s.words[:, :], c.word[:, :]).then_inc(chain, 1)
        dve.wait_ge(chain, k + 1)
        return k + 1

    def tensor(pe, dve_before):
        k = dve_before + 6 + NT
        pe.wait_ge(chain, k)
        pe.matmul(c.small[0:NT, 0:1], c.tot[:, :], m.ones[:, 0:1], start=True, stop=True).then_inc(counted, 1)
        pe.wait_ge(chain, k + 3)
        pe.matmul(c.small[0:NT, 1:2], m.below[0:NT, 0:NT], c.slots[:, :], start=True, stop=True).then_inc(counted, 1)
        pe.matmul(c.small[:, 64:64 + NT], c.slots[:, 0:1].to_broadcast([NT, P]), m.below[0:NT, 0:NT],
                  start=True, stop=True).then_inc(counted, 1)
        pe.matmul(c.small[:, 128:128 + NT], m.below[:, :], c.tot[:, :], start=True, stop=True).then_inc(counted, 1)
        pe.wait_ge(chain, k + 7)
        for h in range(2):
            pe.matmul(c.wide[:, h, 0:half], m.ones[0:NT, :], c.begun[:, h * half:(h + 1) * half],
                      start=True, stop=True).then_inc(counted, 1)

    return vector, tensor


def rank_by_dst(nc, m, s, src, dst, etype, weight):
    with Net(nc) as n:
        loaded, filled, stored = n.sem("ld_edges"), n.sem("ld_filled"), n.sem("ld_stored")
        empty = n.sb("empty", [P, SL, 4])
        vector, tensor = rank_edges(nc, n, m, s.by_dst, s.dst, "rd_")
        blank, built = n.sem("ld_blank"), n.sem("ld_built")
        block = n.block()

        @block.gpsimd
        def _(pool):
            for a, v in ((s.src, PAD_NODE), (s.dst, PAD_NODE), (s.etype, 0)):
                pool.memset(a[:, :], v).then_inc(filled, 1)
            pool.memset(s.weight[:, :], 0.0).then_inc(filled, 1)
            pool.memset(empty[:, :, :], 0.0).then_inc(blank, 1)
            pool.wait_ge(blank, 1)
            pool.memset(empty[:, :, 1:2], KEY_NONE).then_inc(blank, 1)

        @block.sync
        def _(sp):
            sp.wait_ge(filled, 4)
            for a, d in ((s.dst, dst), (s.src, src), (s.etype, etype), (s.weight, weight)):
                for p0, p1, w, piece in edges_as_tiles(d):
                    sp.dma_start(a[p0:p1, 0:w], piece).then_inc(loaded, 16)
            sp.wait_ge(blank, 2)
            for rec in (m.rec_dst, m.rec_src):
                sp.dma_start(rec.rearrange("(p s) w -> p (s w)", p=P),
                             empty[:, :, :].rearrange("p s w -> p (s w)")).then_inc(stored, 16)
            sp.wait_ge(stored, 32)

        @block.tensor
        def _(pe):
            tensor(pe, 0)

        @block.vector
        def _(dve):
            vector(dve, loaded, 16 * 8)
            dve.tensor_copy(s.typef[:, :], s.etype[:, :]).then_inc(built, 1)
            dve.tensor_copy(s.srcf[:, :], s.src[:, :]).then_inc(built, 1)
            r = s.rec_a
            dve.wait_ge(built, 2)
            dve.scalar_tensor_tensor(out=r[:, :, 0].bitcast(U32), in0=s.typef[:, :], scalar=float(NP), in1=s.srcf[:, :],
                                     op0=ALU.mult, op1=ALU.add).then_inc(built, 1)
            dve.tensor_copy(r[:, :, 1], s.by_dst.key[:, :]).then_inc(built, 1)
            dve.tensor_copy(r[:, :, 2].bitcast(I32), s.src[:, :]).then_inc(built, 1)
            dve.tensor_copy(r[:, :, 3], s.typef[:, :]).then_inc(built, 1)
            dve.wait_ge(built, 6)


def scatter_records(pool, n, rows, rec, table, name):
    copied = n.sem(name + "copied")
    issuing = n.sem(name + "issuing")
    landed = [n.sem(name + f"landed{h}") for h in range(2)]
    ring_r = n.sb(name + "ring_r", [P, 2, GROUP], U32)
    ring_d = n.sb(name + "ring_d", [P, 2, GROUP, 4])

    def group(c, h, i):
        at = c * GROUP
        pool.tensor_copy(ring_r[:, h, :], rows[:, bass.ds(at, GROUP)]).then_inc(copied, 1)
        pool.tensor_copy(ring_d[:, h, :, :], rec[:, bass.ds(at, GROUP), :]).then_inc(copied, 1)
        pool.wait_ge(copied, c * 2 + 2)
        pool.sem_inc(issuing, 1)
        for g in range(GROUP):
            pool.indirect_dma_start(table, bass.IndirectOffsetOnAxis(ring_r[:, h, g:g + 1], 0),
                                    ring_d[:, h, g, :], None).then_inc(landed[h], 16)

    for h in range(2):
        group(h, h, 0)
    with pool.Fori(1, COLS // (2 * GROUP)) as i:
        for h in range(2):
            pool.wait_ge(landed[h], i * (16 * GROUP))
            group(i * 2 + h, h, i)
    for h in range(2):
        pool.wait_ge(landed[h], 16 * GROUP * (COLS // (2 * GROUP)))


def run_parts(block, *parts):
    @block.sync
    def _(sp):
        for p in parts:
            if "sp" in p:
                p["sp"](sp)

    @block.tensor
    def _(pe):
        for p in parts:
            if "pe" in p:
                p["pe"](pe)

    @block.vector
    def _(dve):
        for p in parts:
            if "dve" in p:
                p["dve"](dve)

    @block.scalar
    def _(act):
        for p in parts:
            if "act" in p:
                p["act"](act)

    @block.gpsimd
    def _(pool):
        for p in parts:
            if "pool" in p:
                p["pool"](pool)


def load_tiles(eng, words, slot, count):
    out = []
    for w in range(count // PACK):
        word = eng.value_load(words[0:1, bass.ds(slot // PACK + w, 1)], min_val=0, max_val=(1 << BITS * PACK) - 1)
        for q in range(PACK):
            v = (word >> (BITS * q)) & ((1 << BITS) - 1)
            out.append(eng.snap(v.with_bounds(min_val=0, max_val=NT - 1)))
    return out


def rank_by_src(nc, n, m, s):
    vector, tensor = rank_edges(nc, n, m, s.by_src, s.src, "rs_")
    ready, built = n.sem("rs_ready"), n.sem("rs_built")

    def dve(dve):
        dve.sem_inc(ready, 1)
        vector(dve, ready, 1)
        r = s.rec_b
        dve.tensor_copy(r[:, :, 0].bitcast(I32), s.dst[:, :]).then_inc(built, 1)
        dve.tensor_copy(r[:, :, 1], s.by_src.key[:, :]).then_inc(built, 1)
        dve.tensor_copy(r[:, :, 2], s.weight[:, :]).then_inc(built, 1)
        dve.memset(r[:, :, 3], 0.0).then_inc(built, 1)
        dve.wait_ge(built, 4)

    return {"dve": dve, "pe": lambda pe: tensor(pe, 0)}


def key_rows(n, m, loaded, name):
    blocks = -(-SL // P)
    turned, copied, stored = n.sem(name + "turned"), n.sem(name + "copied"), n.sem(name + "stored")
    kt = n.sb(name + "kt", [P, blocks, P], BF16)
    pt = m.ps[:, 0:2, :]

    def width(b):
        return min(P, SL - b * P)

    def view(b):
        return pt[0:width(b), b // 4, (b % 4) * P:(b % 4 + 1) * P]

    def pe(pe):
        pe.wait_ge(loaded, 16)
        for b in range(blocks):
            pe.transpose(view(b), m.rec[:, b * P:b * P + width(b), 1], m.ident[:, :]).then_inc(turned, 1)
        pe.wait_ge(copied, blocks)

    def act(act):
        for b in range(blocks):
            act.wait_ge(turned, min(b // 4 * 4 + 4, blocks))
            act.activation(kt[0:width(b), b, :], view(b), ACT.Copy).then_inc(copied, 1)

    def sp(sp):
        sp.wait_ge(copied, blocks)
        for b in range(blocks):
            sp.dma_start(m.key_rows[b * P:b * P + width(b), :], kt[0:width(b), b, :]).then_inc(stored, 16)
        sp.wait_ge(stored, 16 * blocks)

    return {"pe": pe, "act": act, "sp": sp}


def inverse_counts(nc, n, m):
    loaded = n.sem("ic_loaded")
    rows = key_rows(n, m, loaded, "kd_")
    HALF = BODY // 2
    HALVES = 2 * TURNS
    oh = n.sb("ic_oh", [P, HOTS, P], BF16)
    rel = n.sb("ic_rel", [P, BODY, REL], BF16)
    cnt = n.sb("ic_cnt", [P, NT, REL])
    kb = n.sb("ic_kb", [P, BODY * P], BF16)
    oht = n.sb("ic_oht", [P, BODY, P])
    inv_of = n.sb("ic_inv_of", [P, BODY, REL])
    rel_f = n.sb("ic_rel_f", [P, BODY, REL])
    prod = n.sb("ic_prod", [P, BODY, REL])
    per_edge = n.sb("ic_per_edge", [P, BODY])
    pc = [m.ps[:, 2 + k % RING, 0:REL] for k in range(BODY)]
    px = [m.ps[:, 6 + h, 0:HALF * REL] for h in range(2)]
    begun, inv, stored = n.sem("ic_begun"), n.sem("ic_inv"), n.sem("ic_stored")
    rel_ready = n.sem("ic_rel_ready")
    built = n.sem("ic_built")
    counted = n.sem("ic_counted")
    added = n.sem("ic_added")
    got = [n.sem(f"ic_got{h}") for h in range(2)]
    turned = n.sem("ic_turned")
    rows_set = n.sem("ic_rows_set")
    spread = n.sem("ic_spread")
    rel_set = n.sem("ic_rel_set")
    chosen = n.sem("ic_chosen")
    summed = n.sem("ic_summed")
    wrote = n.sem("ic_wrote")

    def sp(sp):
        sp.dma_start(m.rec[:, :, :].rearrange("p s w -> p (s w)"),
                     m.rec_dst.rearrange("(p s) w -> p (s w)", p=P)).then_inc(loaded, 16)
        rows["sp"](sp)

        def fetch(t, h):
            keys = m.key_rows[bass.ds(t * BODY + h * HALF, HALF), :].rearrange("s e -> (s e)")
            sp.dma_start(kb[:, h * HALF * P:(h + 1) * HALF * P], keys.partition_broadcast(P)).then_inc(got[h], 16)

        for h in range(2):
            fetch(0, h)
        with sp.Fori(0, TURNS) as t:
            for h in range(2):
                sp.wait_ge(turned, t * 2 + (h + 1))
                fetch(t + 1, h)
        sp.wait_ge(wrote, HALVES)
        sp.dma_start(m.rec_dst.rearrange("(p s) w -> p (s w)", p=P),
                     m.rec[:, :, :].rearrange("p s w -> p (s w)")).then_inc(stored, 16)
        sp.wait_ge(stored, 16)
        for h in range(2):
            sp.wait_ge(got[h], 16 * (TURNS + 1))

    def pe(pe):
        rows["pe"](pe)
        pe.sem_inc(counted, HOTS)
        with pe.Fori(0, TURNS) as t:
            for k in range(BODY):
                if k % QUAD == 0:
                    pe.wait_ge(rel_ready, t * NQ + (k // QUAD + 1))
                pe.wait_ge(built, t * BODY + (k + 1))
                pe.wait_ge(added, t * BODY + (k + 1))
                pe.matmul(pc[k], oh[:, k % HOTS, :], rel[:, k, :], start=True, stop=True).then_inc(counted, 1)
        pe.sem_inc(spread, 2)
        with pe.Fori(0, TURNS) as t:
            for h in range(2):
                pe.wait_ge(turned, t * 2 + (h + 1))
                pe.wait_ge(rows_set, t * 2 + (h + 1))
                pe.wait_ge(chosen, t * 2 + (h + 1))
                for k in range(HALF):
                    s = h * HALF + k
                    mm = pe.matmul(px[h][:, k * REL:(k + 1) * REL], oht[:, s, :], inv_of[:, s, :], start=True, stop=True)
                mm.then_inc(spread, 1)
        pe.wait_ge(chosen, HALVES + 2)

    def act(act):
        rows["act"](act)
        act.wait_ge(inv, 2)
        with act.Fori(0, TURNS) as t:
            for h in range(2):
                act.wait_ge(spread, t * 2 + (h + 1))
                for q in range(h * NQ // 2, (h + 1) * NQ // 2):
                    tiles = load_tiles(act, m.words_dst, t * BODY + q * QUAD, QUAD)
                    for k in range(QUAD):
                        ins = act.copy(inv_of[:, q * QUAD + k:q * QUAD + k + 1, :], cnt[:, bass.ds(tiles[k], 1), :])
                ins.then_inc(rows_set, 1)

    def dve(dve):
        dve.wait_ge(loaded, 16)
        dve.memset(cnt[:, :, :], 0.0).then_inc(begun, 1)
        dve.wait_ge(begun, 1)
        dve.sem_inc(added, RING)
        dve.sem_inc(chosen, 2)

        def relations(t, k):
            at = k % BODY
            dve.tensor_tensor(rel[:, at:at + QUAD, :], m.iota_b[:, 0:REL].unsqueeze(1).to_broadcast([P, QUAD, REL]),
                              m.rec[:, bass.ds(t * BODY + k, QUAD), 3:4].to_broadcast([P, QUAD, REL]),
                              ALU.is_equal).then_inc(rel_ready, 1)

        def build(t, k):
            dve.wait_ge(counted, t * BODY + (k + 1))
            dve.tensor_scalar(oh[:, k % HOTS, :], m.iota_b[:, :], m.rec[:, bass.ds(t * BODY + k, 1), 1:2], None,
                              ALU.is_equal).then_inc(built, 1)

        relations(0, 0)
        for k in range(LEAD):
            build(0, k)
        with dve.Fori(0, TURNS) as t:
            for k in range(BODY):
                build(t, k + LEAD)
                if k % QUAD == 0:
                    relations(t, k + LEAD)
                    tiles = load_tiles(dve, m.words_dst, t * BODY + k, QUAD)
                at = cnt[:, bass.ds(tiles[k % QUAD], 1), :]
                dve.wait_ge(counted, t * BODY + (k + 1 + HOTS))
                dve.wait_ge(added, t * BODY + (k + RING))
                dve.tensor_tensor(at, at, pc[k].rearrange("p (a r) -> p a r", a=1), ALU.add).then_inc(added, 1)
        dve.wait_ge(added, SLOTS + RING)
        dve.tensor_scalar(cnt[:, :, :], cnt[:, :, :], 1.0, None, ALU.max).then_inc(inv, 1)
        dve.wait_ge(inv, 1)
        dve.reciprocal(cnt[:, :, :], cnt[:, :, :]).then_inc(inv, 1)

        def turn(t, h):
            dve.wait_ge(got[h], t * 16 + 16)
            dve.tensor_scalar(oht[:, h * HALF:(h + 1) * HALF, :].rearrange("p s e -> p (s e)"),
                              kb[:, h * HALF * P:(h + 1) * HALF * P], m.iota_p[:, 0:1], None, ALU.is_equal)\
               .then_inc(turned, 1)

        def relations_of_half(t, h):
            dve.tensor_tensor(rel_f[:, h * HALF:(h + 1) * HALF, :],
                              m.iota_n[:, 0:REL].unsqueeze(1).to_broadcast([P, HALF, REL]),
                              m.rec[:, bass.ds(t * BODY + h * HALF, HALF), 3:4].to_broadcast([P, HALF, REL]),
                              ALU.is_equal).then_inc(rel_set, 1)

        turn(0, 0)
        relations_of_half(0, 0)
        with dve.Fori(0, TURNS) as t:
            for h in range(2):
                a = slice(h * HALF, (h + 1) * HALF)
                u = t * 2 + h
                turn(t + h, 1 - h)
                dve.wait_ge(spread, u + 3)
                dve.wait_ge(rel_set, u + 1)
                dve.tensor_tensor(prod[:, a, :], rel_f[:, a, :], px[h].rearrange("p (s r) -> p s r", r=REL), ALU.mult)\
                   .then_inc(chosen, 1)
                relations_of_half(t + h, 1 - h)
                dve.wait_ge(chosen, u + 3)
                dve.tensor_reduce(per_edge[:, a], prod[:, a, :], AX.X, ALU.add).then_inc(summed, 1)
                dve.wait_ge(summed, u + 1)
                dve.tensor_scalar(m.rec[:, bass.ds(t * BODY + h * HALF, HALF), 3], per_edge[:, a], 1.0, None, ALU.mult)\
                   .then_inc(wrote, 1)
        dve.wait_ge(turned, HALVES + 1)

    return {"sp": sp, "pe": pe, "act": act, "dve": dve}


def load_records(sp, m, table, loaded):
    sp.dma_start(m.rec[:, :, :].rearrange("p s w -> p (s w)"), table.rearrange("(p s) w -> p (s w)", p=P))\
      .then_inc(loaded, 16)


class Gathers:

    def __init__(self, n, m, table, width, index, name):
        self.m, self.table, self.index = m, table, index
        self.ring = n.sb(name + "ring", [P, BODY, width])
        self.rows = n.sb(name + "rows", [P, BODY], U32)
        self.rows_ready = n.sem(name + "rows_ready")
        self.issuing = n.sem(name + "issuing")
        self.landed = [n.sem(name + f"landed{q}") for q in range(NQ)]
        self.slots_used = n.sem(name + "slots_used")

    def copy_rows(self, act, turn, q):
        at = self.m.rec[:, bass.ds(turn * BODY + q * QUAD, QUAD), self.index].bitcast(U32)
        act.copy(self.rows[:, q * QUAD:(q + 1) * QUAD], at).then_inc(self.rows_ready, 1)

    def copy_next_rows(self, act, t, q):
        act.wait_ge(self.slots_used, t * BODY + (q + 1) * QUAD + HOTS)
        self.copy_rows(act, t + 1, q)

    def issue(self, pool):
        with pool.Fori(0, TURNS) as t:
            for q in range(NQ):
                pool.wait_ge(self.rows_ready, t * NQ + (q + 1))
                pool.sem_inc(self.issuing, 1)
                for k in range(q * QUAD, (q + 1) * QUAD):
                    pool.indirect_dma_start(self.ring[:, k, :], None, self.table,
                                            bass.IndirectOffsetOnAxis(self.rows[:, k:k + 1], 0))\
                        .then_inc(self.landed[q], 16)

    def wait_quad(self, eng, t, q):
        eng.wait_ge(self.landed[q], t * (16 * QUAD) + 16 * QUAD)


def message_pass(nc, m, name, records, words, index, table, heads, width, acc_at, weight=None):
    W = heads * width
    BK = -(-W // 512)
    CB = W // BK
    HB = heads // BK
    RP = 4 // BK
    HALF = BODY // 2
    H2 = 2 * heads
    attend = weight is None
    several = heads > 1
    with Net(nc) as n:
        g = Gathers(n, m, table, W, index, name)
        hot = n.sb(name + "hot", [P, HOTS, heads, P])
        loaded = n.sem(name + "loaded")
        hot_ready = n.sem(name + "hot_ready")
        added = n.sem(name + "added")
        if several:
            plain = n.sb(name + "plain", [P, HOTS, P])
            plain_ready = n.sem(name + "plain_ready")
        if attend:
            kb = n.sb(name + "kb", [P, BODY * P], BF16)
            oht = n.sb(name + "oht", [P, BODY, P])
            z = n.sb(name + "z", [P, 2, HALF, heads])
            wt = n.sb(name + "wt", [P, BODY, heads])
            keys = n.sem(name + "keys")
            turned = n.sem(name + "turned")
            spread = n.sem(name + "spread")
            zs = n.sem(name + "zs")
            weighed = n.sem(name + "weighed")
            px = [m.ps[:, 4 + h, 0:HALF * H2].rearrange("p (s c) -> p s c", c=H2) for h in range(2)]
        block = n.block()

        def product(k):
            return m.ps[:, k % RP * BK:(k % RP + 1) * BK, 0:CB]

        def need_weights(eng, t, k):
            if attend and k % HALF == 0:
                eng.wait_ge(weighed, t * 2 + (k // HALF + 1))

        @block.sync
        def _(sp):
            load_records(sp, m, records, loaded)
            if attend:
                def fetch(t):
                    sp.dma_start(kb[:, :], m.key_rows[bass.ds(t * BODY, BODY), :].rearrange("s e -> (s e)")
                                 .partition_broadcast(P)).then_inc(keys, 16)
                fetch(0)
                with sp.Fori(0, TURNS) as t:
                    sp.wait_ge(turned, t * 2 + 2)
                    fetch(t + 1)

        @block.gpsimd
        def _(pool):
            g.issue(pool)

        @block.scalar
        def _(act):
            def weigh_half(t, h):
                act.wait_ge(zs, t * 8 + (4 * h + 4))
                act.activation(wt[:, h * HALF:(h + 1) * HALF, :], z[:, h, :, :], ACT.Exp)\
                   .then_inc(weighed, 1)

            def weigh_hot(t, k):
                need_weights(act, t + k // BODY, k % BODY)
                act.wait_ge(plain_ready, t * BODY + (k + 1))
                for h in range(heads):
                    ins = act.activation(hot[:, k % HOTS, h, :], plain[:, k % HOTS, :], ACT.Copy,
                                         scale=wt[:, k % BODY, h:h + 1])
                ins.then_inc(hot_ready, 1)

            act.wait_ge(loaded, 16)
            for q in range(NQ):
                g.copy_rows(act, 0, q)
            if attend:
                weigh_half(0, 0)
            if several:
                for k in range(LEAD):
                    weigh_hot(0, k)
            with act.Fori(0, TURNS) as t:
                for k in range(BODY):
                    if several:
                        weigh_hot(t, k + LEAD)
                    if k % QUAD == QUAD - 1:
                        g.copy_next_rows(act, t, k // QUAD)
                    if attend and k == 1:
                        act.wait_ge(hot_ready, t * BODY + LEAD)
                        weigh_half(t, 1)
                    if attend and k == HALF + 2:
                        act.wait_ge(hot_ready, t * BODY + HALF)
                        weigh_half(t + 1, 0)

        @block.tensor
        def _(pe):
            def spread_slot(t, s, tiles):
                h = s // HALF
                if s % QUAD == 0:
                    tiles[:] = load_tiles(pe, words, t * BODY + s, QUAD)
                if s % HALF == 0:
                    pe.wait_ge(turned, t * 2 + (h + 1))
                mm = pe.matmul(px[h][:, s % HALF, :], oht[:, s, :], m.tab[:, bass.ds(tiles[s % QUAD], 1), 0:H2],
                               start=True, stop=True)
                if s % HALF == HALF - 1:
                    mm.then_inc(spread, 1)

            pe.sem_inc(g.slots_used, HOTS)
            tiles = []
            if attend:
                for s in range(BODY):
                    spread_slot(0, s, tiles)
            with pe.Fori(0, TURNS) as t:
                for k in range(BODY):
                    if k % QUAD == 0:
                        g.wait_quad(pe, t, k // QUAD)
                    pe.wait_ge(added, t * BODY + (k + 1))
                    pe.wait_ge(hot_ready, t * BODY + (k + 1))
                    out = product(k)
                    for h in range(heads):
                        c = h % HB * width
                        mm = pe.matmul(out[:, h // HB, c:c + width], hot[:, k % HOTS, h, :],
                                       g.ring[:, k, h * width:(h + 1) * width], start=True, stop=True)
                    mm.then_inc(g.slots_used, 1)
                    ahead = [s for s in (k - 1, k) if attend and (0 <= s < HALF and s == k - 1 or s >= HALF and s == k)]
                    for s in ahead:
                        if s % HALF == 0:
                            pe.wait_ge(zs, t * 8 + (4 * (s // HALF) + 4))
                        spread_slot(t + 1, s, tiles)

        @block.vector
        def _(dve):
            def turn_keys(t, h):
                if h == 0:
                    dve.wait_ge(keys, t * 16 + 16)
                dve.tensor_scalar(oht[:, h * HALF:(h + 1) * HALF, :].rearrange("p s e -> p (s e)"),
                                  kb[:, h * HALF * P:(h + 1) * HALF * P], m.iota_p[:, 0:1], None, ALU.is_equal)\
                   .then_inc(turned, 1)

            def score(t, h, i):
                zh = z[:, h, :, :]
                if i == 0:
                    dve.wait_ge(spread, t * 2 + (h + 1))
                    dve.tensor_tensor(zh, px[h][:, :, 0:heads], m.edge_t[:, bass.ds(t * BODY + h * HALF, HALF), :],
                                      ALU.add).then_inc(zs, 1)
                    return
                dve.wait_ge(zs, t * 8 + (4 * h + i))
                if i == 1:
                    dve.scalar_tensor_tensor(out=zh, in0=zh, scalar=SLOPE, in1=zh, op0=ALU.mult, op1=ALU.max)\
                       .then_inc(zs, 1)
                elif i == 2:
                    dve.tensor_tensor(zh, zh, px[h][:, :, heads:H2], ALU.subtract).then_inc(zs, 1)
                else:
                    dve.tensor_scalar(zh, zh, 0.0, None, ALU.min).then_inc(zs, 1)

            def build(t, k):
                key = m.rec[:, bass.ds(t * BODY + k, 1), 1:2]
                if several:
                    dve.wait_ge(g.slots_used, t * BODY + (k + 1))
                    dve.tensor_scalar(plain[:, k % HOTS, :], m.iota_n[:, :], key, None, ALU.is_equal)\
                       .then_inc(plain_ready, 1)
                    return
                w = wt[:, k % BODY, 0:1] if attend else m.rec[:, bass.ds(t * BODY + k, 1), weight:weight + 1]
                need_weights(dve, t + k // BODY, k % BODY)
                dve.wait_ge(g.slots_used, t * BODY + (k + 1))
                dve.tensor_scalar(hot[:, k % HOTS, 0, :], m.iota_n[:, :], key, w, ALU.is_equal, ALU.mult)\
                   .then_inc(hot_ready, 1)

            def add(t, k, tiles):
                at = m.acc[:, bass.ds(tiles[k % QUAD], 1), acc_at:acc_at + W].rearrange("p a (b c) -> p (a b) c", b=BK)
                dve.wait_ge(g.slots_used, t * BODY + (k + 1 + HOTS))
                dve.wait_ge(added, t * BODY + (k + RP))
                dve.tensor_tensor(at, at, product(k), ALU.add).then_inc(added, 1)

            dve.sem_inc(added, RP)
            dve.wait_ge(loaded, 16)
            if attend:
                turn_keys(0, 0)
                turn_keys(0, 1)
                for i in range(4):
                    score(0, 0, i)
            for k in range(LEAD):
                build(0, k)
            with dve.Fori(0, TURNS) as t:
                for k in range(BODY):
                    half = {0: (t, 1, 0), 1: (t, 1, 2), HALF + 1: (t + 1, 0, 0), HALF + 2: (t + 1, 0, 2)}.get(k)
                    if attend and k in (0, QUAD):
                        turn_keys(t + 1, k // QUAD)
                    build(t, k + LEAD)
                    if k % QUAD == 0:
                        tiles = load_tiles(dve, words, t * BODY + k, QUAD)
                    if attend and half:
                        if half[2] == 0:
                            dve.wait_ge(weighed, t * 2 + 1)
                        score(*half)
                    add(t, k, tiles)
                    if attend and half:
                        score(half[0], half[1], half[2] + 1)
            dve.wait_ge(added, SLOTS + RP)


def max_pass(nc, m, name, records, words, index, table, heads, turn_rows, cleared, fetch_x):
    G = 4 // heads
    GROUPS = BODY // G
    with Net(nc) as n:
        g = Gathers(n, m, table, heads, index, name)
        loaded = n.sem(name + "loaded")
        off = n.sb(name + "off", [P, HOTS, P], BF16)
        slot_max = n.sb(name + "slot_max", [P, RING, G, heads])
        top = n.sb(name + "top", [P, NT, heads])
        off_ready = n.sem(name + "off_ready")
        reduced = n.sem(name + "reduced")
        topped = n.sem(name + "topped")
        kept = n.sem(name + "kept")
        blank, made, x_in = n.sem(name + "blank"), n.sem(name + "made"), n.sem(name + "x_in")
        rows = key_rows(n, m, loaded, name + "k") if turn_rows else None
        block = n.block()
        HC = heads * P

        def bank(k):
            return m.ps[:, 4 + k // G % RING, k % G * HC:(k % G + 1) * HC]

        @block.sync
        def _(sp):
            load_records(sp, m, records, loaded)
            if rows:
                rows["sp"](sp)
            if fetch_x:
                sp.dma_start(m.acc[:, :, X_AT:X_AT + D], node_rows(m.x_kept)).then_inc(x_in, 16)
                sp.wait_ge(x_in, 16)

        @block.gpsimd
        def _(pool):
            pool.memset(m.edge_t[:, SLOTS:SL, :], 0.0).then_inc(blank, 1)
            g.issue(pool)

        @block.scalar
        def _(act):
            if rows:
                rows["act"](act)
            act.wait_ge(loaded, 16)
            for q in range(NQ):
                g.copy_rows(act, 0, q)
            with act.Fori(0, TURNS) as t:
                for q in range(NQ):
                    g.wait_quad(act, t, q)
                    act.copy(m.edge_t[:, bass.ds(t * BODY + q * QUAD, QUAD), :], g.ring[:, q * QUAD:(q + 1) * QUAD, :])\
                       .then_inc(kept, 1)
                    act.wait_ge(kept, t * NQ + (q + 1))
                    g.copy_next_rows(act, t, q)

        @block.tensor
        def _(pe):
            if rows:
                rows["pe"](pe)
            pe.sem_inc(g.slots_used, HOTS)
            pe.wait_ge(blank, 2)
            with pe.Fori(0, TURNS) as t:
                for k in range(BODY):
                    if k % QUAD == 0:
                        g.wait_quad(pe, t, k // QUAD)
                    if k % G == 0:
                        pe.wait_ge(reduced, t * GROUPS + (k // G + 1))
                    pe.wait_ge(off_ready, t * BODY + (k + 1))
                    pe.matmul(bank(k), off[:, k % HOTS, :], m.ident_b[:, :].unsqueeze(1).to_broadcast([P, heads, P]),
                              start=True, stop=False, skip_group_check=True)
                    for h in range(heads):
                        mm = pe.matmul(bank(k)[:, h * P:(h + 1) * P], g.ring[:, k, h:h + 1].to_broadcast([P, P]),
                                       m.ident[:, :], start=False, stop=(h == heads - 1), skip_group_check=True)
                    mm.then_inc(g.slots_used, 1)

        @block.vector
        def _(dve):
            dve.memset(top[:, :, :], NEG).then_inc(blank, 1)
            dve.memset(m.acc[:, :, 0:cleared], 0.0)
            dve.sem_inc(reduced, RING)
            dve.sem_inc(topped, 1)
            dve.wait_ge(loaded, 16)
            dve.wait_ge(blank, 2)

            def build(t, k):
                dve.wait_ge(g.slots_used, t * BODY + (k + 1))
                dve.tensor_scalar(off[:, k % HOTS, :], m.iota_b[:, :], m.rec[:, bass.ds(t * BODY + k, 1), 1:2], NEG,
                                  ALU.not_equal, ALU.mult).then_inc(off_ready, 1)

            def reduce_group(t, i):
                dve.wait_ge(g.slots_used, t * BODY + ((i + 1) * G + HOTS))
                dve.tensor_reduce(slot_max[:, i % RING, :, :],
                                  m.ps[:, 4 + i % RING, :].rearrange("p (g h e) -> p g h e", g=G, h=heads),
                                  AX.X, ALU.max).then_inc(reduced, 1)

            def take(t, k, tiles):
                at = top[:, bass.ds(tiles[k % QUAD], 1), :]
                dve.wait_ge(reduced, t * GROUPS + (k // G + 1 + RING))
                dve.wait_ge(topped, t * BODY + (k + 1))
                dve.tensor_tensor(at, at, slot_max[:, k // G % RING, k % G:k % G + 1, :], ALU.max).then_inc(topped, 1)

            for k in range(LEAD):
                build(0, k)
            with dve.Fori(0, TURNS) as t:
                for k in range(BODY):
                    if k % G == 0:
                        reduce_group(t, k // G)
                    build(t, k + LEAD)
                    if k % QUAD == 0:
                        tiles = load_tiles(dve, words, t * BODY + k, QUAD)
                    take(t, k, tiles)
            dve.wait_ge(topped, SLOTS + 1)
            s, mx = m.tab[:, :, 0:heads], m.tab[:, :, heads:2 * heads]
            dve.tensor_tensor(mx, s, top[:, :, :], ALU.add).then_inc(made, 1)
            dve.wait_ge(made, 1)
            dve.scalar_tensor_tensor(out=mx, in0=mx, scalar=SLOPE, in1=mx, op0=ALU.mult, op1=ALU.max).then_inc(made, 1)


FULL = N // P
REST = N - FULL * P
PAIRS = NT // 2


def node_rows(a):
    return a.rearrange("(j p) d -> p j d", p=P)


def flat(ap):
    return ap.rearrange("p a c -> p (a c)")


def norm_part(n, m, name, ready, count):
    st = n.sb(name + "st", [P, NT, 6])
    mean = n.sb(name + "mean", [P, NT])
    rstd = n.sb(name + "rstd", [P, NT])
    half = n.sb(name + "half", [P, NT])
    var = n.sb(name + "var", [P, NT])
    steps, root = n.sem(name + "steps"), n.sem(name + "root")

    def dve(dve):
        dve.wait_ge(ready, count)
        with dve.Fori(0, NT) as j:
            dve.bn_stats(flat(st[:, bass.ds(j, 1), :]), flat(m.acc[:, bass.ds(j, 1), X_AT:X_AT + D])).then_inc(steps, 1)
        k = NT
        dve.wait_ge(steps, k)
        dve.tensor_tensor(mean[:, :], st[:, :, 1], st[:, :, 4], ALU.add).then_inc(steps, 1)
        dve.tensor_tensor(half[:, :], st[:, :, 1], st[:, :, 4], ALU.subtract).then_inc(steps, 1)
        dve.tensor_tensor(var[:, :], st[:, :, 2], st[:, :, 5], ALU.add).then_inc(steps, 1)
        dve.wait_ge(steps, k + 3)
        dve.tensor_scalar(mean[:, :], mean[:, :], 0.5, None, ALU.mult).then_inc(steps, 1)
        dve.scalar_tensor_tensor(out=half[:, :], in0=half[:, :], scalar=0.25, in1=half[:, :], op0=ALU.mult, op1=ALU.mult)\
           .then_inc(steps, 1)
        dve.tensor_scalar(var[:, :], var[:, :], 1.0 / D, EPS, ALU.mult, ALU.add).then_inc(steps, 1)
        dve.wait_ge(steps, k + 6)
        dve.tensor_tensor(var[:, :], var[:, :], half[:, :], ALU.add).then_inc(steps, 1)
        dve.wait_ge(root, 1)
        dve.reciprocal(rstd[:, :], var[:, :]).then_inc(steps, 1)
        dve.wait_ge(steps, k + 8)

    def act(act):
        act.wait_ge(steps, NT + 7)
        act.activation(var[:, :], var[:, :], ACT.Sqrt).then_inc(root, 1)

    return {"dve": dve, "act": act}, mean, rstd


def relation_weights(n, m, name, comps, bases, root, bias, wr, scratch):
    cb = n.sb(name + "cb", [P, REL * BASES])
    bb = n.sb(name + "bb", [P, D])
    loaded, made = n.sem(name + "loaded"), n.sem(name + "made")
    bs = scratch[:, 0:2 * BASES * D].rearrange("p (k b o) -> p k b o", k=2, b=BASES)

    def sp(sp):
        for b in range(BASES):
            sp.dma_start(bs[:, :, b, :], bases[b, :, :].rearrange("(k p) o -> p k o", p=P)).then_inc(loaded, 16)
        sp.dma_start(wr[:, :, REL * D:(REL + 1) * D], root.rearrange("(k p) o -> p k o", p=P)).then_inc(loaded, 16)
        sp.dma_start(cb[:, :], comps.rearrange("r b -> (r b)").partition_broadcast(P)).then_inc(loaded, 16)
        sp.dma_start(bb[:, :], bias.partition_broadcast(P)).then_inc(loaded, 16)

    def dve(dve):
        dve.wait_ge(loaded, 16 * (BASES + 3))
        for b in range(BASES):
            if b:
                dve.wait_ge(made, REL * b)
            for r in range(REL):
                w = wr[:, :, r * D:(r + 1) * D]
                c = cb[:, r * BASES + b:r * BASES + b + 1]
                if b == 0:
                    dve.tensor_scalar(w, bs[:, :, b, :], c, None, ALU.mult).then_inc(made, 1)
                else:
                    dve.scalar_tensor_tensor(out=w, in0=bs[:, :, b, :], scalar=c, in1=w, op0=ALU.mult, op1=ALU.add)\
                       .then_inc(made, 1)
        dve.wait_ge(made, REL * BASES)

    return {"sp": sp, "dve": dve}, made, REL * BASES, bb


def turned_weights(n, m, name, weights, w):
    rows, cols = weights.shape[0] // P, weights.shape[1] // P
    raw = n.sb(name + "raw", [P, rows, cols * P])
    loaded, turned, made = n.sem(name + "loaded"), n.sem(name + "turned"), n.sem(name + "made")
    pairs = [(a, k) for a in range(rows) for k in range(cols)]
    per = len(pairs) // 2

    def place(i):
        return m.ps[:, i // per, i % per * P:(i % per + 1) * P]

    def sp(sp):
        sp.dma_start(raw[:, :, :], weights.rearrange("(a p) c -> p a c", p=P)).then_inc(loaded, 16)

    def pe(pe):
        pe.wait_ge(loaded, 16)
        for i, (a, k) in enumerate(pairs):
            pe.transpose(place(i), raw[:, a, k * P:(k + 1) * P], m.ident[:, :]).then_inc(turned, 1)
        pe.wait_ge(made, len(pairs))

    def act(act):
        for i, (a, k) in enumerate(pairs):
            act.wait_ge(turned, (i // per + 1) * per)
            act.activation(w[:, k, a * P:(a + 1) * P], place(i), ACT.Copy).then_inc(made, 1)

    return {"sp": sp, "pe": pe, "act": act}, made, len(pairs)


def transform(n, m, name, source, w, w_ready, w_count, kind, norm=None, heads=0, table=None, t_table=None,
              bias=None, vectors=None, vectors_ready=None, vectors_count=0, elu=None):
    KT, cols = w.shape[1], w.shape[2]
    banks = -(-cols // 512)
    OW = {"relation": REL * D, "support": D, "attention": cols + heads}[kind]
    xn = n.sb(name + "xn", [P, 2, KT * P])
    ht = n.sb(name + "ht", [P, 2, KT * P])
    ob = n.sb(name + "ob", [P, 2, OW])
    given = n.sem(name + "given")
    turned = n.sem(name + "turned")
    cut = n.sem(name + "cut")
    done = n.sem(name + "done")
    taken_a = n.sem(name + "taken_a")
    taken_d = n.sem(name + "taken_d")
    ob_free = n.sem(name + "ob_free")
    stored = [n.sem(name + f"stored{r}") for r in range(2)]
    owner = {"relation": "aaadd", "support": "d", "attention": "d" if bias is not None else "a"}[kind]
    share = {e: [b for b in range(banks) if owner[b] == e] for e in "ad"}
    na, nd = len(share["a"]), len(share["d"])
    product = [m.ps[:, b, 0:min(512, cols - b * 512)] for b in range(banks)]
    ps_t = [m.ps[:, 6 + r, 0:KT * P] for r in range(2)]
    if kind == "attention":
        dh = cols // heads
        dots = n.sb(name + "dots", [P, 2, 2 * heads])
        junk = n.sb(name + "junk", [P, 2 * heads, dh])
        dotted = n.sem(name + "dotted")
        ones_set = n.sem(name + "ones_set")
        ob_h = [ob[:, r, :].rearrange("p (h c) -> p h c", h=heads) for r in range(2)]
        per_tile = 2 * heads

    def sp(sp):
        sp.sem_inc(ob_free, 2)
        with sp.Fori(0, PAIRS) as i:
            for r in range(2):
                j = i * 2 + r
                if na:
                    sp.wait_ge(taken_a, j * na + 2 * na)
                if kind == "relation":
                    sp.wait_ge(taken_d, j * nd + 2 * nd)
                    z = m.z.rearrange("(q j p) d -> p q j d", q=REL, p=P)[:, :, bass.ds(j, 1), :]
                    sp.dma_start(z.rearrange("p q j d -> p q (j d)"), ob[:, r, :].rearrange("p (q d) -> p q d", q=REL))\
                      .then_inc(stored[r], 16)
                else:
                    if nd:
                        sp.wait_ge(taken_d, j * nd + 2 * nd)
                    sp.dma_start(flat(node_rows(table)[:, bass.ds(j, 1), :]), ob[:, r, :]).then_inc(stored[r], 16)
                if kind == "attention":
                    sp.wait_ge(dotted, j * (per_tile + 1) + (per_tile + 1))
                    sp.dma_start(flat(node_rows(t_table)[:, bass.ds(j, 1), :]), dots[:, r, heads:]).then_inc(stored[r], 16)
                    sp.wait_ge(stored[r], i * 32 + 32)
                else:
                    sp.wait_ge(stored[r], i * 16 + 16)
                sp.sem_inc(ob_free, 1)

    def pairs(eng, work):
        with eng.Fori(0, PAIRS - 1) as i:
            for r in range(2):
                work(i * 2 + r, r, True)
        for r in range(2):
            work(NT - 2 + r, r, r == 0)

    def pe(pe):
        def turn(j, r):
            pe.wait_ge(given, j + 1)
            for k in range(KT):
                mm = pe.transpose(ps_t[r][:, k * P:(k + 1) * P], xn[:, r, k * P:(k + 1) * P], m.ident[:, :])
            mm.then_inc(turned, 1)

        def work(j, r, more):
            if more:
                turn(j + 1, 1 - r)
            pe.wait_ge(cut, j + 1)
            for b in range(banks):
                e, sem, of = owner[b], (taken_a if owner[b] == "a" else taken_d), (na if owner[b] == "a" else nd)
                pe.wait_ge(sem, j * of + (share[e].index(b) + 1))
                width = product[b].shape[1]
                for k in range(KT):
                    mm = pe.matmul(product[b], ht[:, r, k * P:(k + 1) * P], w[:, k, b * 512:b * 512 + width],
                                   start=(k == 0), stop=(k == KT - 1))
                mm.then_inc(done, 1)

        pe.wait_ge(w_ready, w_count)
        turn(0, 0)
        pairs(pe, work)

    def act(act):
        def copy(j, r):
            if elu:
                elu["act"](act, r, j)
            act.wait_ge(turned, j + 1)
            if elu:
                act.activation(ht[:, r, :], ps_t[r], ACT.Copy, bias=-1.0).then_inc(cut, 1)
            else:
                act.activation(ht[:, r, :], ps_t[r], ACT.Relu).then_inc(cut, 1)

        def work(j, r, more):
            if more:
                copy(j + 1, 1 - r)
            for b in share["a"]:
                act.wait_ge(done, j * banks + (b + 1))
                if b == share["a"][0]:
                    act.wait_ge(ob_free, j + 1)
                if kind == "attention":
                    act.activation(ob_h[r][:, :, 0:dh], product[b].rearrange("p (h c) -> p h c", h=heads), ACT.Copy)\
                       .then_inc(taken_a, 1)
                else:
                    width = product[b].shape[1]
                    act.activation(ob[:, r, b * 512:b * 512 + width], product[b], ACT.Copy).then_inc(taken_a, 1)

        if na:
            act.sem_inc(taken_a, na)
        copy(0, 0)
        pairs(act, work)

    def dve(dve):
        def give(j, r):
            if source == "norm":
                dve.tensor_scalar(xn[:, r, :], flat(m.acc[:, bass.ds(j, 1), X_AT:X_AT + D]),
                                  norm[0][:, bass.ds(j, 1)], norm[1][:, bass.ds(j, 1)], ALU.subtract, ALU.mult)\
                   .then_inc(given, 1)
            elif source == "acc":
                dve.tensor_scalar(xn[:, r, :], flat(m.acc[:, bass.ds(j, 1), 0:D]), 1.0, None, ALU.mult)\
                   .then_inc(given, 1)
            else:
                elu["dve"](dve, r, j, xn, given)

        def work(j, r, more):
            if more:
                give(j + 1, 1 - r)
            dve.wait_ge(done, j * banks + (4 if kind == "relation" else banks))
            dve.wait_ge(ob_free, j + 1)
            if kind == "relation":
                dve.tensor_copy(ob[:, r, 3 * 512:4 * 512], product[3]).then_inc(taken_d, 1)
                dve.wait_ge(done, j * banks + 5)
                dve.tensor_tensor(m.acc[:, bass.ds(j, 1), 0:D], product[4].rearrange("p (a c) -> p a c", a=1),
                                  bias[:, :].rearrange("p (a c) -> p a c", a=1), ALU.add).then_inc(taken_d, 1)
                return
            if kind == "support":
                dve.tensor_copy(ob[:, r, :], product[0]).then_inc(taken_d, 1)
                return
            if nd:
                dve.tensor_tensor(ob_h[r][:, :, 0:dh], product[0].rearrange("p (h c) -> p h c", h=heads),
                                  bias[:, :].rearrange("p (h c) -> p h c", h=heads), ALU.add).then_inc(taken_d, 1)
                dve.wait_ge(taken_d, j + 2)
            else:
                dve.wait_ge(taken_a, j + 2)
            for v in range(2 * heads):
                dve.tensor_tensor_reduce(junk[:, v, :], ob_h[r][:, v % heads, 0:dh], vectors[:, v, :], 1.0, 0.0,
                                         ALU.mult, ALU.add, dots[:, r, v:v + 1]).then_inc(dotted, 1)
            dve.wait_ge(dotted, j * (per_tile + 1) + per_tile)
            dve.tensor_scalar(m.tab[:, bass.ds(j, 1), 0:heads],
                              dots[:, r, 0:heads].rearrange("p (a c) -> p a c", a=1), 1.0, None, ALU.mult)\
               .then_inc(dotted, 1)

        if nd:
            dve.sem_inc(taken_d, nd)
        if kind == "attention":
            for r in range(2):
                dve.memset(ob_h[r][:, :, dh:dh + 1], 1.0).then_inc(ones_set, 1)
            dve.wait_ge(ones_set, 2)
            dve.wait_ge(vectors_ready, vectors_count)
        give(0, 0)
        pairs(dve, work)

    return {"sp": sp, "pe": pe, "act": act, "dve": dve}


def attention_vectors(n, name, own, other, heads, dh, bias=None):
    v = n.sb(name + "v", [P, 2 * heads, dh])
    b = n.sb(name + "b", [P, heads * dh]) if bias is not None else None
    loaded = n.sem(name + "loaded")
    count = 0
    pieces = []
    for side, a in enumerate((own, other)):
        for h in range(heads):
            pieces.append((v[:, side * heads + h, :], a[h]))
    if b is not None:
        pieces.append((b[:, :], bias))

    def sp(sp):
        for to, a in pieces:
            sp.dma_start(to, a.partition_broadcast(P)).then_inc(loaded, 16)

    return {"sp": sp}, v, b, loaded, 16 * len(pieces)


def weights_part(n, name, weights, w):
    loaded = n.sem(name + "loaded")

    def sp(sp):
        sp.dma_start(w[:, :, :], weights.rearrange("(k p) o -> p k o", p=P)).then_inc(loaded, 16)

    return {"sp": sp}, loaded, 16



def rgcn_first(n, m, a):
    wr = n.sb("r0_wr", [P, 2, (REL + 1) * D])
    cleared, x_in = n.sem("r0_cleared"), n.sem("r0_x_in")
    norm, mean, rstd = norm_part(n, m, "r0_n_", x_in, 32)
    scratch = n.sb("r0_bases", [P, 2 * BASES * D])
    made, ready, count, bb = relation_weights(n, m, "r0_w_", a.comps[0, :, :], a.bases[0, :, :, :], a.roots[0, :, :],
                                              a.biases[0, :], wr, scratch[:, :])
    tr = transform(n, m, "r0_", "norm", wr, ready, count, "relation", norm=(mean, rstd), bias=bb)

    def sp(sp):
        sp.wait_ge(cleared, 1)
        to = m.acc[:, :, X_AT:X_AT + D]
        sp.dma_start(to[:, 0:FULL, :], node_rows(a.x[0:FULL * P, :])).then_inc(x_in, 16)
        sp.dma_start(to[0:REST, FULL, :], a.x[FULL * P:N, :]).then_inc(x_in, 16)

    def dve(dve):
        dve.memset(m.acc[:, FULL:NT, X_AT:X_AT + D], 0.0).then_inc(cleared, 1)

    return [{"sp": sp, "dve": dve}, {"sp": made["sp"]}], [{"dve": made["dve"]}, norm, tr]


def rgcn_second(nc, m, a):
    with Net(nc) as n:
        wr = n.sb("r1_wr", [P, 2, (REL + 1) * D])
        scratch = n.sb("r1_bases", [P, 2 * BASES * D])
        made, ready, count, bb = relation_weights(n, m, "r1_w_", a.comps[1, :, :], a.bases[1, :, :, :],
                                                  a.roots[1, :, :], a.biases[1, :], wr, scratch[:, :])
        tr = transform(n, m, "r1_", "acc", wr, ready, count, "relation", bias=bb)
        run_parts(n.block(), made, tr)


def gcn_support(nc, m, a):
    with Net(nc) as n:
        w = n.sb("g_w", [P, 2, D])
        ready = n.sem("g_ready")
        wp, wl, wc = weights_part(n, "g_w_", a.gcn_w, w)
        norm, mean, rstd = norm_part(n, m, "g_n_", ready, 1)
        tr = transform(n, m, "g_", "norm", w, wl, wc, "support", norm=(mean, rstd), table=m.support)

        def dve(dve):
            x = m.acc[:, :, X_AT:X_AT + D]
            dve.tensor_tensor(x, x, m.acc[:, :, 0:D], ALU.add).then_inc(ready, 1)

        run_parts(n.block(), {"dve": dve}, wp, norm, tr)


def gat_tables(nc, m, a):
    with Net(nc) as n:
        w = n.sb("a_w", [P, 2, D])
        ready = n.sem("a_ready")
        wp, wl, wc = weights_part(n, "a_w_", a.gat_w, w)
        heads, dh = 2, D // 2
        vp, v, b, vl, vc = attention_vectors(n, "a_v_", [a.gat_a[0:dh]] * heads, [a.gat_a[dh:2 * dh]] * heads,
                                             heads, dh, a.gat_b)
        norm, mean, rstd = norm_part(n, m, "a_n_", ready, 1)
        tr = transform(n, m, "a_", "norm", w, wl, wc, "attention", norm=(mean, rstd), heads=heads, table=m.gat_rows,
                       t_table=m.gat_t, bias=b, vectors=v, vectors_ready=vl, vectors_count=vc)
        run_parts(n.block(), {"dve": lambda dve: dve.sem_inc(ready, 1)}, wp, vp, norm, tr)


def inverse_sums(n, m, name, heads, width, least):
    inv = n.sb(name + "inv", [P, NT, heads])
    step = n.sem(name + "inv_step")
    sums = m.acc[:, :, 0:heads * width].rearrange("p j (h c) -> p j h c", h=heads)[:, :, :, width - 1]

    def dve(dve):
        dve.tensor_scalar(inv[:, :, :], sums, least, None, ALU.add).then_inc(step, 1)
        dve.wait_ge(step, 1)
        dve.reciprocal(inv[:, :, :], inv[:, :, :]).then_inc(step, 1)
        dve.wait_ge(step, 2)

    return {"dve": dve}, inv, sums


def gat_first_of_two(nc, m, a):
    with Net(nc) as n:
        heads, dh = 2, D // 2
        own = n.sb("b_own", [P, NT, heads * (dh + 1)])
        none = n.sb("b_none", [P, NT, heads])
        step, ready, own_in, kept = n.sem("b_step"), n.sem("b_ready"), n.sem("b_own_in"), n.sem("b_kept")
        inv = n.sb("b_inv", [P, NT, heads])
        sums = m.acc[:, :, 0:heads * (dh + 1)].rearrange("p j (h c) -> p j h c", h=heads)[:, :, :, dh]

        def sp(sp):
            sp.dma_start(own[:, :, :], node_rows(m.gat_rows)).then_inc(own_in, 16)

        def dve(dve):
            dve.tensor_scalar(none[:, :, :], sums, 0.0, None, ALU.is_equal).then_inc(step, 1)
            dve.wait_ge(step, 1)
            dve.tensor_tensor(inv[:, :, :], sums, none[:, :, :], ALU.add).then_inc(step, 1)
            dve.wait_ge(step, 2)
            dve.reciprocal(inv[:, :, :], inv[:, :, :]).then_inc(step, 1)
            dve.wait_ge(own_in, 16)
            dve.wait_ge(step, 3)
            k = 3
            for h in range(heads):
                x = m.acc[:, :, X_AT + h * dh:X_AT + (h + 1) * dh]
                got = m.acc[:, :, h * (dh + 1):h * (dh + 1) + dh]
                self_row = own[:, :, h * (dh + 1):h * (dh + 1) + dh]
                dve.tensor_tensor(got, got, inv[:, :, h:h + 1].to_broadcast([P, NT, dh]), ALU.mult).then_inc(step, 1)
                dve.tensor_tensor(self_row, self_row, none[:, :, h:h + 1].to_broadcast([P, NT, dh]), ALU.mult)\
                   .then_inc(step, 1)
                dve.wait_ge(step, k + 1)
                dve.tensor_tensor(x, x, got, ALU.add).then_inc(step, 1)
                dve.wait_ge(step, k + 3)
                dve.tensor_tensor(x, x, self_row, ALU.add).then_inc(step, 1)
                k += 4
            dve.wait_ge(step, k)
            dve.sem_inc(ready, 1)

        def keep(sp):
            sp.wait_ge(ready, 1)
            sp.dma_start(node_rows(m.x_kept), m.acc[:, :, X_AT:X_AT + D]).then_inc(kept, 16)
            sp.wait_ge(kept, 16)

        run_parts(n.block(), {"sp": sp, "dve": dve}, {"sp": keep})
    with Net(nc) as n:
        heads, dh = 4, P
        w = n.sb("c_w", [P, 2, heads * dh])
        ready = n.sem("c_ready")
        wp, wl, wc = turned_weights(n, m, "c_w_", a.w1, w)
        vp, v, b, vl, vc = attention_vectors(n, "c_v_", [a.a_dst1[0, h, :] for h in range(heads)],
                                             [a.a_src1[0, h, :] for h in range(heads)], heads, dh)
        norm, mean, rstd = norm_part(n, m, "c_n_", ready, 1)
        tr = transform(n, m, "c_", "norm", w, wl, wc, "attention", norm=(mean, rstd), heads=heads, table=m.rows1,
                       t_table=m.t1, vectors=v, vectors_ready=vl, vectors_count=vc)
        run_parts(n.block(), {"dve": lambda dve: dve.sem_inc(ready, 1)}, wp, vp, norm, tr)


def gat_second_of_two(nc, m, a):
    heads, dh = 4, P
    with Net(nc) as n:
        w = n.sb("d_w", [P, 4, D])
        wp, wl, wc = turned_weights(n, m, "d_w_", a.w2, w)
        vp, v, b, vl, vc = attention_vectors(n, "d_v_", [a.a_dst2[0, 0, :]], [a.a_src2[0, 0, :]], 1, D)
        ip, inv, sums = inverse_sums(n, m, "d_", heads, dh + 1, 1e-16)
        b1 = n.sb("d_b1", [P, heads * dh])
        y = n.sb("d_y", [P, 2, heads * dh])
        low = n.sb("d_low", [P, 2, heads * dh])
        b_in, steps, raised = n.sem("d_b_in"), n.sem("d_steps"), n.sem("d_raised")
        PER = heads + 1

        def elu_dve(dve, r, j, xn, given):
            for h in range(heads):
                dve.scalar_tensor_tensor(out=y[:, r, h * dh:(h + 1) * dh],
                                         in0=flat(m.acc[:, bass.ds(j, 1), h * (dh + 1):h * (dh + 1) + dh]),
                                         scalar=flat(inv[:, bass.ds(j, 1), h:h + 1]), in1=b1[:, h * dh:(h + 1) * dh],
                                         op0=ALU.mult, op1=ALU.add).then_inc(steps, 1)
            dve.wait_ge(steps, j * PER + heads)
            dve.tensor_scalar(low[:, r, :], y[:, r, :], 0.0, None, ALU.min).then_inc(steps, 1)
            dve.wait_ge(raised, j + 1)
            dve.scalar_tensor_tensor(out=xn[:, r, :], in0=y[:, r, :], scalar=0.0, in1=low[:, r, :],
                                     op0=ALU.max, op1=ALU.add).then_inc(given, 1)

        def elu_act(act, r, j):
            act.wait_ge(steps, j * PER + PER)
            act.activation(low[:, r, :], low[:, r, :], ACT.Exp).then_inc(raised, 1)

        tr = transform(n, m, "d_", "elu", w, wl, wc, "attention", heads=1, table=m.rows2, t_table=m.t2,
                       vectors=v, vectors_ready=vl, vectors_count=vc, elu={"dve": elu_dve, "act": elu_act})
        run_parts(n.block(), {"sp": lambda sp: sp.dma_start(b1[:, :], a.b1.partition_broadcast(P)).then_inc(b_in, 16),
                              "dve": lambda dve: dve.wait_ge(b_in, 16)}, wp, vp, ip, tr)


def finish(nc, m, a, out):
    with Net(nc) as n:
        ip, inv, sums = inverse_sums(n, m, "f_", 1, D + 1, 1e-16)
        b2 = n.sb("f_b2", [P, D])
        b_in, step, stored = n.sem("f_b_in"), n.sem("f_step"), n.sem("f_stored")
        x, got = m.acc[:, :, X_AT:X_AT + D], m.acc[:, :, 0:D]
        b_all = b2[:, :].unsqueeze(1).to_broadcast([P, NT, D])

        def sp(sp):
            sp.dma_start(b2[:, :], a.b2.partition_broadcast(P)).then_inc(b_in, 16)
            sp.wait_ge(step, 3)
            sp.dma_start(node_rows(out[0:FULL * P, :]), x[:, 0:FULL, :]).then_inc(stored, 16)
            sp.dma_start(out[FULL * P:N, :], x[0:REST, FULL, :]).then_inc(stored, 16)
            sp.wait_ge(stored, 32)

        def dve(dve):
            dve.tensor_tensor(got, got, inv[:, :, 0:1].to_broadcast([P, NT, D]), ALU.mult).then_inc(step, 1)
            dve.wait_ge(b_in, 16)
            dve.wait_ge(step, 1)
            dve.tensor_tensor(x, x, got, ALU.add).then_inc(step, 1)
            dve.wait_ge(step, 2)
            dve.tensor_tensor(x, x, b_all, ALU.add).then_inc(step, 1)

        run_parts(n.block(), ip, {"sp": sp, "dve": dve})


def build(nc, a, out, upto=99):
    m = named()
    dram = nc.dram_tensor
    m.rec_dst = dram("rec_dst", [P * SL, 4], F32).ap()
    m.rec_src = dram("rec_src", [P * SL, 4], F32).ap()
    m.key_rows = dram("key_rows", [SL, P], BF16).ap()
    m.z = dram("z", [REL * NP, D], F32).ap()
    m.support = dram("support", [NP, D], F32).ap()
    m.gat_rows = dram("gat_rows", [NP, D + 2], F32).ap()
    m.gat_t = dram("gat_t", [NP, 2], F32).ap()
    m.rows1 = dram("rows1", [NP, 4 * (P + 1)], F32).ap()
    m.t1 = dram("t1", [NP, 4], F32).ap()
    m.rows2 = dram("rows2", [NP, D + 1], F32).ap()
    m.t2 = dram("t2", [NP, 1], F32).ap()
    m.x_kept = dram("x_kept", [NP, D], F32).ap()
    with Net(nc) as n:
        m.ps = n.ps("ps", [P, 8, 512])
        m.iota_n, m.iota_p = n.sb("iota_n", [P, P]), n.sb("iota_p", [P, 1])
        m.iota_b, m.ident_b = n.sb("iota_b", [P, P], BF16), n.sb("ident_b", [P, P], BF16)
        m.ident = n.sb("ident", [P, P])
        m.words_dst = n.sb("words_dst", [1, SL // PACK], I32)
        m.words_src = n.sb("words_src", [1, SL // PACK], I32)
        m.rec = n.sb("rec", [P, SL, 4])
        m.acc = n.sb("acc", [P, NT, W_ACC])
        sort_edges(nc, m, a)
        if upto < 1: return
        message_pass(nc, m, "p0_", m.rec_dst, m.words_dst, 0, m.z, 1, D, 0, weight=3)
        rgcn_second(nc, m, a)
        message_pass(nc, m, "p1_", m.rec_dst, m.words_dst, 0, m.z, 1, D, 0, weight=3)
        if upto < 2: return
        gcn_support(nc, m, a)
        message_pass(nc, m, "p2_", m.rec_src, m.words_src, 0, m.support, 1, D, X_AT, weight=2)
        if upto < 3: return
        for i, (heads, width, tables, rec, words, index, rows, t) in enumerate((
                (2, P + 1, gat_tables, m.rec_src, m.words_src, 0, m.gat_rows, m.gat_t),
                (4, P + 1, gat_first_of_two, m.rec_dst, m.words_dst, 2, m.rows1, m.t1),
                (1, D + 1, gat_second_of_two, m.rec_dst, m.words_dst, 2, m.rows2, m.t2))):
            with Net(nc) as k:
                m.tab = k.sb(f"tab{i}", [P, NT, 2 * heads])
                tables(nc, m, a)
                with Net(nc) as e:
                    m.edge_t = e.sb(f"edge_t{i}", [P, SL, heads])
                    max_pass(nc, m, f"m{i}_", rec, words, index, t, heads, i < 2, heads * width, i == 2)
                    message_pass(nc, m, f"q{i}_", rec, words, index, rows, heads, width, 0)
            if upto < 4 + i: return
        finish(nc, m, a, out)


def sort_edges(nc, m, a):
    with Net(nc) as k:
        row_b = k.sb("row_b", [P, COLS], U32)
        rec_b = k.sb("rec_b", [P, COLS, 4])
        with Net(nc) as n:
            m.ones, m.below = n.sb("ones", [P, P]), n.sb("below", [P, P])
            m.iota_s = n.sb("iota_s", [P, SL])
            constants(nc, m)
            column = {name: n.sb("s_" + name, [P, COLS], dt) for name, dt in
                      (("src", I32), ("dst", I32), ("etype", I32), ("weight", F32), ("typef", F32), ("srcf", F32))}
            s = named(rec_b=rec_b, rec_a=m.rec[:, 0:COLS, :], **column)
            s.by_dst = named(tile=n.sb("d_tile", [P, COLS]), key=n.sb("d_key", [P, COLS]),
                                       row=n.sb("d_row", [P, COLS], U32), words=m.words_dst)
            s.by_src = named(tile=s.typef, key=s.srcf, row=row_b, words=m.words_src)
            rank_by_dst(nc, m, s, a.src, a.dst, a.etype, a.weight)
            with Net(nc) as e:
                rank = rank_by_src(nc, e, m, s)
                run_parts(e.block(), rank,
                          {"pool": lambda pool: scatter_records(pool, e, s.by_dst.row, s.rec_a, m.rec_dst, "sa_")})
        with Net(nc) as n:
            loads, tables = rgcn_first(n, m, a)
            run_parts(n.block(), *loads, inverse_counts(nc, n, m), *tables,
                      {"pool": lambda pool: scatter_records(pool, n, row_b, rec_b, m.rec_src, "sb_")})


_INS = {"x": "x", "src": "src", "dst": "dst", "edge_type_8": "etype", "edge_weight": "weight",
        "L0_gnn_comps": "comps", "L0_gnn_bases": "bases", "L0_gnn_roots": "roots", "L0_gnn_biases": "biases",
        "L1_gnn_weight": "gcn_w", "L2_gnn_W_w": "gat_w", "L2_gnn_W_b": "gat_b", "L2_gnn_a": "gat_a",
        "L3_gnn_W1": "w1", "L3_gnn_a_src1": "a_src1", "L3_gnn_a_dst1": "a_dst1", "L3_gnn_b1": "b1",
        "L3_gnn_W2": "w2", "L3_gnn_a_src2": "a_src2", "L3_gnn_a_dst2": "a_dst2", "L3_gnn_b2": "b2"}


def kernel(**inputs):
    import concourse.bacc as _bacc
    from concourse.bass_utils import run_bass_kernel_spmd as _run

    nc = _bacc.Bacc("TRN2", target_bir_lowering=False, num_devices=1)
    arrays, aps = {}, {}
    for name, short in _INS.items():
        v = np.ascontiguousarray(inputs[name])
        arrays[f"in_{name}"] = v
        aps[short] = nc.dram_tensor(f"in_{name}", v.shape, mybir.dt.from_np(v.dtype), kind="ExternalInput").ap()
    out = nc.dram_tensor("out_x", (N, D), F32, kind="ExternalOutput").ap()
    build(nc, named(**aps), out)
    return _run(nc, [arrays], core_ids=[0]).results[0]["out_x"]
```

```python
from contextlib import ExitStack

import numpy as np
import concourse.bass as bass
from concourse import mybir

ALU = mybir.AluOpType
ACT = mybir.ActivationFunctionType
AX = mybir.AxisListType
F32 = mybir.dt.float32
BF16 = mybir.dt.bfloat16
I32 = mybir.dt.int32
U32 = mybir.dt.uint32

P = 128
N = 6250
E = 100000
D = 256
REL, BASES = 8, 4
NT = -(-N // P)
NT += NT % 2
PAD_NODE = (NT - 1) * P
NP = NT * P
COLS = -(-E // P)
BODY = 16
QUAD = 4
NQ = BODY // QUAD
SLOTS = -(-((COLS * P + (P - 1) * NT) // P) // BODY) * BODY
TURNS = SLOTS // BODY
SL = SLOTS + BODY
PACK = 4
BITS = 6
KEY_NONE = 999.0
W_ACC = 516
X_AT = W_ACC - D
NEG = -1.0e30
EPS = 1e-5
SLOPE = 0.2
RING = 4
HOTS = 8
LEAD = 4
GROUP = next(g for g in range(20, 0, -1) if COLS % (2 * g) == 0)
STATS = next(u for u in range(10, 0, -1) if NT % u == 0)
assert NT <= TURNS and NT <= 1 << BITS and SL % PACK == 0


def named(**parts):
    return type("Named", (), parts)


class Net:

    def __init__(self, nc):
        self.nc, self.ctx, self.sems = nc, ExitStack(), []

    def __enter__(self):
        self.ctx.__enter__()
        return self

    def __exit__(self, *a):
        done = self.ctx.__exit__(*a)
        if self.sems and not a[0]:
            self.nc.clear_and_free_semaphores(self.sems)
            self.nc.all_engine_barrier()
        return done

    def sb(self, name, shape, dt=F32):
        return self.ctx.enter_context(self.nc.sbuf_tensor(name, shape, dt))

    def ps(self, name, shape, dt=F32):
        return self.ctx.enter_context(self.nc.psum_tensor(name, shape, dt))

    def sem(self, name):
        self.sems.append(self.nc.alloc_semaphore(name=name))
        return self.sems[-1]

    def block(self):
        return self.ctx.enter_context(self.nc.Block())


def edges_as_tiles(a):
    full = E // COLS
    rest = E - full * COLS
    return ((0, full, COLS, a[0:full * COLS].rearrange("(p c) -> p c", c=COLS)),
            (full, full + 1, rest, a[full * COLS:E].rearrange("(p c) -> p c", p=1)))


def constants(nc, m):
    with Net(nc) as n:
        made = n.sem("c_made")
        moved = n.sem("c_moved")
        block = n.block()

        @block.gpsimd
        def _(pool):
            pool.iota(m.iota_n[:, :], [[1, P]], base=0, channel_multiplier=0,
                      allow_small_or_imprecise_dtypes=True).then_inc(made, 1)
            pool.iota(m.iota_b[:, :], [[1, P]], base=0, channel_multiplier=0,
                      allow_small_or_imprecise_dtypes=True).then_inc(made, 1)
            pool.iota(m.iota_p[:, :], [[0, 1]], base=0, channel_multiplier=1,
                      allow_small_or_imprecise_dtypes=True).then_inc(made, 1)
            pool.iota(m.iota_s[:, :], [[1, SL]], base=0, channel_multiplier=0,
                      allow_small_or_imprecise_dtypes=True).then_inc(made, 1)
            pool.memset(m.ones[:, :], 1.0).then_inc(made, 1)

        @block.vector
        def _(dve):
            dve.wait_ge(made, 5)
            dve.tensor_scalar(m.ident[:, :], m.iota_n[:, :], m.iota_p[:, 0:1], None, ALU.is_equal).then_inc(moved, 1)
            dve.tensor_scalar(m.ident_b[:, :], m.iota_n[:, :], m.iota_p[:, 0:1], None, ALU.is_equal).then_inc(moved, 1)
            dve.tensor_scalar(m.below[:, :], m.iota_n[:, :], m.iota_p[:, 0:1], None, ALU.is_gt).then_inc(moved, 1)


def rank_edges(nc, n, m, s, key, name):
    last = COLS - 1
    c = named(
        tot=n.sb(name + "tot", [P, NT]), mask=n.sb(name + "mask", [P, COLS]), cum=n.sb(name + "cum", [P, COLS]),
        sel=n.sb(name + "sel", [P, COLS]), place=n.sb(name + "place", [P, COLS]),
        zero=n.sb(name + "zero", [P, COLS]), base=n.sb(name + "base", [P, NT]),
        count=n.sb(name + "count", [NT, 1]), count_i=n.sb(name + "count_i", [NT, 1], I32),
        slots_i=n.sb(name + "slots_i", [NT, 1], I32), slots=n.sb(name + "slots", [NT, 1]),
        first=n.sb(name + "first", [NT, 1]), begun=n.sb(name + "begun", [NT, SL]),
        word=n.sb(name + "word", [1, SL // PACK]), place_i=n.sb(name + "place_i", [P, COLS], I32),
        lane=n.sb(name + "lane", [P, COLS], I32), slot=n.sb(name + "slot", [P, COLS], I32),
        small=m.ps[:, 0, :], wide=m.ps[:, 1:3, :])
    spare = m.acc[:, 0:-(-COLS // W_ACC), :].rearrange("p j c -> p (j c)")
    c.masks = [c.mask, spare[:, 0:COLS]]
    c.cums = [c.cum, c.sel]
    chain = n.sem(name + "chain")
    counted = n.sem(name + "counted")
    half = SL // 2

    def vector(dve, loaded, loads):
        k = 0
        dve.wait_ge(loaded, loads)
        dve.tensor_scalar(c.place_i[:, :], key[:, :], 7, None, ALU.logical_shift_right).then_inc(chain, 1)
        dve.tensor_scalar(c.lane[:, :], key[:, :], P - 1, None, ALU.bitwise_and).then_inc(chain, 1)
        dve.memset(c.zero[:, :], 0.0).then_inc(chain, 1)
        dve.memset(c.place[:, :], 0.0).then_inc(chain, 1)
        k = 4
        dve.wait_ge(chain, k)
        dve.tensor_copy(s.tile[:, :], c.place_i[:, :]).then_inc(chain, 1)
        dve.tensor_copy(s.key[:, :], c.lane[:, :]).then_inc(chain, 1)
        k += 2
        dve.wait_ge(chain, k)
        with dve.Fori(0, NT // 2) as i:
            for r in range(2):
                b = i * 2 + r
                dve.wait_ge(chain, b + (k - 1))
                dve.tensor_scalar(c.masks[r][:, :], s.tile[:, :], m.iota_n[:, bass.ds(b, 1)], None, ALU.is_equal,
                                  ALU.add, accum_out=c.tot[:, bass.ds(b, 1)]).then_inc(chain, 1)
        k += NT
        dve.wait_ge(counted, 1)
        dve.wait_ge(chain, k)
        dve.tensor_scalar(c.count_i[:, :], c.small[0:NT, 0:1], float(P - 1), None, ALU.add).then_inc(chain, 1)
        dve.wait_ge(chain, k + 1)
        dve.tensor_scalar(c.slots_i[:, :], c.count_i[:, :], 7, None, ALU.logical_shift_right).then_inc(chain, 1)
        dve.wait_ge(chain, k + 2)
        dve.tensor_copy(c.slots[:, :], c.slots_i[:, :]).then_inc(chain, 1)
        k += 3
        dve.wait_ge(counted, 4)
        dve.tensor_scalar(c.base[:, :], c.small[:, 64:64 + NT], float(P), None, ALU.mult).then_inc(chain, 1)
        dve.wait_ge(chain, k + 1)
        dve.tensor_tensor(c.base[:, :], c.base[:, :], c.small[:, 128:128 + NT], ALU.add).then_inc(chain, 1)
        dve.tensor_copy(c.first[:, :], c.small[0:NT, 1:2]).then_inc(chain, 1)
        k += 3
        dve.wait_ge(chain, k)
        dve.tensor_scalar(c.begun[:, :], m.iota_s[0:NT, :], c.first[:, 0:1], None, ALU.is_ge).then_inc(chain, 1)
        k += 1
        with dve.Fori(0, NT // 2) as i:
            at = i * 8
            for r in range(2):
                dve.wait_ge(chain, at + (k - 2 + r))
                dve.tensor_scalar(c.masks[r][:, :], s.tile[:, :], m.iota_n[:, bass.ds(i * 2 + r, 1)], None,
                                  ALU.is_equal).then_inc(chain, 1)
            for r in range(2):
                dve.wait_ge(chain, at + (k + 1 + r))
                dve.tensor_tensor_scan(c.cums[r][:, :], c.masks[r][:, :], c.zero[:, :], c.base[:, bass.ds(i * 2 + r, 1)],
                                       ALU.add, ALU.add).then_inc(chain, 1)
            for r in range(2):
                dve.wait_ge(chain, at + (k + 3 + r))
                dve.tensor_tensor(c.cums[r][:, :], c.masks[r][:, :], c.cums[r][:, :], ALU.mult).then_inc(chain, 1)
            for r in range(2):
                dve.wait_ge(chain, at + (k + 5 + 2 * r))
                dve.tensor_tensor(c.place[:, :], c.place[:, :], c.cums[r][:, :], ALU.add).then_inc(chain, 1)
        k += 4 * NT
        dve.wait_ge(chain, k)
        dve.tensor_scalar(c.place_i[:, :], c.place[:, :], -1.0, None, ALU.add).then_inc(chain, 1)
        dve.wait_ge(chain, k + 1)
        dve.tensor_scalar(c.lane[:, :], c.place_i[:, :], P - 1, None, ALU.bitwise_and).then_inc(chain, 1)
        dve.tensor_scalar(c.slot[:, :], c.place_i[:, :], 7, None, ALU.logical_shift_right).then_inc(chain, 1)
        dve.wait_ge(chain, k + 3)
        dve.tensor_copy(c.cum[:, :], c.lane[:, :]).then_inc(chain, 1)
        dve.tensor_copy(c.sel[:, :], c.slot[:, :]).then_inc(chain, 1)
        dve.wait_ge(chain, k + 5)
        dve.scalar_tensor_tensor(out=s.row[:, :], in0=c.cum[:, :], scalar=float(SL), in1=c.sel[:, :],
                                 op0=ALU.mult, op1=ALU.add).then_inc(chain, 1)
        k += 6
        dve.wait_ge(counted, 6)
        t = [c.wide[0:1, h, 0:half].rearrange("o (w q) -> o w q", q=PACK) for h in range(2)]
        hw = half // PACK
        for h in range(2):
            w = c.word[:, h * hw:(h + 1) * hw]
            dve.tensor_scalar(w, t[h][:, :, PACK - 1], -1.0, None, ALU.add).then_inc(chain, 1)
            k += 1
            for q in range(PACK - 2, -1, -1):
                dve.wait_ge(chain, k)
                dve.tensor_scalar(w, w, float(1 << BITS), -1.0, ALU.mult, ALU.add).then_inc(chain, 1)
                dve.wait_ge(chain, k + 1)
                dve.tensor_tensor(w, w, t[h][:, :, q], ALU.add).then_inc(chain, 1)
                k += 2
        dve.wait_ge(chain, k)
        dve.tensor_copy(s.words[:, :], c.word[:, :]).then_inc(chain, 1)
        dve.wait_ge(chain, k + 1)
        return k + 1

    def tensor(pe, dve_before):
        k = dve_before + 6 + NT
        pe.wait_ge(chain, k)
        pe.matmul(c.small[0:NT, 0:1], c.tot[:, :], m.ones[:, 0:1], start=True, stop=True).then_inc(counted, 1)
        pe.wait_ge(chain, k + 3)
        pe.matmul(c.small[0:NT, 1:2], m.below[0:NT, 0:NT], c.slots[:, :], start=True, stop=True).then_inc(counted, 1)
        pe.matmul(c.small[:, 64:64 + NT], c.slots[:, 0:1].to_broadcast([NT, P]), m.below[0:NT, 0:NT],
                  start=True, stop=True).then_inc(counted, 1)
        pe.matmul(c.small[:, 128:128 + NT], m.below[:, :], c.tot[:, :], start=True, stop=True).then_inc(counted, 1)
        pe.wait_ge(chain, k + 7)
        for h in range(2):
            pe.matmul(c.wide[:, h, 0:half], m.ones[0:NT, :], c.begun[:, h * half:(h + 1) * half],
                      start=True, stop=True).then_inc(counted, 1)

    return vector, tensor


def rank_by_dst(nc, m, s, src, dst, etype, weight):
    with Net(nc) as n:
        loaded, filled, stored = n.sem("ld_edges"), n.sem("ld_filled"), n.sem("ld_stored")
        empty = n.sb("empty", [P, SL, 4])
        vector, tensor = rank_edges(nc, n, m, s.by_dst, s.dst, "rd_")
        blank, built = n.sem("ld_blank"), n.sem("ld_built")
        block = n.block()

        @block.gpsimd
        def _(pool):
            for a, v in ((s.src, PAD_NODE), (s.dst, PAD_NODE), (s.etype, 0)):
                pool.memset(a[:, :], v).then_inc(filled, 1)
            pool.memset(s.weight[:, :], 0.0).then_inc(filled, 1)
            pool.memset(empty[:, :, :], 0.0).then_inc(blank, 1)
            pool.wait_ge(blank, 1)
            pool.memset(empty[:, :, 1:2], KEY_NONE).then_inc(blank, 1)

        @block.sync
        def _(sp):
            sp.wait_ge(filled, 4)
            for a, d in ((s.dst, dst), (s.src, src), (s.etype, etype), (s.weight, weight)):
                for p0, p1, w, piece in edges_as_tiles(d):
                    sp.dma_start(a[p0:p1, 0:w], piece).then_inc(loaded, 16)
            sp.wait_ge(blank, 2)
            for rec in (m.rec_dst, m.rec_src):
                sp.dma_start(rec.rearrange("(p s) w -> p (s w)", p=P),
                             empty[:, :, :].rearrange("p s w -> p (s w)")).then_inc(stored, 16)
            sp.wait_ge(stored, 32)

        @block.tensor
        def _(pe):
            tensor(pe, 0)

        @block.vector
        def _(dve):
            vector(dve, loaded, 16 * 8)
            dve.tensor_copy(s.typef[:, :], s.etype[:, :]).then_inc(built, 1)
            dve.tensor_copy(s.srcf[:, :], s.src[:, :]).then_inc(built, 1)
            r = s.rec_a
            dve.wait_ge(built, 2)
            dve.scalar_tensor_tensor(out=r[:, :, 0].bitcast(U32), in0=s.typef[:, :], scalar=float(NP), in1=s.srcf[:, :],
                                     op0=ALU.mult, op1=ALU.add).then_inc(built, 1)
            dve.tensor_copy(r[:, :, 1], s.by_dst.key[:, :]).then_inc(built, 1)
            dve.tensor_copy(r[:, :, 2].bitcast(I32), s.src[:, :]).then_inc(built, 1)
            dve.tensor_copy(r[:, :, 3], s.typef[:, :]).then_inc(built, 1)
            dve.wait_ge(built, 6)


def scatter_records(pool, n, rows, rec, table, name):
    copied = n.sem(name + "copied")
    issuing = n.sem(name + "issuing")
    landed = [n.sem(name + f"landed{h}") for h in range(2)]
    ring_r = n.sb(name + "ring_r", [P, 2, GROUP], U32)
    ring_d = n.sb(name + "ring_d", [P, 2, GROUP, 4])

    def group(c, h, i):
        at = c * GROUP
        pool.tensor_copy(ring_r[:, h, :], rows[:, bass.ds(at, GROUP)]).then_inc(copied, 1)
        pool.tensor_copy(ring_d[:, h, :, :], rec[:, bass.ds(at, GROUP), :]).then_inc(copied, 1)
        pool.wait_ge(copied, c * 2 + 2)
        pool.sem_inc(issuing, 1)
        for g in range(GROUP):
            pool.indirect_dma_start(table, bass.IndirectOffsetOnAxis(ring_r[:, h, g:g + 1], 0),
                                    ring_d[:, h, g, :], None).then_inc(landed[h], 16)

    for h in range(2):
        group(h, h, 0)
    with pool.Fori(1, COLS // (2 * GROUP)) as i:
        for h in range(2):
            pool.wait_ge(landed[h], i * (16 * GROUP))
            group(i * 2 + h, h, i)
    for h in range(2):
        pool.wait_ge(landed[h], 16 * GROUP * (COLS // (2 * GROUP)))


def run_parts(block, *parts):
    @block.sync
    def _(sp):
        for p in parts:
            if "sp" in p:
                p["sp"](sp)

    @block.tensor
    def _(pe):
        for p in parts:
            if "pe" in p:
                p["pe"](pe)

    @block.vector
    def _(dve):
        for p in parts:
            if "dve" in p:
                p["dve"](dve)

    @block.scalar
    def _(act):
        for p in parts:
            if "act" in p:
                p["act"](act)

    @block.gpsimd
    def _(pool):
        for p in parts:
            if "pool" in p:
                p["pool"](pool)


def load_tiles(eng, words, slot, count):
    out = []
    for w in range(count // PACK):
        word = eng.value_load(words[0:1, bass.ds(slot // PACK + w, 1)], min_val=0, max_val=(1 << BITS * PACK) - 1)
        for q in range(PACK):
            v = (word >> (BITS * q)) & ((1 << BITS) - 1)
            out.append(eng.snap(v.with_bounds(min_val=0, max_val=NT - 1)))
    return out


def rank_by_src(nc, n, m, s):
    vector, tensor = rank_edges(nc, n, m, s.by_src, s.src, "rs_")
    ready, built = n.sem("rs_ready"), n.sem("rs_built")

    def dve(dve):
        dve.sem_inc(ready, 1)
        vector(dve, ready, 1)
        r = s.rec_b
        dve.tensor_copy(r[:, :, 0].bitcast(I32), s.dst[:, :]).then_inc(built, 1)
        dve.tensor_copy(r[:, :, 1], s.by_src.key[:, :]).then_inc(built, 1)
        dve.tensor_copy(r[:, :, 2], s.weight[:, :]).then_inc(built, 1)
        dve.memset(r[:, :, 3], 0.0).then_inc(built, 1)
        dve.wait_ge(built, 4)

    return {"dve": dve, "pe": lambda pe: tensor(pe, 0)}


def split_exactly(dve, source, rest, parts, step):
    left = source
    for i in range(3):
        dve.tensor_copy(parts(i), left).then_inc(step, 1)
        dve.wait_ge(step, 2 * i + 1)
        if i < 2:
            dve.tensor_tensor(rest, left, parts(i), ALU.subtract).then_inc(step, 1)
            dve.wait_ge(step, 2 * i + 2)
            left = rest


def key_rows(n, m, name, loaded=None):
    blocks = -(-SL // P)
    turned, copied, stored = n.sem(name + "turned"), n.sem(name + "copied"), n.sem(name + "stored")
    kt = n.sb(name + "kt", [P, blocks, P], BF16)
    pt = m.ps[:, 0:2, :]

    def width(b):
        return min(P, SL - b * P)

    def view(b):
        return pt[0:width(b), b // 4, (b % 4) * P:(b % 4 + 1) * P]

    def pe(pe):
        if loaded:
            pe.wait_ge(loaded, 16)
        for b in range(blocks):
            pe.transpose(view(b), m.rec[:, b * P:b * P + width(b), 1], m.ident[:, :]).then_inc(turned, 1)
        pe.wait_ge(copied, blocks)

    def act(act):
        for b in range(blocks):
            act.wait_ge(turned, min(b // 4 * 4 + 4, blocks))
            act.activation(kt[0:width(b), b, :], view(b), ACT.Copy).then_inc(copied, 1)

    def sp(sp):
        sp.wait_ge(copied, blocks)
        for b in range(blocks):
            sp.dma_start(m.key_rows[b * P:b * P + width(b), :], kt[0:width(b), b, :]).then_inc(stored, 16)
        sp.wait_ge(stored, 16 * blocks)

    return {"pe": pe, "act": act, "sp": sp}


def inverse_counts(nc, n, m):
    loaded = n.sem("ic_loaded")
    rows = key_rows(n, m, "kd_", loaded)
    HALF = BODY // 2
    HALVES = 2 * TURNS
    oh = n.sb("ic_oh", [P, HOTS, P], BF16)
    rel = n.sb("ic_rel", [P, BODY, REL], BF16)
    cnt = n.sb("ic_cnt", [P, NT, REL])
    odd = n.sb("ic_odd", [P, NT, REL])
    kb = n.sb("ic_kb", [P, BODY * P], BF16)
    oht = n.sb("ic_oht", [P, BODY, P], BF16)
    rest = n.sb("ic_rest", [P, NT, REL])
    inv3 = n.sb("ic_inv3", [P, NT, 3 * REL], BF16)
    inv_of = n.sb("ic_inv_of", [P, HALF, 3 * REL], BF16)
    rel_f = n.sb("ic_rel_f", [P, BODY, REL])
    prod = n.sb("ic_prod", [P, BODY, 3, REL])
    per_edge = n.sb("ic_per_edge", [P, BODY])
    pc = [m.ps[:, 4 + k // QUAD % 2, k % QUAD * REL:(k % QUAD + 1) * REL] for k in range(BODY)]
    px = [m.ps[:, 6 + h, 0:HALF * 3 * REL].rearrange("p (s c) -> p s c", s=HALF) for h in range(2)]
    begun, inv = n.sem("ic_begun"), n.sem("ic_inv")
    rel_ready = n.sem("ic_rel_ready")
    built = n.sem("ic_built")
    counted = n.sem("ic_counted")
    added = n.sem("ic_added")
    got = [n.sem(f"ic_got{h}") for h in range(2)]
    turned = n.sem("ic_turned")
    parted = n.sem("ic_parted")
    rows_set = n.sem("ic_rows_set")
    spread = n.sem("ic_spread")
    rel_set = n.sem("ic_rel_set")
    chosen = n.sem("ic_chosen")
    summed = n.sem("ic_summed")
    wrote = n.sem("ic_wrote")

    def sp(sp):
        sp.dma_start(m.rec[:, :, :].rearrange("p s w -> p (s w)"),
                     m.rec_dst.rearrange("(p s) w -> p (s w)", p=P)).then_inc(loaded, 16)
        rows["sp"](sp)

    def sp_after(sp):
        def fetch(t, h):
            keys = m.key_rows[bass.ds(t * BODY + h * HALF, HALF), :].rearrange("s e -> (s e)")
            sp.dma_start(kb[:, h * HALF * P:(h + 1) * HALF * P], keys.partition_broadcast(P)).then_inc(got[h], 16)

        for h in range(2):
            fetch(0, h)
        with sp.Fori(0, TURNS) as t:
            for h in range(2):
                sp.wait_ge(turned, t * 2 + (h + 1))
                fetch(t + 1, h)
        for h in range(2):
            sp.wait_ge(got[h], 16 * (TURNS + 1))

    def pe(pe):
        rows["pe"](pe)
        pe.sem_inc(counted, 2)

    def pe_count(pe, t, q):
        pe.wait_ge(rel_ready, t * NQ + (q + 1))
        pe.wait_ge(built, t * NQ + (q + 1))
        pe.wait_ge(added, t * BODY + (q + 1) * QUAD)
        for k in range(q * QUAD, (q + 1) * QUAD):
            mm = pe.matmul(pc[k], oh[:, k % HOTS, :], rel[:, k, :], start=True, stop=True)
        mm.then_inc(counted, 1)

    def pe_after(pe):
        pe.sem_inc(spread, 2)
        pe.wait_ge(parted, 5)
        with pe.Fori(0, TURNS) as t:
            tiles = load_tiles(pe, m.words_dst, t * BODY + HALF, HALF)
            for h in range(2):
                if h == 0:
                    pe.wait_ge(rows_set, t + 1)
                pe.wait_ge(turned, t * 2 + (h + 1))
                pe.wait_ge(chosen, t * 2 + (h + 1))
                for k in range(HALF):
                    rows_k = inv_of[:, k, :] if h == 0 else inv3[:, bass.ds(tiles[k], 1), :]
                    mm = pe.matmul(px[h][:, k, :], oht[:, h * HALF + k, :], rows_k, start=True, stop=True)
                mm.then_inc(spread, 1)
        pe.wait_ge(chosen, HALVES + 2)

    def act_after(act):
        act.wait_ge(parted, 5)
        with act.Fori(0, TURNS) as t:
            act.wait_ge(spread, t * 2 + 1)
            for q in range(NQ // 2):
                tiles = load_tiles(act, m.words_dst, t * BODY + q * QUAD, QUAD)
                for k in range(QUAD):
                    ins = act.copy(inv_of[:, q * QUAD + k:q * QUAD + k + 1, :], inv3[:, bass.ds(tiles[k], 1), :])
            ins.then_inc(rows_set, 1)

    def dve(dve):
        dve.wait_ge(loaded, 16)
        dve.memset(cnt[:, :, :], 0.0).then_inc(begun, 1)
        dve.memset(odd[:, :, :], 0.0).then_inc(begun, 1)
        dve.wait_ge(begun, 2)
        dve.sem_inc(added, 2 * QUAD)
        dve.sem_inc(chosen, 2)
        build(dve, 0, 0)

    def build(dve, t, q):
        at = q * QUAD % BODY
        keys = m.rec[:, bass.ds(t * BODY + q * QUAD, QUAD), :]
        dve.wait_ge(counted, t * NQ + (q + 1))
        dve.tensor_tensor(rel[:, at:at + QUAD, :], m.iota_b[:, 0:REL].unsqueeze(1).to_broadcast([P, QUAD, REL]),
                          keys[:, :, 3:4].to_broadcast([P, QUAD, REL]), ALU.is_equal).then_inc(rel_ready, 1)
        dve.tensor_tensor(oh[:, at % HOTS:at % HOTS + QUAD, :], m.iota_b[:, :].unsqueeze(1).to_broadcast([P, QUAD, P]),
                          keys[:, :, 1:2].to_broadcast([P, QUAD, P]), ALU.is_equal).then_inc(built, 1)

    def dve_count(dve, t, q):
        build(dve, t, q + 1)
        tiles = load_tiles(dve, m.words_dst, t * BODY + q * QUAD, QUAD)
        dve.wait_ge(counted, t * NQ + (q + 3))
        for k in range(q * QUAD, (q + 1) * QUAD):
            at = (odd if k % 2 else cnt)[:, bass.ds(tiles[k % QUAD], 1), :]
            dve.wait_ge(added, t * BODY + (k + 2 * QUAD - 1))
            dve.tensor_tensor(at, at, pc[k].rearrange("p (a r) -> p a r", a=1), ALU.add).then_inc(added, 1)

    def dve_after(dve):
        dve.wait_ge(added, SLOTS + 2 * QUAD)
        dve.tensor_tensor(cnt[:, :, :], cnt[:, :, :], odd[:, :, :], ALU.add).then_inc(inv, 1)
        dve.wait_ge(inv, 1)
        dve.tensor_scalar(cnt[:, :, :], cnt[:, :, :], 1.0, None, ALU.max).then_inc(inv, 1)
        dve.wait_ge(inv, 2)
        dve.reciprocal(cnt[:, :, :], cnt[:, :, :]).then_inc(inv, 1)
        dve.wait_ge(inv, 3)
        split_exactly(dve, cnt[:, :, :], rest[:, :, :], lambda i: inv3[:, :, i * REL:(i + 1) * REL], parted)

        def turn(t, h):
            dve.wait_ge(got[h], t * 16 + 16)
            dve.tensor_scalar(oht[:, h * HALF:(h + 1) * HALF, :].rearrange("p s e -> p (s e)"),
                              kb[:, h * HALF * P:(h + 1) * HALF * P], m.iota_p[:, 0:1], None, ALU.is_equal)\
               .then_inc(turned, 1)

        def relations_of_half(t, h):
            dve.tensor_tensor(rel_f[:, h * HALF:(h + 1) * HALF, :],
                              m.iota_n[:, 0:REL].unsqueeze(1).to_broadcast([P, HALF, REL]),
                              m.rec[:, bass.ds(t * BODY + h * HALF, HALF), 3:4].to_broadcast([P, HALF, REL]),
                              ALU.is_equal).then_inc(rel_set, 1)

        turn(0, 0)
        relations_of_half(0, 0)
        with dve.Fori(0, TURNS) as t:
            for h in range(2):
                a = slice(h * HALF, (h + 1) * HALF)
                u = t * 2 + h
                turn(t + h, 1 - h)
                dve.wait_ge(spread, u + 3)
                dve.wait_ge(rel_set, u + 1)
                dve.tensor_tensor(prod[:, a, :, :], rel_f[:, a, :].unsqueeze(2).to_broadcast([P, HALF, 3, REL]),
                                  px[h].rearrange("p s (q r) -> p s q r", q=3), ALU.mult).then_inc(chosen, 1)
                relations_of_half(t + h, 1 - h)
                dve.wait_ge(chosen, u + 3)
                dve.tensor_reduce(per_edge[:, a], prod[:, a, :, :].rearrange("p s q r -> p s (q r)"), AX.X, ALU.add)\
                   .then_inc(summed, 1)
                dve.wait_ge(summed, u + 1)
                dve.tensor_scalar(m.rec[:, bass.ds(t * BODY + h * HALF, HALF), 3], per_edge[:, a], 1.0, None, ALU.mult)\
                   .then_inc(wrote, 1)
        dve.wait_ge(wrote, HALVES)
        dve.wait_ge(turned, HALVES + 1)

    before = {"sp": sp, "pe": pe, "act": rows["act"], "dve": dve}
    return before, {"pe": pe_count, "dve": dve_count}, {"sp": sp_after, "pe": pe_after, "act": act_after,
                                                        "dve": dve_after}


def load_records(sp, m, table, loaded):
    sp.dma_start(m.rec[:, :, :].rearrange("p s w -> p (s w)"), table.rearrange("(p s) w -> p (s w)", p=P))\
      .then_inc(loaded, 16)
    sp.wait_ge(loaded, 16)


class Gathers:

    def __init__(self, n, m, table, width, index, name):
        self.m, self.table, self.index = m, table, index
        self.ring = n.sb(name + "ring", [P, BODY, width])
        self.rows = n.sb(name + "rows", [P, BODY], U32)
        self.rows_ready = n.sem(name + "rows_ready")
        self.issuing = n.sem(name + "issuing")
        self.landed = [n.sem(name + f"landed{q}") for q in range(NQ)]
        self.slots_used = n.sem(name + "slots_used")

    def copy_rows(self, act, turn, q):
        at = self.m.rec[:, bass.ds(turn * BODY + q * QUAD, QUAD), self.index].bitcast(U32)
        act.copy(self.rows[:, q * QUAD:(q + 1) * QUAD], at).then_inc(self.rows_ready, 1)

    def copy_next_rows(self, act, t, q):
        act.wait_ge(self.slots_used, t * BODY + (q + 1) * QUAD + HOTS)
        self.copy_rows(act, t + 1, q)

    def issue(self, pool):
        with pool.Fori(0, TURNS) as t:
            for q in range(NQ):
                pool.wait_ge(self.rows_ready, t * NQ + (q + 1))
                pool.sem_inc(self.issuing, 1)
                for k in range(q * QUAD, (q + 1) * QUAD):
                    pool.indirect_dma_start(self.ring[:, k, :], None, self.table,
                                            bass.IndirectOffsetOnAxis(self.rows[:, k:k + 1], 0))\
                        .then_inc(self.landed[q], 16)

    def wait_quad(self, eng, t, q):
        eng.wait_ge(self.landed[q], t * (16 * QUAD) + 16 * QUAD)


def message_pass(nc, m, name, words, index, table, heads, width, acc_at, weight=None):
    W = heads * width
    BK = -(-W // 512)
    CB = W // BK
    HB = heads // BK
    RP = 4 // BK
    HALF = BODY // 2
    H2 = 2 * heads
    attend = weight is None
    several = heads > 1
    helped = heads > 2
    with Net(nc) as n:
        g = Gathers(n, m, table, W, index, name)
        hot = n.sb(name + "hot", [P, HOTS, heads, P])
        hot_ready = n.sem(name + "hot_ready")
        added = n.sem(name + "added")
        if several:
            plain = n.sb(name + "plain", [P, HOTS, P])
            plain_ready = n.sem(name + "plain_ready")
            direct_ready = n.sem(name + "direct_ready")
        if attend:
            kb = n.sb(name + "kb", [P, BODY * P], BF16)
            oht = n.sb(name + "oht", [P, BODY, P], BF16)
            own = n.sb(name + "own", [P, 2, HALF, H2])
            z = n.sb(name + "z", [P, 2, HALF, heads])
            wt = n.sb(name + "wt", [P, BODY, heads])
            keys = n.sem(name + "keys")
            turned = n.sem(name + "turned")
            spread = n.sem(name + "spread")
            zs = n.sem(name + "zs")
            weighed = n.sem(name + "weighed")
            px = [m.ps[:, 4 + h, 0:HALF * 3 * H2].rearrange("p (s c) -> p s c", c=3 * H2) for h in range(2)]
        block = n.block()

        def product(k):
            return m.ps[:, k % RP * BK:(k % RP + 1) * BK, 0:CB]

        def need_weights(eng, t, k):
            if attend and k % HALF == 0:
                eng.wait_ge(weighed, t * 2 + (k // HALF + 1))

        @block.sync
        def _(sp):
            if attend:
                def fetch(t):
                    sp.dma_start(kb[:, :], m.key_rows[bass.ds(t * BODY, BODY), :].rearrange("s e -> (s e)")
                                 .partition_broadcast(P)).then_inc(keys, 16)
                fetch(0)
                with sp.Fori(0, TURNS) as t:
                    sp.wait_ge(turned, t * 2 + 2)
                    fetch(t + 1)

        @block.gpsimd
        def _(pool):
            g.issue(pool)

        @block.scalar
        def _(act):
            def weigh_half(t, h):
                act.wait_ge(zs, t * 10 + (5 * h + 5))
                act.activation(wt[:, h * HALF:(h + 1) * HALF, :], z[:, h, :, :], ACT.Exp)\
                   .then_inc(weighed, 1)

            def weigh_hot(t, k):
                need_weights(act, t + k // BODY, k % BODY)
                act.wait_ge(plain_ready, t * BODY + (k + 1))
                for h in range(heads - (helped and k % 2)):
                    ins = act.activation(hot[:, k % HOTS, h, :], plain[:, k % HOTS, :], ACT.Copy,
                                         scale=wt[:, k % BODY, h:h + 1])
                ins.then_inc(hot_ready, 1)

            for q in range(NQ):
                g.copy_rows(act, 0, q)
            if attend:
                weigh_half(0, 0)
            if several:
                for k in range(LEAD):
                    weigh_hot(0, k)
            with act.Fori(0, TURNS) as t:
                for k in range(BODY):
                    if several:
                        weigh_hot(t, k + LEAD)
                    if k % QUAD == QUAD - 1:
                        g.copy_next_rows(act, t, k // QUAD)
                    if attend and k == 2:
                        act.wait_ge(hot_ready, t * BODY + LEAD)
                        if helped:
                            act.wait_ge(direct_ready, t * HALF + LEAD // 2)
                        weigh_half(t, 1)
                    if attend and k == HALF + 3:
                        act.wait_ge(hot_ready, t * BODY + HALF)
                        if helped:
                            act.wait_ge(direct_ready, t * HALF + HALF // 2)
                        weigh_half(t + 1, 0)

        @block.tensor
        def _(pe):
            def spread_slot(t, s, tiles):
                h = s // HALF
                if s % QUAD == 0:
                    tiles[:] = load_tiles(pe, words, t * BODY + s, QUAD)
                if s % HALF == 0:
                    pe.wait_ge(turned, t * 2 + (h + 1))
                mm = pe.matmul(px[h][:, s % HALF, :], oht[:, s, :], m.tab3[:, bass.ds(tiles[s % QUAD], 1), :],
                               start=True, stop=True)
                if s % HALF == HALF - 1:
                    mm.then_inc(spread, 1)

            pe.sem_inc(g.slots_used, HOTS)
            tiles = []
            if attend:
                for s in range(BODY):
                    spread_slot(0, s, tiles)
            with pe.Fori(0, TURNS) as t:
                for k in range(BODY):
                    if k % QUAD == 0:
                        g.wait_quad(pe, t, k // QUAD)
                    pe.wait_ge(added, t * BODY + (k + 1))
                    pe.wait_ge(hot_ready, t * BODY + (k + 1))
                    if helped and k % 2:
                        pe.wait_ge(direct_ready, t * HALF + (k // 2 + 1))
                    out = product(k)
                    for h in range(heads):
                        c = h % HB * width
                        mm = pe.matmul(out[:, h // HB, c:c + width], hot[:, k % HOTS, h, :],
                                       g.ring[:, k, h * width:(h + 1) * width], start=True, stop=True)
                    mm.then_inc(g.slots_used, 1)
                    ahead = [s for s in (k - 1, k) if attend and (0 <= s < HALF and s == k - 1 or s >= HALF and s == k)]
                    for s in ahead:
                        if s % HALF == 0:
                            pe.wait_ge(zs, t * 10 + (5 * (s // HALF) + 1))
                        spread_slot(t + 1, s, tiles)

        @block.vector
        def _(dve):
            def turn_keys(t, h):
                if h == 0:
                    dve.wait_ge(keys, t * 16 + 16)
                dve.tensor_scalar(oht[:, h * HALF:(h + 1) * HALF, :].rearrange("p s e -> p (s e)"),
                                  kb[:, h * HALF * P:(h + 1) * HALF * P], m.iota_p[:, 0:1], None, ALU.is_equal)\
                   .then_inc(turned, 1)

            def score(t, h, i):
                zh = z[:, h, :, :]
                if i == 0:
                    dve.wait_ge(spread, t * 2 + (h + 1))
                    dve.tensor_reduce(own[:, h, :, :], px[h].rearrange("p s (q c) -> p s c q", q=3), AX.X, ALU.add)\
                       .then_inc(zs, 1)
                    return
                dve.wait_ge(zs, t * 10 + (5 * h + i))
                if i == 1:
                    dve.tensor_tensor(zh, own[:, h, :, 0:heads], m.edge_t[:, bass.ds(t * BODY + h * HALF, HALF), :],
                                      ALU.add).then_inc(zs, 1)
                elif i == 2:
                    dve.scalar_tensor_tensor(out=zh, in0=zh, scalar=SLOPE, in1=zh, op0=ALU.mult, op1=ALU.max)\
                       .then_inc(zs, 1)
                elif i == 3:
                    dve.tensor_tensor(zh, zh, own[:, h, :, heads:H2], ALU.subtract).then_inc(zs, 1)
                else:
                    dve.tensor_scalar(zh, zh, 0.0, None, ALU.min).then_inc(zs, 1)

            def build(t, k):
                key = m.rec[:, bass.ds(t * BODY + k, 1), 1:2]
                if several:
                    dve.wait_ge(g.slots_used, t * BODY + (k + 1))
                    dve.tensor_scalar(plain[:, k % HOTS, :], m.iota_n[:, :], key, None, ALU.is_equal)\
                       .then_inc(plain_ready, 1)
                    if helped and k % 2:
                        need_weights(dve, t + k // BODY, k % BODY // 2 * 2)
                        dve.tensor_scalar(hot[:, k % HOTS, heads - 1, :], m.iota_n[:, :], key,
                                          wt[:, k % BODY, heads - 1:heads], ALU.is_equal, ALU.mult)\
                           .then_inc(direct_ready, 1)
                    return
                w = wt[:, k % BODY, 0:1] if attend else m.rec[:, bass.ds(t * BODY + k, 1), weight:weight + 1]
                need_weights(dve, t + k // BODY, k % BODY)
                dve.wait_ge(g.slots_used, t * BODY + (k + 1))
                dve.tensor_scalar(hot[:, k % HOTS, 0, :], m.iota_n[:, :], key, w, ALU.is_equal, ALU.mult)\
                   .then_inc(hot_ready, 1)

            def add(t, k, tiles):
                at = m.acc[:, bass.ds(tiles[k % QUAD], 1), acc_at:acc_at + W].rearrange("p a (b c) -> p (a b) c", b=BK)
                dve.wait_ge(g.slots_used, t * BODY + (k + 1 + HOTS))
                dve.wait_ge(added, t * BODY + (k + RP))
                dve.tensor_tensor(at, at, product(k), ALU.add).then_inc(added, 1)

            dve.sem_inc(added, RP)
            if attend:
                turn_keys(0, 0)
                turn_keys(0, 1)
                for i in range(5):
                    score(0, 0, i)
            for k in range(LEAD):
                build(0, k)
            with dve.Fori(0, TURNS) as t:
                for k in range(BODY):
                    begin = HALF + 1 if k > HALF else 0
                    half = (t + 1, 0) if k > HALF else (t, 1)
                    steps = range(2 * (k - begin), 5)[:2] if attend and k != HALF else ()
                    if attend and k in (0, QUAD):
                        turn_keys(t + 1, k // QUAD)
                    build(t, k + LEAD)
                    if k % QUAD == 0:
                        tiles = load_tiles(dve, words, t * BODY + k, QUAD)
                    for i in steps[:1]:
                        if i == 0:
                            dve.wait_ge(weighed, t * 2 + 1)
                        score(*half, i)
                    add(t, k, tiles)
                    for i in steps[1:]:
                        score(*half, i)
            dve.wait_ge(added, SLOTS + RP)


def max_pass(nc, m, name, words, index, table, heads, turn_rows, fetch_x):
    G = 4 // heads
    GROUPS = BODY // G
    with Net(nc) as n:
        g = Gathers(n, m, table, heads, index, name)
        off = n.sb(name + "off", [P, HOTS, P], BF16)
        slot_max = n.sb(name + "slot_max", [P, RING, G, heads])
        top = n.sb(name + "top", [P, NT, heads])
        rest = n.sb(name + "rest", [P, NT, 2 * heads])
        parted = n.sem(name + "parted")
        off_ready = n.sem(name + "off_ready")
        reduced = n.sem(name + "reduced")
        topped = n.sem(name + "topped")
        kept = n.sem(name + "kept")
        blank, made, x_in = n.sem(name + "blank"), n.sem(name + "made"), n.sem(name + "x_in")
        rows = key_rows(n, m, name + "k") if turn_rows else None
        block = n.block()
        HC = heads * P

        def bank(k):
            return m.ps[:, 4 + k // G % RING, k % G * HC:(k % G + 1) * HC]

        @block.sync
        def _(sp):
            if rows:
                rows["sp"](sp)
            if fetch_x:
                sp.dma_start(m.acc[:, :, X_AT:X_AT + D], node_rows(m.x_kept)).then_inc(x_in, 16)
                sp.wait_ge(x_in, 16)

        @block.gpsimd
        def _(pool):
            pool.memset(m.edge_t[:, SLOTS:SL, :], 0.0).then_inc(blank, 1)
            g.issue(pool)

        @block.scalar
        def _(act):
            if rows:
                rows["act"](act)
            for q in range(NQ):
                g.copy_rows(act, 0, q)
            with act.Fori(0, TURNS) as t:
                for q in range(NQ):
                    g.wait_quad(act, t, q)
                    act.copy(m.edge_t[:, bass.ds(t * BODY + q * QUAD, QUAD), :], g.ring[:, q * QUAD:(q + 1) * QUAD, :])\
                       .then_inc(kept, 1)
                    act.wait_ge(kept, t * NQ + (q + 1))
                    g.copy_next_rows(act, t, q)

        @block.tensor
        def _(pe):
            if rows:
                rows["pe"](pe)
            pe.sem_inc(g.slots_used, HOTS)
            pe.wait_ge(blank, 2)
            with pe.Fori(0, TURNS) as t:
                for k in range(BODY):
                    if k % QUAD == 0:
                        g.wait_quad(pe, t, k // QUAD)
                    if k % G == 0:
                        pe.wait_ge(reduced, t * GROUPS + (k // G + 1))
                    pe.wait_ge(off_ready, t * BODY + (k + 1))
                    pe.matmul(bank(k), off[:, k % HOTS, :], m.ident_b[:, :].unsqueeze(1).to_broadcast([P, heads, P]),
                              start=True, stop=False, skip_group_check=True)
                    for h in range(heads):
                        mm = pe.matmul(bank(k)[:, h * P:(h + 1) * P], g.ring[:, k, h:h + 1].to_broadcast([P, P]),
                                       m.ident[:, :], start=False, stop=(h == heads - 1), skip_group_check=True)
                    mm.then_inc(g.slots_used, 1)

        @block.vector
        def _(dve):
            dve.memset(top[:, :, :], NEG).then_inc(blank, 1)
            dve.sem_inc(reduced, RING)
            dve.sem_inc(topped, 1)
            dve.wait_ge(blank, 2)

            def build(t, k):
                dve.wait_ge(g.slots_used, t * BODY + (k + 1))
                dve.tensor_scalar(off[:, k % HOTS, :], m.iota_b[:, :], m.rec[:, bass.ds(t * BODY + k, 1), 1:2], NEG,
                                  ALU.not_equal, ALU.mult).then_inc(off_ready, 1)

            def reduce_group(t, i):
                dve.wait_ge(g.slots_used, t * BODY + ((i + 1) * G + HOTS))
                dve.tensor_reduce(slot_max[:, i % RING, :, :],
                                  m.ps[:, 4 + i % RING, :].rearrange("p (g h e) -> p g h e", g=G, h=heads),
                                  AX.X, ALU.max).then_inc(reduced, 1)

            def take(t, k, tiles):
                at = top[:, bass.ds(tiles[k % QUAD], 1), :]
                dve.wait_ge(reduced, t * GROUPS + (k // G + 1 + RING))
                dve.wait_ge(topped, t * BODY + (k + 1))
                dve.tensor_tensor(at, at, slot_max[:, k // G % RING, k % G:k % G + 1, :], ALU.max).then_inc(topped, 1)

            for k in range(LEAD):
                build(0, k)
            with dve.Fori(0, TURNS) as t:
                for k in range(BODY):
                    if k % G == 0:
                        reduce_group(t, k // G)
                    build(t, k + LEAD)
                    if k % QUAD == 0:
                        tiles = load_tiles(dve, words, t * BODY + k, QUAD)
                    take(t, k, tiles)
            dve.wait_ge(topped, SLOTS + 1)
            s, mx = m.tab[:, :, 0:heads], m.tab[:, :, heads:2 * heads]
            dve.tensor_tensor(mx, s, top[:, :, :], ALU.add).then_inc(made, 1)
            dve.wait_ge(made, 1)
            dve.scalar_tensor_tensor(out=mx, in0=mx, scalar=SLOPE, in1=mx, op0=ALU.mult, op1=ALU.max).then_inc(made, 1)
            dve.wait_ge(made, 2)
            split_exactly(dve, m.tab[:, :, :], rest[:, :, :],
                          lambda i: m.tab3[:, :, i * 2 * heads:(i + 1) * 2 * heads], parted)


FULL = N // P
REST = N - FULL * P
PAIRS = NT // 2


def node_rows(a):
    return a.rearrange("(j p) d -> p j d", p=P)


def flat(ap):
    return ap.rearrange("p a c -> p (a c)")


def norm_part(n, m, name, ready, count):
    st = n.sb(name + "st", [P, NT, 6])
    mean = n.sb(name + "mean", [P, NT])
    rstd = n.sb(name + "rstd", [P, NT])
    half = n.sb(name + "half", [P, NT])
    var = n.sb(name + "var", [P, NT])
    steps, root = n.sem(name + "steps"), n.sem(name + "root")

    def dve(dve):
        dve.wait_ge(ready, count)
        with dve.Fori(0, NT // STATS) as i:
            for r in range(STATS):
                j = i * STATS + r
                dve.bn_stats(flat(st[:, bass.ds(j, 1), :]), flat(m.acc[:, bass.ds(j, 1), X_AT:X_AT + D])).then_inc(steps, 1)
        k = NT
        dve.wait_ge(steps, k)
        dve.tensor_tensor(mean[:, :], st[:, :, 1], st[:, :, 4], ALU.add).then_inc(steps, 1)
        dve.tensor_tensor(half[:, :], st[:, :, 1], st[:, :, 4], ALU.subtract).then_inc(steps, 1)
        dve.tensor_tensor(var[:, :], st[:, :, 2], st[:, :, 5], ALU.add).then_inc(steps, 1)
        dve.wait_ge(steps, k + 3)
        dve.tensor_scalar(mean[:, :], mean[:, :], 0.5, None, ALU.mult).then_inc(steps, 1)
        dve.scalar_tensor_tensor(out=half[:, :], in0=half[:, :], scalar=0.25, in1=half[:, :], op0=ALU.mult, op1=ALU.mult)\
           .then_inc(steps, 1)
        dve.tensor_scalar(var[:, :], var[:, :], 1.0 / D, EPS, ALU.mult, ALU.add).then_inc(steps, 1)
        dve.wait_ge(steps, k + 6)
        dve.tensor_tensor(var[:, :], var[:, :], half[:, :], ALU.add).then_inc(steps, 1)
        dve.wait_ge(root, 1)
        dve.reciprocal(rstd[:, :], var[:, :]).then_inc(steps, 1)
        dve.wait_ge(steps, k + 8)

    def act(act):
        act.wait_ge(steps, NT + 7)
        act.activation(var[:, :], var[:, :], ACT.Sqrt).then_inc(root, 1)

    return {"dve": dve, "act": act}, mean, rstd


def relation_weights(n, m, name, comps, bases, root, bias, wr, scratch):
    cb = n.sb(name + "cb", [P, REL * BASES])
    bb = n.sb(name + "bb", [P, D])
    loaded, made = n.sem(name + "loaded"), n.sem(name + "made")
    bs = scratch[:, 0:2 * BASES * D].rearrange("p (k b o) -> p k b o", k=2, b=BASES)

    def sp(sp):
        for b in range(BASES):
            sp.dma_start(bs[:, :, b, :], bases[b, :, :].rearrange("(k p) o -> p k o", p=P)).then_inc(loaded, 16)
        sp.dma_start(wr[:, :, REL * D:(REL + 1) * D], root.rearrange("(k p) o -> p k o", p=P)).then_inc(loaded, 16)
        sp.dma_start(cb[:, :], comps.rearrange("r b -> (r b)").partition_broadcast(P)).then_inc(loaded, 16)
        sp.dma_start(bb[:, :], bias.partition_broadcast(P)).then_inc(loaded, 16)

    def dve(dve):
        dve.wait_ge(loaded, 16 * (BASES + 3))
        for b in range(BASES):
            if b:
                dve.wait_ge(made, REL * b)
            for r in range(REL):
                w = wr[:, :, r * D:(r + 1) * D]
                c = cb[:, r * BASES + b:r * BASES + b + 1]
                if b == 0:
                    dve.tensor_scalar(w, bs[:, :, b, :], c, None, ALU.mult).then_inc(made, 1)
                else:
                    dve.scalar_tensor_tensor(out=w, in0=bs[:, :, b, :], scalar=c, in1=w, op0=ALU.mult, op1=ALU.add)\
                       .then_inc(made, 1)
        dve.wait_ge(made, REL * BASES)

    return {"sp": sp, "dve": dve}, made, REL * BASES, bb


def turned_weights(n, m, name, weights, w):
    rows, cols = weights.shape[0] // P, weights.shape[1] // P
    raw = n.sb(name + "raw", [P, rows, cols * P])
    loaded, turned, made = n.sem(name + "loaded"), n.sem(name + "turned"), n.sem(name + "made")
    pairs = [(a, k) for a in range(rows) for k in range(cols)]
    per = len(pairs) // 2

    def place(i):
        return m.ps[:, i // per, i % per * P:(i % per + 1) * P]

    def sp(sp):
        sp.dma_start(raw[:, :, :], weights.rearrange("(a p) c -> p a c", p=P)).then_inc(loaded, 16)

    def pe(pe):
        pe.wait_ge(loaded, 16)
        for i, (a, k) in enumerate(pairs):
            pe.transpose(place(i), raw[:, a, k * P:(k + 1) * P], m.ident[:, :]).then_inc(turned, 1)
        pe.wait_ge(made, len(pairs))

    def act(act):
        for i, (a, k) in enumerate(pairs):
            act.wait_ge(turned, (i // per + 1) * per)
            act.activation(w[:, k, a * P:(a + 1) * P], place(i), ACT.Copy).then_inc(made, 1)

    return {"sp": sp, "pe": pe, "act": act}, made, len(pairs)


def transform(n, m, name, source, w, w_ready, w_count, kind, norm=None, heads=0, table=None, t_table=None,
              bias=None, vectors=None, vectors_ready=None, vectors_count=0, elu=None, clear=0, beside=None):
    KT, cols = w.shape[1], w.shape[2]
    banks = -(-cols // 512)
    OW = {"relation": REL * D, "support": D, "attention": cols + heads}[kind]
    xn = n.sb(name + "xn", [P, 2, KT * P])
    ht = n.sb(name + "ht", [P, 2, KT * P])
    ob = n.sb(name + "ob", [P, 2, OW])
    given = n.sem(name + "given")
    turned = n.sem(name + "turned")
    cut = n.sem(name + "cut")
    done = n.sem(name + "done")
    taken_a = n.sem(name + "taken_a")
    taken_d = n.sem(name + "taken_d")
    ob_free = n.sem(name + "ob_free")
    stored = [n.sem(name + f"stored{r}") for r in range(2)]
    owner = {"relation": "ddaaa", "support": "d", "attention": "d" if bias is not None else "a"}[kind]
    order = [3, 4, 0, 1, 2] if kind == "relation" else list(range(banks))
    place = [0, 1, 2, 3, 0] if beside else list(range(banks))
    depth = 2 if banks == 1 else 1
    turn_first = kind == "relation"
    share = {e: [b for b in range(banks) if owner[b] == e] for e in "ad"}
    na, nd = len(share["a"]), len(share["d"])
    product = [[m.ps[:, place[b] + r * (depth - 1), 0:min(512, cols - order[b] * 512)] for b in range(banks)]
               for r in range(2)]
    ps_t = [m.ps[:, 6 + r, 0:KT * P] for r in range(2)]
    if kind == "attention":
        dh = cols // heads
        dots = n.sb(name + "dots", [P, 2, 2 * heads])
        junk = n.sb(name + "junk", [P, 2 * heads, dh])
        dotted = n.sem(name + "dotted")
        ones_set = n.sem(name + "ones_set")
        ob_h = [ob[:, r, :].rearrange("p (h c) -> p h c", h=heads) for r in range(2)]
        per_tile = 2 * heads

    def sp(sp):
        sp.sem_inc(ob_free, 2)
        with sp.Fori(0, PAIRS) as i:
            for r in range(2):
                j = i * 2 + r
                if na:
                    sp.wait_ge(taken_a, j * na + (depth + 1) * na)
                if kind == "relation":
                    sp.wait_ge(taken_d, j * nd + (depth + 1) * nd)
                    z = m.z.rearrange("(q j p) d -> p q j d", q=REL, p=P)[:, :, bass.ds(j, 1), :]
                    sp.dma_start(z.rearrange("p q j d -> p q (j d)"), ob[:, r, :].rearrange("p (q d) -> p q d", q=REL))\
                      .then_inc(stored[r], 16)
                else:
                    if nd:
                        sp.wait_ge(taken_d, j * nd + (depth + 1) * nd)
                    sp.dma_start(flat(node_rows(table)[:, bass.ds(j, 1), :]), ob[:, r, :]).then_inc(stored[r], 16)
                if kind == "attention":
                    sp.wait_ge(dotted, j * (per_tile + 1) + (per_tile + 1))
                    sp.dma_start(flat(node_rows(t_table)[:, bass.ds(j, 1), :]), dots[:, r, heads:]).then_inc(stored[r], 16)
                    sp.wait_ge(stored[r], i * 32 + 32)
                else:
                    sp.wait_ge(stored[r], i * 16 + 16)
                sp.sem_inc(ob_free, 1)

    def pairs(eng, work):
        with eng.Fori(0, PAIRS - 1) as i:
            for r in range(2):
                work(i * 2 + r, r, True)
        for r in range(2):
            work(NT - 2 + r, r, r == 0)

    def rest_of_turns(eng, key):
        if beside:
            with eng.Fori(NT, TURNS) as t:
                for q in range(NQ):
                    beside[key](eng, t, q)

    def pe(pe):
        def turn(j, r):
            pe.wait_ge(given, j + 1)
            for k in range(KT):
                mm = pe.transpose(ps_t[r][:, k * P:(k + 1) * P], xn[:, r, k * P:(k + 1) * P], m.ident[:, :])
            mm.then_inc(turned, 1)

        def work(j, r, more):
            if more and turn_first:
                turn(j + 1, 1 - r)
            pe.wait_ge(cut, j + 1)
            for b in range(banks):
                e, sem, of = owner[b], (taken_a if owner[b] == "a" else taken_d), (na if owner[b] == "a" else nd)
                pe.wait_ge(sem, j * of + (share[e].index(b) + 1))
                if beside and b == 0:
                    pe.wait_ge(taken_a, j * na + na)
                if beside and b == banks - 1:
                    pe.wait_ge(taken_d, j * nd + (nd + 1))
                at, width = order[b] * 512, product[r][b].shape[1]
                for k in range(KT):
                    mm = pe.matmul(product[r][b], ht[:, r, k * P:(k + 1) * P], w[:, k, at:at + width],
                                   start=(k == 0), stop=(k == KT - 1))
                mm.then_inc(done, 1)
                if beside and b < NQ:
                    beside["pe"](pe, j, b)
            if more and not turn_first:
                turn(j + 1, 1 - r)

        pe.wait_ge(w_ready, w_count)
        turn(0, 0)
        pairs(pe, work)
        rest_of_turns(pe, "pe")

    def act(act):
        def copy(j, r):
            act.wait_ge(turned, j + 1)
            if elu:
                act.activation(ht[:, r, :], ps_t[r], ACT.Copy, bias=-1.0).then_inc(cut, 1)
            else:
                act.activation(ht[:, r, :], ps_t[r], ACT.Relu).then_inc(cut, 1)

        def work(j, r, more):
            if more and turn_first:
                copy(j + 1, 1 - r)
            if more and elu:
                elu["act"](act, 1 - r, j + 1)
            for b in share["a"]:
                act.wait_ge(done, j * banks + (b + 1))
                if b == share["a"][0]:
                    act.wait_ge(ob_free, j + 1)
                if kind == "attention":
                    act.activation(ob_h[r][:, :, 0:dh], product[r][b].rearrange("p (h c) -> p h c", h=heads), ACT.Copy)\
                       .then_inc(taken_a, 1)
                else:
                    at, width = order[b] * 512, product[r][b].shape[1]
                    act.activation(ob[:, r, at:at + width], product[r][b], ACT.Copy).then_inc(taken_a, 1)
            if more and not turn_first:
                copy(j + 1, 1 - r)

        if na:
            act.sem_inc(taken_a, na * depth)
        if elu:
            elu["act"](act, 0, 0)
        copy(0, 0)
        pairs(act, work)

    def dve(dve):
        def give(j, r):
            if source == "norm":
                dve.tensor_scalar(xn[:, r, :], flat(m.acc[:, bass.ds(j, 1), X_AT:X_AT + D]),
                                  norm[0][:, bass.ds(j, 1)], norm[1][:, bass.ds(j, 1)], ALU.subtract, ALU.mult)\
                   .then_inc(given, 1)
            elif source == "acc":
                dve.tensor_scalar(xn[:, r, :], flat(m.acc[:, bass.ds(j, 1), 0:D]), 1.0, None, ALU.mult)\
                   .then_inc(given, 1)
            else:
                elu["dve"](dve, r, j, xn, given)

        def work(j, r, more):
            if more:
                give(j + 1, 1 - r)
            if beside:
                beside["dve"](dve, j, 0)
            dve.wait_ge(done, j * banks + (1 if kind == "relation" else banks))
            dve.wait_ge(ob_free, j + 1)
            if kind == "relation":
                dve.tensor_copy(ob[:, r, 3 * 512:4 * 512], product[r][0]).then_inc(taken_d, 1)
                if beside:
                    beside["dve"](dve, j, 1)
                dve.wait_ge(done, j * banks + 2)
                dve.tensor_tensor(m.acc[:, bass.ds(j, 1), 0:D], product[r][1].rearrange("p (a c) -> p a c", a=1),
                                  bias[:, :].rearrange("p (a c) -> p a c", a=1), ALU.add).then_inc(taken_d, 1)
                if beside:
                    for q in range(2, NQ):
                        beside["dve"](dve, j, q)
                return
            if kind == "support":
                dve.tensor_copy(ob[:, r, :], product[r][0]).then_inc(taken_d, 1)
                return
            if nd:
                dve.tensor_tensor(ob_h[r][:, :, 0:dh], product[r][0].rearrange("p (h c) -> p h c", h=heads),
                                  bias[:, :].rearrange("p (h c) -> p h c", h=heads), ALU.add).then_inc(taken_d, 1)
                dve.wait_ge(taken_d, j + depth + 1)
            else:
                dve.wait_ge(taken_a, j + depth + 1)
            for v in range(2 * heads):
                dve.tensor_tensor_reduce(junk[:, v, :], ob_h[r][:, v % heads, 0:dh], vectors[:, v, :], 1.0, 0.0,
                                         ALU.mult, ALU.add, dots[:, r, v:v + 1]).then_inc(dotted, 1)
            dve.wait_ge(dotted, j * (per_tile + 1) + per_tile)
            dve.tensor_scalar(m.tab[:, bass.ds(j, 1), 0:heads],
                              dots[:, r, 0:heads].rearrange("p (a c) -> p a c", a=1), 1.0, None, ALU.mult)\
               .then_inc(dotted, 1)

        if nd:
            dve.sem_inc(taken_d, nd * depth)
        if kind == "attention":
            for r in range(2):
                dve.memset(ob_h[r][:, :, dh:dh + 1], 1.0).then_inc(ones_set, 1)
            dve.wait_ge(ones_set, 2)
            dve.wait_ge(vectors_ready, vectors_count)
        give(0, 0)
        pairs(dve, work)
        rest_of_turns(dve, "dve")

    def pool(pool):
        for j in range(0, NT, STATS):
            pool.wait_ge(given, j + STATS)
            pool.memset(m.acc[:, j:j + STATS, 0:clear], 0.0).then_inc(cleared, 1)

    parts = {"sp": sp, "pe": pe, "act": act, "dve": dve}
    if clear:
        cleared = n.sem(name + "cleared")
        parts["pool"] = pool
    return parts


def attention_vectors(n, name, own, other, heads, dh, bias=None):
    v = n.sb(name + "v", [P, 2 * heads, dh])
    b = n.sb(name + "b", [P, heads * dh]) if bias is not None else None
    loaded = n.sem(name + "loaded")
    count = 0
    pieces = []
    for side, a in enumerate((own, other)):
        for h in range(heads):
            pieces.append((v[:, side * heads + h, :], a[h]))
    if b is not None:
        pieces.append((b[:, :], bias))

    def sp(sp):
        for to, a in pieces:
            sp.dma_start(to, a.partition_broadcast(P)).then_inc(loaded, 16)

    return {"sp": sp}, v, b, loaded, 16 * len(pieces)


def weights_part(n, name, weights, w):
    loaded = n.sem(name + "loaded")

    def sp(sp):
        sp.dma_start(w[:, :, :], weights.rearrange("(k p) o -> p k o", p=P)).then_inc(loaded, 16)

    return {"sp": sp}, loaded, 16



def rgcn_first(n, m, a, beside):
    wr = n.sb("r0_wr", [P, 2, (REL + 1) * D])
    cleared, x_in = n.sem("r0_cleared"), n.sem("r0_x_in")
    norm, mean, rstd = norm_part(n, m, "r0_n_", x_in, 32)
    scratch = n.sb("r0_bases", [P, 2 * BASES * D])
    made, ready, count, bb = relation_weights(n, m, "r0_w_", a.comps[0, :, :], a.bases[0, :, :, :], a.roots[0, :, :],
                                              a.biases[0, :], wr, scratch[:, :])
    tr = transform(n, m, "r0_", "norm", wr, ready, count, "relation", norm=(mean, rstd), bias=bb, beside=beside)

    def sp(sp):
        sp.wait_ge(cleared, 1)
        to = m.acc[:, :, X_AT:X_AT + D]
        sp.dma_start(to[:, 0:FULL, :], node_rows(a.x[0:FULL * P, :])).then_inc(x_in, 16)
        sp.dma_start(to[0:REST, FULL, :], a.x[FULL * P:N, :]).then_inc(x_in, 16)

    def dve(dve):
        dve.memset(m.acc[:, FULL:NT, X_AT:X_AT + D], 0.0).then_inc(cleared, 1)

    return [{"sp": sp, "dve": dve}, {"sp": made["sp"]}], [{"dve": made["dve"]}, norm, tr]


def rgcn_second(nc, m, a):
    with Net(nc) as n:
        wr = n.sb("r1_wr", [P, 2, (REL + 1) * D])
        scratch = n.sb("r1_bases", [P, 2 * BASES * D])
        made, ready, count, bb = relation_weights(n, m, "r1_w_", a.comps[1, :, :], a.bases[1, :, :, :],
                                                  a.roots[1, :, :], a.biases[1, :], wr, scratch[:, :])
        tr = transform(n, m, "r1_", "acc", wr, ready, count, "relation", bias=bb)
        run_parts(n.block(), made, tr)


def gcn_support(nc, m, a):
    with Net(nc) as n:
        w = n.sb("g_w", [P, 2, D])
        ready = n.sem("g_ready")
        wp, wl, wc = weights_part(n, "g_w_", a.gcn_w, w)
        norm, mean, rstd = norm_part(n, m, "g_n_", ready, 1)
        tr = transform(n, m, "g_", "norm", w, wl, wc, "support", norm=(mean, rstd), table=m.support)

        def dve(dve):
            x = m.acc[:, :, X_AT:X_AT + D]
            dve.tensor_tensor(x, x, m.acc[:, :, 0:D], ALU.add).then_inc(ready, 1)

        recs = n.sem("g_recs")
        run_parts(n.block(), {"dve": dve}, wp, {"sp": lambda sp: load_records(sp, m, m.rec_src, recs)}, norm, tr)


def gat_tables(nc, m, a):
    with Net(nc) as n:
        w = n.sb("a_w", [P, 2, D])
        ready = n.sem("a_ready")
        wp, wl, wc = weights_part(n, "a_w_", a.gat_w, w)
        heads, dh = 2, D // 2
        vp, v, b, vl, vc = attention_vectors(n, "a_v_", [a.gat_a[0:dh]] * heads, [a.gat_a[dh:2 * dh]] * heads,
                                             heads, dh, a.gat_b)
        norm, mean, rstd = norm_part(n, m, "a_n_", ready, 1)
        tr = transform(n, m, "a_", "norm", w, wl, wc, "attention", norm=(mean, rstd), heads=heads, table=m.gat_rows,
                       t_table=m.gat_t, bias=b, vectors=v, vectors_ready=vl, vectors_count=vc, clear=D + heads)
        run_parts(n.block(), {"dve": lambda dve: dve.sem_inc(ready, 1)}, wp, vp, norm, tr)


def inverse_sums(n, m, name, heads, width, least):
    inv = n.sb(name + "inv", [P, NT, heads])
    step = n.sem(name + "inv_step")
    sums = m.acc[:, :, 0:heads * width].rearrange("p j (h c) -> p j h c", h=heads)[:, :, :, width - 1]

    def dve(dve):
        dve.tensor_scalar(inv[:, :, :], sums, least, None, ALU.add).then_inc(step, 1)
        dve.wait_ge(step, 1)
        dve.reciprocal(inv[:, :, :], inv[:, :, :]).then_inc(step, 1)
        dve.wait_ge(step, 2)

    return {"dve": dve}, inv, sums


def gat_first_of_two(nc, m, a):
    with Net(nc) as n:
        heads, dh = 2, D // 2
        own = n.sb("b_own", [P, NT, heads * (dh + 1)])
        none = n.sb("b_none", [P, NT, heads])
        step, own_in = n.sem("b_step"), n.sem("b_own_in")
        inv = n.sb("b_inv", [P, NT, heads])
        sums = m.acc[:, :, 0:heads * (dh + 1)].rearrange("p j (h c) -> p j h c", h=heads)[:, :, :, dh]

        def sp(sp):
            sp.dma_start(own[:, :, :], node_rows(m.gat_rows)).then_inc(own_in, 16)

        def dve(dve):
            dve.tensor_scalar(none[:, :, :], sums, 0.0, None, ALU.is_equal).then_inc(step, 1)
            dve.wait_ge(step, 1)
            dve.tensor_tensor(inv[:, :, :], sums, none[:, :, :], ALU.add).then_inc(step, 1)
            dve.wait_ge(step, 2)
            dve.reciprocal(inv[:, :, :], inv[:, :, :]).then_inc(step, 1)
            dve.wait_ge(step, 3)
            k = 3

            def add_to_x(h, a):
                x = m.acc[:, :, X_AT + h * dh:X_AT + (h + 1) * dh]
                dve.tensor_tensor(x, x, a, ALU.add).then_inc(step, 1)

            got = [m.acc[:, :, h * (dh + 1):h * (dh + 1) + dh] for h in range(heads)]
            for h in range(heads):
                dve.tensor_tensor(got[h], got[h], inv[:, :, h:h + 1].to_broadcast([P, NT, dh]), ALU.mult).then_inc(step, 1)
            for h in range(heads):
                dve.wait_ge(step, k + heads)
                add_to_x(h, got[h])
            k += 2 * heads
            dve.wait_ge(own_in, 16)
            own_h = [own[:, :, h * (dh + 1):h * (dh + 1) + dh] for h in range(heads)]
            for h in range(heads):
                dve.tensor_tensor(own_h[h], own_h[h], none[:, :, h:h + 1].to_broadcast([P, NT, dh]), ALU.mult)\
                   .then_inc(step, 1)
            for h in range(heads):
                dve.wait_ge(step, k + heads)
                add_to_x(h, own_h[h])
            k += 2 * heads
            dve.wait_ge(step, k)

        run_parts(n.block(), {"sp": sp, "dve": dve})
    with Net(nc) as n:
        heads, dh = 4, P
        w = n.sb("c_w", [P, 2, heads * dh])
        ready = n.sem("c_ready")
        wp, wl, wc = turned_weights(n, m, "c_w_", a.w1, w)
        vp, v, b, vl, vc = attention_vectors(n, "c_v_", [a.a_dst1[0, h, :] for h in range(heads)],
                                             [a.a_src1[0, h, :] for h in range(heads)], heads, dh)
        norm, mean, rstd = norm_part(n, m, "c_n_", ready, 1)
        tr = transform(n, m, "c_", "norm", w, wl, wc, "attention", norm=(mean, rstd), heads=heads, table=m.rows1,
                       t_table=m.t1, vectors=v, vectors_ready=vl, vectors_count=vc, clear=heads * (dh + 1))
        kept = n.sem("c_kept")

        def keep(sp):
            sp.dma_start(node_rows(m.x_kept), m.acc[:, :, X_AT:X_AT + D]).then_inc(kept, 16)
        recs = n.sem("c_recs")
        run_parts(n.block(), {"dve": lambda dve: dve.sem_inc(ready, 1)}, wp, vp,
                  {"sp": lambda sp: load_records(sp, m, m.rec_dst, recs)},
                  {"sp": keep, "pool": lambda pool: pool.wait_ge(kept, 16)}, norm, tr)


def gat_second_of_two(nc, m, a):
    heads, dh = 4, P
    with Net(nc) as n:
        w = n.sb("d_w", [P, 4, D])
        wp, wl, wc = turned_weights(n, m, "d_w_", a.w2, w)
        vp, v, b, vl, vc = attention_vectors(n, "d_v_", [a.a_dst2[0, 0, :]], [a.a_src2[0, 0, :]], 1, D)
        ip, inv, sums = inverse_sums(n, m, "d_", heads, dh + 1, 1e-16)
        b1 = n.sb("d_b1", [P, heads * dh])
        y = n.sb("d_y", [P, 2, heads * dh])
        low = n.sb("d_low", [P, 2, heads * dh])
        b_in, steps, raised = n.sem("d_b_in"), n.sem("d_steps"), n.sem("d_raised")
        PER = heads + 1

        def elu_dve(dve, r, j, xn, given):
            for h in range(heads):
                dve.scalar_tensor_tensor(out=y[:, r, h * dh:(h + 1) * dh],
                                         in0=flat(m.acc[:, bass.ds(j, 1), h * (dh + 1):h * (dh + 1) + dh]),
                                         scalar=flat(inv[:, bass.ds(j, 1), h:h + 1]), in1=b1[:, h * dh:(h + 1) * dh],
                                         op0=ALU.mult, op1=ALU.add).then_inc(steps, 1)
            dve.wait_ge(steps, j * PER + heads)
            dve.tensor_scalar(low[:, r, :], y[:, r, :], 0.0, None, ALU.min).then_inc(steps, 1)
            dve.wait_ge(raised, j + 1)
            dve.scalar_tensor_tensor(out=xn[:, r, :], in0=y[:, r, :], scalar=0.0, in1=low[:, r, :],
                                     op0=ALU.max, op1=ALU.add).then_inc(given, 1)

        def elu_act(act, r, j):
            act.wait_ge(steps, j * PER + PER)
            act.activation(low[:, r, :], low[:, r, :], ACT.Exp).then_inc(raised, 1)

        tr = transform(n, m, "d_", "elu", w, wl, wc, "attention", heads=1, table=m.rows2, t_table=m.t2,
                       vectors=v, vectors_ready=vl, vectors_count=vc, elu={"dve": elu_dve, "act": elu_act}, clear=D + 1)
        run_parts(n.block(), {"sp": lambda sp: sp.dma_start(b1[:, :], a.b1.partition_broadcast(P)).then_inc(b_in, 16),
                              "dve": lambda dve: dve.wait_ge(b_in, 16)}, wp, vp, ip, tr)


def finish(nc, m, a, out):
    with Net(nc) as n:
        ip, inv, sums = inverse_sums(n, m, "f_", 1, D + 1, 1e-16)
        b2 = n.sb("f_b2", [P, D])
        b_in, step, stored = n.sem("f_b_in"), n.sem("f_step"), n.sem("f_stored")
        x, got = m.acc[:, :, X_AT:X_AT + D], m.acc[:, :, 0:D]
        b_all = b2[:, :].unsqueeze(1).to_broadcast([P, NT, D])

        def sp(sp):
            sp.dma_start(b2[:, :], a.b2.partition_broadcast(P)).then_inc(b_in, 16)
            sp.wait_ge(step, 3)
            sp.dma_start(node_rows(out[0:FULL * P, :]), x[:, 0:FULL, :]).then_inc(stored, 16)
            sp.dma_start(out[FULL * P:N, :], x[0:REST, FULL, :]).then_inc(stored, 16)
            sp.wait_ge(stored, 32)

        def dve(dve):
            dve.tensor_tensor(got, got, inv[:, :, 0:1].to_broadcast([P, NT, D]), ALU.mult).then_inc(step, 1)
            dve.wait_ge(b_in, 16)
            dve.wait_ge(step, 1)
            dve.tensor_tensor(x, x, got, ALU.add).then_inc(step, 1)
            dve.wait_ge(step, 2)
            dve.tensor_tensor(x, x, b_all, ALU.add).then_inc(step, 1)

        run_parts(n.block(), ip, {"sp": sp, "dve": dve})


def build(nc, a, out, upto=99):
    m = named()
    dram = nc.dram_tensor
    m.rec_dst = dram("rec_dst", [P * SL, 4], F32).ap()
    m.rec_src = dram("rec_src", [P * SL, 4], F32).ap()
    m.key_rows = dram("key_rows", [SL, P], BF16).ap()
    m.z = dram("z", [REL * NP, D], F32).ap()
    m.support = dram("support", [NP, D], F32).ap()
    m.gat_rows = dram("gat_rows", [NP, D + 2], F32).ap()
    m.gat_t = dram("gat_t", [NP, 2], F32).ap()
    m.rows1 = dram("rows1", [NP, 4 * (P + 1)], F32).ap()
    m.t1 = dram("t1", [NP, 4], F32).ap()
    m.rows2 = dram("rows2", [NP, D + 1], F32).ap()
    m.t2 = dram("t2", [NP, 1], F32).ap()
    m.x_kept = dram("x_kept", [NP, D], F32).ap()
    with Net(nc) as n:
        m.ps = n.ps("ps", [P, 8, 512])
        m.iota_n, m.iota_p = n.sb("iota_n", [P, P]), n.sb("iota_p", [P, 1])
        m.iota_b, m.ident_b = n.sb("iota_b", [P, P], BF16), n.sb("ident_b", [P, P], BF16)
        m.ident = n.sb("ident", [P, P])
        m.words_dst = n.sb("words_dst", [1, SL // PACK], I32)
        m.words_src = n.sb("words_src", [1, SL // PACK], I32)
        m.rec = n.sb("rec", [P, SL, 4])
        m.acc = n.sb("acc", [P, NT, W_ACC])
        sort_edges(nc, m, a)
        if upto < 1: return
        message_pass(nc, m, "p0_", m.words_dst, 0, m.z, 1, D, 0, weight=3)
        rgcn_second(nc, m, a)
        message_pass(nc, m, "p1_", m.words_dst, 0, m.z, 1, D, 0, weight=3)
        if upto < 2: return
        gcn_support(nc, m, a)
        message_pass(nc, m, "p2_", m.words_src, 0, m.support, 1, D, X_AT, weight=2)
        if upto < 3: return
        for i, (heads, width, tables, words, index, rows, t) in enumerate((
                (2, P + 1, gat_tables, m.words_src, 0, m.gat_rows, m.gat_t),
                (4, P + 1, gat_first_of_two, m.words_dst, 2, m.rows1, m.t1),
                (1, D + 1, gat_second_of_two, m.words_dst, 2, m.rows2, m.t2))):
            with Net(nc) as k:
                m.tab = k.sb(f"tab{i}", [P, NT, 2 * heads])
                m.tab3 = k.sb(f"tab3{i}", [P, NT, 3 * 2 * heads], BF16)
                tables(nc, m, a)
                with Net(nc) as e:
                    m.edge_t = e.sb(f"edge_t{i}", [P, SL, heads])
                    max_pass(nc, m, f"m{i}_", words, index, t, heads, i < 2, i == 2)
                    message_pass(nc, m, f"q{i}_", words, index, rows, heads, width, 0)
            if upto < 4 + i: return
        finish(nc, m, a, out)


def sort_edges(nc, m, a):
    with Net(nc) as k:
        row_b = k.sb("row_b", [P, COLS], U32)
        rec_b = k.sb("rec_b", [P, COLS, 4])
        with Net(nc) as n:
            m.ones, m.below = n.sb("ones", [P, P]), n.sb("below", [P, P])
            m.iota_s = n.sb("iota_s", [P, SL])
            constants(nc, m)
            column = {name: n.sb("s_" + name, [P, COLS], dt) for name, dt in
                      (("src", I32), ("dst", I32), ("etype", I32), ("weight", F32), ("typef", F32), ("srcf", F32))}
            s = named(rec_b=rec_b, rec_a=m.rec[:, 0:COLS, :], **column)
            s.by_dst = named(tile=n.sb("d_tile", [P, COLS]), key=n.sb("d_key", [P, COLS]),
                                       row=n.sb("d_row", [P, COLS], U32), words=m.words_dst)
            s.by_src = named(tile=s.typef, key=s.srcf, row=row_b, words=m.words_src)
            rank_by_dst(nc, m, s, a.src, a.dst, a.etype, a.weight)
            with Net(nc) as e:
                rank = rank_by_src(nc, e, m, s)
                run_parts(e.block(), rank,
                          {"pool": lambda pool: scatter_records(pool, e, s.by_dst.row, s.rec_a, m.rec_dst, "sa_")})
        with Net(nc) as n:
            before, count, after = inverse_counts(nc, n, m)
            loads, tables = rgcn_first(n, m, a, count)
            run_parts(n.block(), *loads, before, *tables, after,
                      {"pool": lambda pool: scatter_records(pool, n, row_b, rec_b, m.rec_src, "sb_")})


_INS = {"x": "x", "src": "src", "dst": "dst", "edge_type_8": "etype", "edge_weight": "weight",
        "L0_gnn_comps": "comps", "L0_gnn_bases": "bases", "L0_gnn_roots": "roots", "L0_gnn_biases": "biases",
        "L1_gnn_weight": "gcn_w", "L2_gnn_W_w": "gat_w", "L2_gnn_W_b": "gat_b", "L2_gnn_a": "gat_a",
        "L3_gnn_W1": "w1", "L3_gnn_a_src1": "a_src1", "L3_gnn_a_dst1": "a_dst1", "L3_gnn_b1": "b1",
        "L3_gnn_W2": "w2", "L3_gnn_a_src2": "a_src2", "L3_gnn_a_dst2": "a_dst2", "L3_gnn_b2": "b2"}


def kernel(**inputs):
    import concourse.bacc as _bacc
    from concourse.bass_utils import run_bass_kernel_spmd as _run

    nc = _bacc.Bacc("TRN2", target_bir_lowering=False, num_devices=1)
    arrays, aps = {}, {}
    for name, short in _INS.items():
        v = np.ascontiguousarray(inputs[name])
        arrays[f"in_{name}"] = v
        aps[short] = nc.dram_tensor(f"in_{name}", v.shape, mybir.dt.from_np(v.dtype), kind="ExternalInput").ap()
    out = nc.dram_tensor("out_x", (N, D), F32, kind="ExternalOutput").ap()
    build(nc, named(**aps), out)
    return _run(nc, [arrays], core_ids=[0]).results[0]["out_x"]
```
